# Optimizing a Trainium2 kernel written in Bass

```python
import numpy as np
import jax
import jax.numpy as jnp

def _softmax(x, axis=-1):
    return jax.nn.softmax(x, axis=axis)

def _gelu(x):
    return jax.nn.gelu(x, approximate=True)

def _silu(x):
    return jax.nn.silu(x)

def _sigmoid(x):
    return jax.nn.sigmoid(x)

def _layernorm(x, axis=-1, eps=1e-05):
    m = jnp.mean(x, axis=axis, keepdims=True)
    v = jnp.var(x, axis=axis, keepdims=True)
    return (x - m) / jnp.sqrt(v + eps)

def _scatter_add(tgt, idx, src, axis=0):
    return tgt.at[idx].add(src)

def _segment_sum(src, seg, n):
    return jax.ops.segment_sum(src, seg, n)
kernel_name = 'mk_decoder_preln_d1_seqx_r8_4f09e4'

def setup_inputs(seed: int=0):
    np.random.seed(seed)
    _w = jnp.asarray

    def _rec_inputs():
        import jax
        import jax.numpy as jnp
        _rk = jax.random.key(seed)
        x = -0.0002928 + 1 * jax.random.normal(jax.random.fold_in(_rk, 1), (4, 512, 128), jnp.float32)
        _lenS = 512 - jax.random.randint(jax.random.fold_in(_rk, 7), (4,), 0, max(1, 512 // 4) + 1, jnp.int32)
        _lenS2 = 154 - jax.random.randint(jax.random.fold_in(_rk, 8), (4,), 0, max(1, 154 // 4) + 1, jnp.int32)
        _ctx_1024P = jax.random.normal(jax.random.fold_in(_rk, 11), (4, 16, 128), jnp.float32)
        _ctx_1024c = jax.random.dirichlet(jax.random.fold_in(_rk, 511), 0.3 * jnp.ones((16,), jnp.float32), (4, 154))
        _ctx_1024t = jnp.einsum('bsk,bkd->bsd', _ctx_1024c, _ctx_1024P)
        _ctx_1024t = _ctx_1024t * jax.lax.rsqrt(jnp.mean(jnp.square(_ctx_1024t)) + 1e-12) * 0.953939
        ctx_1024 = -1.39393e-06 + 0.999914 * (_ctx_1024t + 0.3 * jax.random.normal(jax.random.fold_in(_rk, 611), (4, 154, 128), jnp.float32))
        return (x, ctx_1024)
    x, ctx_1024 = _rec_inputs()

    def _L0_attn_setup():
        import jax, jax.numpy as jnp
        import numpy as np
        B, T, D = (4, 256, 128)
        H, Dh = (16, 64)
        key = jax.random.key(seed)
        ks = jax.random.split(key, 5)
        std_qkv = float(np.sqrt(2.0 / (Dh * D)))
        std_o = float(np.sqrt(2.0 / (D * Dh)))
        return {'x': jax.random.normal(ks[0], (B, T, D), dtype=jnp.float32), 'W_Q': jax.random.normal(ks[1], (H, Dh, D), dtype=jnp.float32) * std_qkv, 'b_Q': jnp.zeros((H, Dh), dtype=jnp.float32), 'W_K': jax.random.normal(ks[2], (H, Dh, D), dtype=jnp.float32) * std_qkv, 'b_K': jnp.zeros((H, Dh), dtype=jnp.float32), 'W_V': jax.random.normal(ks[3], (H, Dh, D), dtype=jnp.float32) * std_qkv, 'b_V': jnp.zeros((H, Dh), dtype=jnp.float32), 'W_O': jax.random.normal(ks[4], (H, D, Dh), dtype=jnp.float32) * std_o, 'b_O': jnp.zeros((D,), dtype=jnp.float32)}
    _L0_attn_all = _L0_attn_setup()
    _L0_attn_in = {k: v for k, v in _L0_attn_all.items() if k in ('W_Q', 'b_Q', 'W_K', 'b_K', 'W_V', 'b_V', 'W_O', 'b_O')}
    del _L0_attn_all

    def _L0_xattn_setup():
        import jax, jax.numpy as jnp
        import numpy as np
        D_MODEL = 128
        N_HEADS = 16
        HEAD_DIM = D_MODEL // N_HEADS
        B, L = (2, 256)
        key = jax.random.key(seed)
        ks = jax.random.split(key, 11)
        s = 1.0 / np.sqrt(D_MODEL)
        inp = {'query': jax.random.normal(ks[0], (B, L, D_MODEL), dtype=jnp.float32), 'key': jax.random.normal(ks[1], (B, L, D_MODEL), dtype=jnp.float32), 'value': jax.random.normal(ks[2], (B, L, D_MODEL), dtype=jnp.float32), 'Wq_w': jax.random.normal(ks[3], (D_MODEL, D_MODEL), dtype=jnp.float32) * s, 'Wq_b': jnp.zeros((D_MODEL,), dtype=jnp.float32), 'Wk_w': jax.random.normal(ks[4], (D_MODEL, D_MODEL), dtype=jnp.float32) * s, 'Wk_b': jnp.zeros((D_MODEL,), dtype=jnp.float32), 'Wv_w': jax.random.normal(ks[5], (D_MODEL, D_MODEL), dtype=jnp.float32) * s, 'Wv_b': jnp.zeros((D_MODEL,), dtype=jnp.float32), 'Wo_w': jax.random.normal(ks[6], (D_MODEL, D_MODEL), dtype=jnp.float32) * s, 'Wo_b': jnp.zeros((D_MODEL,), dtype=jnp.float32)}
        return inp
    _L0_xattn_all = _L0_xattn_setup()
    _L0_xattn_in = {k: v for k, v in _L0_xattn_all.items() if k in ('Wq_w', 'Wq_b', 'Wk_w', 'Wk_b', 'Wv_w', 'Wv_b', 'Wo_w', 'Wo_b')}
    del _L0_xattn_all

    def _L0_ffn_setup():
        import jax, jax.numpy as jnp
        import numpy as np
        LN_EPS = 1e-05

        def entmax15(z):
            z = z / 2.0
            z = z - jnp.max(z, axis=-1, keepdims=True)
            zs = -jnp.sort(-z, axis=-1)
            k = jnp.arange(1, z.shape[-1] + 1, dtype=z.dtype)
            mean = jnp.cumsum(zs, axis=-1) / k
            meansq = jnp.cumsum(zs * zs, axis=-1) / k
            ss = k * (meansq - jnp.square(mean))
            delta = (1.0 - ss) / k
            tau = mean - jnp.sqrt(jnp.clip(delta, 0.0))
            support = jnp.sum((tau <= zs).astype(jnp.int32), axis=-1, keepdims=True)
            tau_star = jnp.take_along_axis(tau, support - 1, axis=-1)
            return jnp.square(jnp.clip(z - tau_star, 0.0))

        def layernorm_noaffine(v):
            m = jnp.mean(v, axis=-1, keepdims=True)
            var = jnp.mean(jnp.square(v - m), axis=-1, keepdims=True)
            return (v - m) / jnp.sqrt(var + LN_EPS)

        def cp_mumoe(x, gate, Win, Wout):
            ones = jnp.ones(x.shape[:-1] + (1,), x.dtype)
            xb = jnp.concatenate([x, ones], axis=-1)
            z = jnp.einsum('btd,dr->btr', xb, Win) * gate
            return jnp.einsum('btr,or->bto', z, Wout)
        key = jax.random.key(seed)
        ks = jax.random.split(key, 8)
        B, T, D, O, D2, E, R = (8, 256, 128, 512, 128, 16, 64)
        s = lambda k, shape, scale: jax.random.normal(k, shape, jnp.float32) * scale
        return {'x': s(ks[0], (B, T, D), 1.0), 'proj': s(ks[1], (D, E), D ** (-0.5)), 'C1': s(ks[2], (E, R), E ** (-0.5)), 'Win1': s(ks[3], (D + 1, R), D ** (-0.5)), 'Wout1': s(ks[4], (O, R), R ** (-0.5)), 'C2': s(ks[5], (E, R), E ** (-0.5)), 'Win2': s(ks[6], (O + 1, R), O ** (-0.5)), 'Wout2': s(ks[7], (D2, R), R ** (-0.5))}
    _L0_ffn_all = _L0_ffn_setup()
    _L0_ffn_in = {k: v for k, v in _L0_ffn_all.items() if k in ('proj', 'C1', 'Win1', 'Wout1', 'C2', 'Win2', 'Wout2')}
    del _L0_ffn_all
    return {'x': x, 'ctx_1024': ctx_1024, 'L0_attn_W_Q': _L0_attn_in['W_Q'], 'L0_attn_b_Q': _L0_attn_in['b_Q'], 'L0_attn_W_K': _L0_attn_in['W_K'], 'L0_attn_b_K': _L0_attn_in['b_K'], 'L0_attn_W_V': _L0_attn_in['W_V'], 'L0_attn_b_V': _L0_attn_in['b_V'], 'L0_attn_W_O': _L0_attn_in['W_O'], 'L0_attn_b_O': _L0_attn_in['b_O'], 'L0_xattn_Wq_w': _L0_xattn_in['Wq_w'], 'L0_xattn_Wq_b': _L0_xattn_in['Wq_b'], 'L0_xattn_Wk_w': _L0_xattn_in['Wk_w'], 'L0_xattn_Wk_b': _L0_xattn_in['Wk_b'], 'L0_xattn_Wv_w': _L0_xattn_in['Wv_w'], 'L0_xattn_Wv_b': _L0_xattn_in['Wv_b'], 'L0_xattn_Wo_w': _L0_xattn_in['Wo_w'], 'L0_xattn_Wo_b': _L0_xattn_in['Wo_b'], 'L0_ffn_proj': _L0_ffn_in['proj'], 'L0_ffn_C1': _L0_ffn_in['C1'], 'L0_ffn_Win1': _L0_ffn_in['Win1'], 'L0_ffn_Wout1': _L0_ffn_in['Wout1'], 'L0_ffn_C2': _L0_ffn_in['C2'], 'L0_ffn_Win2': _L0_ffn_in['Win2'], 'L0_ffn_Wout2': _L0_ffn_in['Wout2']}

def reference(x, ctx_1024, L0_attn_W_Q, L0_attn_b_Q, L0_attn_W_K, L0_attn_b_K, L0_attn_W_V, L0_attn_b_V, L0_attn_W_O, L0_attn_b_O, L0_xattn_Wq_w, L0_xattn_Wq_b, L0_xattn_Wk_w, L0_xattn_Wk_b, L0_xattn_Wv_w, L0_xattn_Wv_b, L0_xattn_Wo_w, L0_xattn_Wo_b, L0_ffn_proj, L0_ffn_C1, L0_ffn_Win1, L0_ffn_Wout1, L0_ffn_C2, L0_ffn_Win2, L0_ffn_Wout2):
    import jax
    import jax.numpy as jnp

    def _L0_attn_ref(x, W_Q, b_Q, W_K, b_K, W_V, b_V, W_O, b_O):
        import jax, jax.numpy as jnp
        import numpy as np
        B, T, D = (4, 256, 128)
        H, Dh = (16, 64)
        Q = jnp.einsum('btd,hkd->bthk', x, W_Q) + b_Q
        K = jnp.einsum('btd,hkd->bthk', x, W_K) + b_K
        V = jnp.einsum('btd,hkd->bthk', x, W_V) + b_V
        d_head = W_Q.shape[1]
        scores = jnp.einsum('bqhk,bshk->bhqs', Q, K) / jnp.sqrt(jnp.asarray(d_head, x.dtype))
        attn = jax.nn.softmax(scores, axis=-1)
        out_h = jnp.einsum('bhqs,bshk->bqhk', attn, V)
        return jnp.einsum('bqhk,hdk->bqd', out_h, W_O) + b_O

    def _L0_xattn_ref(query, key, value, Wq_w, Wq_b, Wk_w, Wk_b, Wv_w, Wv_b, Wo_w, Wo_b):
        import jax, jax.numpy as jnp
        import numpy as np
        D_MODEL = 128
        N_HEADS = 16
        HEAD_DIM = D_MODEL // N_HEADS
        B, L = (2, 256)
        b = query.shape[0]
        Q = query @ Wq_w.T + Wq_b
        K = key @ Wk_w.T + Wk_b
        V = value @ Wv_w.T + Wv_b

        def split_heads(x):
            return x.reshape(b, -1, N_HEADS, HEAD_DIM).transpose(0, 2, 1, 3)
        Qh, Kh, Vh = (split_heads(Q), split_heads(K), split_heads(V))
        scale = 1.0 / jnp.sqrt(jnp.float32(HEAD_DIM))
        energy = jnp.einsum('bhqd,bhkd->bhqk', Qh, Kh) * scale
        attn = jax.nn.softmax(energy, axis=1)
        out = jnp.einsum('bhqk,bhkd->bhqd', attn, Vh)
        out = out.transpose(0, 2, 1, 3).reshape(b, -1, D_MODEL)
        return out @ Wo_w.T + Wo_b

    def _L0_ffn_ref(x, proj, C1, Win1, Wout1, C2, Win2, Wout2):
        import jax, jax.numpy as jnp
        import numpy as np
        LN_EPS = 1e-05

        def entmax15(z):
            z = z / 2.0
            z = z - jnp.max(z, axis=-1, keepdims=True)
            zs = -jnp.sort(-z, axis=-1)
            k = jnp.arange(1, z.shape[-1] + 1, dtype=z.dtype)
            mean = jnp.cumsum(zs, axis=-1) / k
            meansq = jnp.cumsum(zs * zs, axis=-1) / k
            ss = k * (meansq - jnp.square(mean))
            delta = (1.0 - ss) / k
            tau = mean - jnp.sqrt(jnp.clip(delta, 0.0))
            support = jnp.sum((tau <= zs).astype(jnp.int32), axis=-1, keepdims=True)
            tau_star = jnp.take_along_axis(tau, support - 1, axis=-1)
            return jnp.square(jnp.clip(z - tau_star, 0.0))

        def layernorm_noaffine(v):
            m = jnp.mean(v, axis=-1, keepdims=True)
            var = jnp.mean(jnp.square(v - m), axis=-1, keepdims=True)
            return (v - m) / jnp.sqrt(var + LN_EPS)

        def cp_mumoe(x, gate, Win, Wout):
            ones = jnp.ones(x.shape[:-1] + (1,), x.dtype)
            xb = jnp.concatenate([x, ones], axis=-1)
            z = jnp.einsum('btd,dr->btr', xb, Win) * gate
            return jnp.einsum('btr,or->bto', z, Wout)
        a = entmax15(layernorm_noaffine(jnp.einsum('btd,de->bte', x, proj)))
        g1 = jnp.einsum('bte,er->btr', a, C1)
        h = cp_mumoe(x, g1, Win1, Wout1)
        h = jax.nn.gelu(h, approximate=False)
        g2 = jnp.einsum('bte,er->btr', a, C2)
        return cp_mumoe(h, g2, Win2, Wout2)
    x = x + _L0_attn_ref(_layernorm(x, axis=-1), L0_attn_W_Q, L0_attn_b_Q, L0_attn_W_K, L0_attn_b_K, L0_attn_W_V, L0_attn_b_V, L0_attn_W_O, L0_attn_b_O)
    x = x + _L0_xattn_ref(_layernorm(x, axis=-1), ctx_1024, ctx_1024, L0_xattn_Wq_w, L0_xattn_Wq_b, L0_xattn_Wk_w, L0_xattn_Wk_b, L0_xattn_Wv_w, L0_xattn_Wv_b, L0_xattn_Wo_w, L0_xattn_Wo_b)
    x = x + _L0_ffn_ref(_layernorm(x, axis=-1), L0_ffn_proj, L0_ffn_C1, L0_ffn_Win1, L0_ffn_Wout1, L0_ffn_C2, L0_ffn_Win2, L0_ffn_Wout2)
    return x

_drawn_inputs = setup_inputs


def setup_inputs(seed=0):
    import zlib

    import numpy as np

    out = dict(_drawn_inputs(seed))
    spreads = {'L0_attn_b_Q': (0.0, 0.8),
     'L0_attn_b_K': (0.0, 0.8),
     'L0_attn_b_V': (0.0, 0.1),
     'L0_attn_b_O': (0.0, 0.1),
     'L0_xattn_Wq_b': (0.0, 0.1),
     'L0_xattn_Wk_b': (0.0, 0.1),
     'L0_xattn_Wv_b': (0.0, 0.1),
     'L0_xattn_Wo_b': (0.0, 0.432)}
    factors = {'L0_attn_W_Q': 8.0,
     'L0_attn_W_K': 8.0,
     'L0_attn_W_V': 8.0,
     'L0_ffn_proj': 8.0,
     'L0_ffn_C1': 8.0,
     'L0_ffn_Win1': 8.0,
     'L0_ffn_Wout1': 8.0,
     'L0_ffn_C2': 8.0,
     'L0_ffn_Win2': 8.0,
     'L0_ffn_Wout2': 8.0}
    for name, (base, spread) in spreads.items():
        noise = np.random.default_rng([zlib.crc32(name.encode()), seed]).standard_normal(out[name].shape)
        drawn = base * np.exp(spread * noise) if base else spread * noise
        out[name] = jnp.asarray(drawn.astype(out[name].dtype))
    for name, factor in factors.items():
        out[name] = (out[name] * factor).astype(out[name].dtype)
    return out
```

```python
from contextlib import ExitStack

import numpy as np

import concourse.bass as bass
from concourse import mybir

F32 = mybir.dt.float32
F16 = mybir.dt.float16
BF16 = mybir.dt.bfloat16
ALU = mybir.AluOpType
ACT = mybir.ActivationFunctionType
AX_X = mybir.AxisListType.X

B, T, D = 4, 512, 128
H, DH = 16, 64
PAIRS = H // 2
NP = B * PAIRS
KT = T // 128
S = 154
SL = S - 128
SLP = 32
XH, XD = 16, 8
XT = B + 1
E, R, O = 16, 64, 512
TT = B * KT
EPS = 1e-5
MS = 64.0
DMAS = 4


def decoder(nc, x, ctx_main, ctx_left, wq, wk, wv, wo, bias_qkv, b_o, xwq, xwk, xwv, xwo, xb, xbv,
            proj, c12, win1, bin1, wout1, win2, bin2, wout2, consts, out):
    with ExitStack() as stack:
        def sb(name, shape, dt):
            return stack.enter_context(nc.sbuf_tensor(name, shape, dt))

        def sem(name):
            return stack.enter_context(nc.semaphore(name))

        cst = sb("cst", [128, 5 * 128 + 16 + B + 16], F32)
        centre, mean, ident = cst[:, 0:128], cst[:, 128:256], cst[:, 256:384]
        head_mask = cst[:, 640:656]
        batch_mask = cst[:, 656:660]
        inv_k = cst[:, 660:676]
        minus_ident = sb("minus_ident", [128, 128], BF16)
        ones_row = cst[:, 384:512]
        xT = sb("xT", [128, B * T], F32)
        biases = sb("biases", [128, 3, PAIRS], F32)
        w_split = sb("w_split", [128, 2 * 3 * H * DH], F16)
        w_hi = w_split[:, 0:3 * H * DH].rearrange("p (a n) -> p a n", a=3)
        w_lo = w_split[:, 3 * H * DH:].rearrange("p (a n) -> p a n", a=3)
        xn3 = w_split[:, 0:2 * B * T].bitcast(F32).rearrange("p (b t) -> p b t", b=B)
        wo_hi = sb("wo_hi", [128, PAIRS, D], F16)
        wo_lo = sb("wo_lo", [128, PAIRS, D], F16)
        bo = sb("bo", [128, 1], F32)
        xw = sb("xw", [128, 4, 128], F32)
        xbias = sb("xbias", [128, 3], F32)
        xbv_row = sb("xbv_row", [1, 128], F32)
        proj_sb = sb("proj_sb", [128, E], F32)
        c12_sb = sb("c12_sb", [E, 2 * R], F32)
        win1_sb = sb("win1_sb", [128, R], F32)
        wout1_sb = sb("wout1_sb", [R, O], F32)
        win2_sb = sb("win2_sb", [128, O // 128, R], F32)
        wout2_sb = sb("wout2_sb", [128, D], F32)
        bin_sb = sb("bin_sb", [128, 1], F32)
        eps = sb("eps", [128, 1], F32)
        xn_hi = sb("xn_hi", [128, B, T], F16)
        xn_lo = sb("xn_lo", [128, B, T], F16)

        r1 = sb("r1", [128, 64 * 1024 // 4], F32)
        w_raw = r1[:, 0:3 * 1024].rearrange("p (a n) -> p a n", a=3)
        wo_raw = r1[:, 3 * 1024:4 * 1024].rearrange("p (a n) -> p a n", a=PAIRS)
        r1h = r1[:, :].bitcast(F16)
        oT_hi = r1h[:, 0:NP * T].rearrange("p (n t) -> p n t", n=NP)
        oT_lo = r1h[:, NP * T:2 * NP * T].rearrange("p (n t) -> p n t", n=NP)
        left = r1[:, 0:XH * T].rearrange("p (h t) -> p h t", h=XH)
        left_hi = left.bitcast(BF16).rearrange("p h (t two) -> p h t two", two=2)[:, :, :, 1]
        left_lo = r1h[:, 2 * XH * T:3 * XH * T].rearrange("p (h t) -> p h t", h=XH)

        r2 = sb("r2", [128, 40 * 1024 // 4], F32)
        r2h = r2[:, :].bitcast(F16)

        def r2_f16(start, n):
            return r2h[:, start:start + n]
        prob = r2[:, 0:2 * KT * T].rearrange("p (h k t) -> p h k t", h=2, k=KT)
        prob_hi = prob.bitcast(BF16).rearrange("p h k (t two) -> p h k t two", two=2)[:, :, :, :, 1]
        base = 4 * KT * T
        prob_lo = r2_f16(base, 2 * KT * T).rearrange("p (h k t) -> p h k t", h=2, k=KT)
        base += 2 * KT * T
        stacks = r2_f16(base, 16 * T).rearrange("p (s h j t) -> p s h j t", s=2, h=2, j=4)
        qa, kb, qb, ka = (stacks[:, :, :, j, :] for j in range(4))
        keys_hi = r2_f16(0, XH * XT * 128).rearrange("p (h k) -> p h k", h=XH)
        keys_lo = r2_f16(XH * XT * 128, XH * XT * 128).rearrange("p (h k) -> p h k", h=XH)

        parts = sb("parts", [128, 5, T], F16)
        q_hi_t, k_hi_t, q_lo_t, k_hi_2, k_lo_t = (parts[:, j, :] for j in range(5))
        v_hi_t = sb("v_hi", [128, 2, KT, 2, DH + 1], F16)
        v_lo_t = sb("v_lo", [128, 2, KT, 2, DH], F16)
        bias_now = sb("bias_now", [128, 2, 2], F32)
        m_q = sb("m_q", [128, 2, KT, 2], F32)
        m_row = sb("m_row", [2, T], F16)
        rsum = sb("rsum", [128, 2, KT], F32)
        o_n = sb("o_n", [128, KT, 2, DH], F32)
        ln_sq = sb("ln_sq", [128, T], F32)
        ln_lg = sb("ln_lg", [128, T], F32)
        ln_rs = sb("ln_rs", [128, T], F32)
        ln_out = sb("ln_out", [128, T], F32)
        ctx_sb = sb("ctx_sb", [128, XT * 128], F32)
        kT_hi = sb("kT_hi", [128, XT * 128], F16)
        kT_lo = sb("kT_lo", [128, XT * 128], F16)
        xv_hi = sb("xv_hi", [128, B, 128], F16)
        xv_lo = sb("xv_lo", [128, B, 128], F16)
        xvl_hi = sb("xvl_hi", [128, B, 128], F16)
        xvl_lo = sb("xvl_lo", [128, B, 128], F16)
        xq_hi, xq_lo = xn_hi, xn_lo
        xm = sb("xm", [128, 2, 64], BF16)
        xe = sb("xe", [128, 2, XH, 64], F32)
        xs8 = sb("xs8", [128, 8, 64], F32)
        xs4 = sb("xs4", [128, 4, 64], F32)
        xs2 = sb("xs2", [128, 2, 64], F32)
        xsum = sb("xsum", [128, 2, 64], F32)
        xrec = sb("xrec", [128, 2, 64], F32)
        xa0 = sb("xa0", [128, XH, 128], F32)
        xal0 = sb("xal0", [128, XH, 128], F16)
        free1 = XH * T + XH * T // 2
        xa1 = r1[:, free1:free1 + XH * 128].rearrange("p (h t) -> p h t", h=XH)
        free1 = 2 * (free1 + XH * 128)
        xal1 = r1h[:, free1:free1 + XH * 128].rearrange("p (h t) -> p h t", h=XH)
        xa, xa_lo = [xa0[:, :, :], xa1], [xal0[:, :, :], xal1]
        xa_hi = [a.bitcast(BF16).rearrange("p h (t two) -> p h t two", two=2)[:, :, :, 1] for a in xa]
        xo = sb("xo", [128, 128], F32)
        xoT = sb("xoT", [128, T], F32)
        hid = r2[:, 0:O // 128 * T].rearrange("p (m t) -> p m t", m=O // 128)
        gates, z2 = r2[:, 2048:2560], r2[:, 3072:3584]
        z1, aT = r2[0:R, 2560:3072], r2[0:E, 3584:4096]
        c_a, c_b = (r2[:, n:n + 512].rearrange("p (a t e) -> p a t e", a=2, t=TT) for n in (4096, 4608))
        gz, gs, gq = (r2[:, n:n + 256].rearrange("p (t e) -> p t e", t=TT) for n in (5120, 5376, 5632))
        g1 = sb("g1", [128, TT], F32)

        ps = stack.enter_context(nc.psum_tensor("ps", [128, 8, 512], F32))
        st = [ps[:, 0:2, :], ps[:, 2:4, :]]
        bank_p, bank_s, bank_o = ps[:, 4, :], [ps[:, 5, :], ps[:, 6, :]], ps[:, 7, :]

        loaded = sem("loaded")
        loaded_x = sem("loaded_x")
        loaded_w = sem("loaded_w")
        stored = sem("stored")
        setup = sem("setup")
        w_hi_done = sem("w_hi_done")
        w_lo_done = sem("w_lo_done")
        pe_ln = sem("pe_ln")
        act_ln = sem("act_ln")
        dve_ln = sem("dve_ln")
        bias_done = sem("bias_done")
        q_proj, k_proj, v_proj = sem("q_proj"), sem("k_proj"), sem("v_proj")
        k_hi2 = sem("k_hi2")
        q_hi, k_hi, v_hi = sem("q_hi_done"), sem("k_hi_done"), sem("v_hi_done")
        q_lo, k_lo, v_lo = sem("q_lo_done"), sem("k_lo_done"), sem("v_lo_done")
        stacked, m_placed = sem("stacked"), sem("m_placed")
        s_done, max_done = sem("s_done"), sem("max_done")
        m_turned, m_out = sem("m_turned"), sem("m_out")
        st_done, exp_done = sem("st_done"), sem("exp_done")
        lo_dve, lo_pool = sem("lo_dve"), sem("lo_pool")
        pv_done, r_done, o_done = sem("pv_done"), sem("r_done"), sem("o_done")
        oT_turned, oT_hi_done, oT_done = sem("oT_turned"), sem("oT_hi_done"), sem("oT_done")
        minus_done, ctx_k, ctx_v, key_parts, val_parts = (sem(n) for n in (
            "minus_done", "ctx_k", "ctx_v", "key_parts", "val_parts"))
        key_hi_done, val_hi_done, masked = (sem(n) for n in ("key_hi_done", "val_hi_done", "masked"))
        proj_o, resid, pe_ln2, act_ln2, normed, xq_done, xq_parts = (sem(n) for n in (
            "proj_o", "resid", "pe_ln2", "act_ln2", "normed", "xq_done", "xq_parts"))
        e_done, x_max, x_shift, x_exp, x_tree, x_sum, x_rec, x_norm, x_lo_d, x_lo_p = (sem(n) for n in (
            "e_done", "x_max", "x_shift", "x_exp", "x_tree", "x_sum", "x_rec", "x_norm", "x_lo_d", "x_lo_p"))
        x_pv, x_out, x_turned, x_T, x_proj, resid2, pe_ln3, act_ln3, normed3, scored = (sem(n) for n in (
            "x_pv", "x_out", "x_turned", "x_T", "x_proj", "resid2", "pe_ln3", "act_ln3", "normed3", "scored"))
        g_step, g_act, a_done, aT_turned, aT_out, g_done, g_out = (sem(n) for n in (
            "g_step", "g_act", "a_done", "aT_turned", "aT_out", "g_done", "g_out"))
        z1_done, z1_out, h_done, h_out, z2_done, z2_out, y_done = (sem(n) for n in (
            "z1_done", "z1_out", "h_done", "h_out", "z2_done", "z2_out", "y_done"))

        W_LOADS = 4
        X_LOADS = 3
        OTHER_LOADS = 18
        GSQRT = 7 + 3 * TT + 2 + 8 + 6
        UL, UM = T // 64, B * T // 64

        block = stack.enter_context(nc.Block())

        @block.sync
        def _(sp):
            for b in range(B):
                sp.dma_start(xT[:, b * T:(b + 1) * T], x[:, b * T:(b + 1) * T]).then_inc(loaded_x, 16)
                if b == 0:
                    sp.dma_start(cst[:, :], consts).then_inc(loaded_x, 16)
            for j, w in enumerate((wq, wk, wv)):
                sp.dma_start(w_raw[:, j, :], w).then_inc(loaded_w, 16)
            sp.dma_start(wo_raw, wo).then_inc(loaded_w, 16)
            sp.dma_start(biases[:, :, :], bias_qkv).then_inc(loaded, 16)
            sp.dma_start(bo[:, :], b_o).then_inc(loaded, 16)
            for j, w in enumerate((xwq, xwk, xwv, xwo)):
                sp.dma_start(xw[:, j, :], w).then_inc(loaded, 16)
            sp.dma_start(xbias[:, :], xb).then_inc(loaded, 16)
            sp.dma_start(xbv_row[:, :], xbv).then_inc(loaded, 16)
            sp.dma_start(proj_sb[:, :], proj).then_inc(loaded, 16)
            sp.dma_start(c12_sb[:, :], c12).then_inc(loaded, 16)
            sp.dma_start(win1_sb[:, :], win1).then_inc(loaded, 16)
            sp.dma_start(wout1_sb[:, :], wout1).then_inc(loaded, 16)
            sp.dma_start(win2_sb[:, :, :], win2).then_inc(loaded, 16)
            sp.dma_start(wout2_sb[R:2 * R, :], wout2).then_inc(loaded, 16)
            sp.dma_start(bin_sb[0:R, :], bin1).then_inc(loaded, 16)
            sp.dma_start(bin_sb[R:2 * R, :], bin2).then_inc(loaded, 16)
            sp.dma_start(ctx_sb[:, 0:B * 128], ctx_main).then_inc(loaded, 16)
            sp.wait_ge(setup, 1)
            sp.dma_start(ctx_sb[:, B * 128:].rearrange("p (b k) -> p b k", b=B)[:, :, 0:SL],
                         ctx_left).then_inc(loaded, 16)

            def reg(n):
                return n if isinstance(n, int) else sp.to_reg(n)

            def stack_pair(n, slot, first=False):
                pairs, used, placed = reg(n + 1), reg(4 * n - 4), reg(16 * DMAS * n)
                if not first:
                    if not isinstance(n, int) or n >= 2:
                        sp.wait_ge(st_done, used)
                    sp.wait_ge(stacked, placed)
                sp.wait_ge(q_hi, pairs)
                sp.wait_ge(k_hi, pairs)
                sp.wait_ge(q_lo, pairs)
                sp.wait_ge(k_lo, pairs)
                sp.wait_ge(k_hi2, pairs)
                for h in range(2):
                    rows = slice(DH * h, DH * h + DH)
                    sp.dma_start(stacks[0:DH, slot, h, :, :], parts[rows, 0:4, :]).then_inc(stacked, 16)
                    sp.dma_start(stacks[DH:128, slot, h, 0:4:3, :], parts[rows, 0:5:4, :]).then_inc(stacked, 16)

            def place_maxima(n, slot):
                sp.wait_ge(m_out, reg(n + 1))
                sp.dma_start(qb[DH:DH + 1, slot, :, :], m_row[:, :]).then_inc(m_placed, 16)

            stack_pair(0, 0, first=True)
            stack_pair(1, 1)
            place_maxima(0, 0)
            stack_pair(2, 0)
            place_maxima(1, 1)
            with sp.Fori(0, (NP - 4) // 2) as it:
                stack_pair(2 * it + 3, 1)
                place_maxima(2 * it + 2, 0)
                stack_pair(2 * it + 4, 0)
                place_maxima(2 * it + 3, 1)
            stack_pair(NP - 1, 1)
            place_maxima(NP - 2, 0)
            place_maxima(NP - 1, 1)
            for b in range(B):
                sp.wait_ge(stored, b + 1)
                sp.dma_start(out[:, b * T:(b + 1) * T], xT[:, b * T:(b + 1) * T]).then_inc(m_placed, 16)
            sp.wait_ge(m_placed, 16 * (NP + B))

        @block.gpsimd
        def _(pool):
            pool.memset(ctx_sb[:, B * 128:], 0.0).then_inc(setup, 1)
            pool.wait_ge(setup, 1)
            pool.memset(kb[DH:DH + 1, :, :, :], MS).then_inc(setup, 1)
            pool.wait_ge(setup, 2)
            pool.memset(v_hi_t[:, :, :, :, DH:DH + 1], 1.0).then_inc(setup, 1)
            pool.wait_ge(setup, 3)
            pool.memset(eps[:, :], EPS).then_inc(setup, 1)

            def low_parts(g, h):
                pool.wait_ge(exp_done, 2 * g + 2)
                nc.gpsimd.tensor_tensor(prob_lo[:, h, 1:4, :], prob[:, h, 1:4, :], prob_hi[:, h, 1:4, :],
                                        ALU.subtract).then_inc(lo_pool, 1)

            with pool.Fori(0, NP) as i:
                low_parts(2 * i, 0)
                low_parts(2 * i + 1, 1)

            def sum_heads(w, slot, first=False):
                pool.wait_ge(x_exp, w + 1)
                e = xe[:, slot, :, :]
                pool.tensor_tensor(xs8[:, :, :], e[:, 0:8, :], e[:, 8:16, :], ALU.add).then_inc(x_tree, 1)
                pool.wait_ge(x_tree, 3 * w + 1)
                pool.tensor_tensor(xs4[:, :, :], xs8[:, 0:4, :], xs8[:, 4:8, :], ALU.add).then_inc(x_tree, 1)
                pool.wait_ge(x_tree, 3 * w + 2)
                pool.tensor_tensor(xs2[:, :, :], xs4[:, 0:2, :], xs4[:, 2:4, :], ALU.add).then_inc(x_tree, 1)
                pool.wait_ge(x_tree, 3 * w + 3)
                if not first:
                    pool.wait_ge(x_rec, w - 1)
                pool.tensor_tensor(xsum[:, slot, :], xs2[:, 0, :], xs2[:, 1, :], ALU.add).then_inc(x_sum, 1)

            def weights_low(w, a, hi, lo, cols):
                pool.wait_ge(x_norm, w + 1)
                pool.tensor_tensor(lo[:, 8:16, cols], a[:, 8:16, cols], hi[:, 8:16, cols],
                                   ALU.subtract).then_inc(x_lo_p, 1)

            for u in range(2):
                sum_heads(u, u, first=True)
                if u:
                    weights_low(0, left, left_hi, left_lo, slice(0, 64))
            with pool.Fori(0, UL // 2 - 1) as it:
                for j in range(2):
                    w = 2 * it + 2 + j
                    sum_heads(w, j)
                    weights_low(w - 1, left, left_hi, left_lo, bass.ds((w - 1) * 64, 64))
            weights_low(UL - 1, left, left_hi, left_lo, slice((UL - 1) * 64, UL * 64))
            with pool.Fori(0, B) as b:
                for c in range(8):
                    w = 8 * b + UL + c
                    sum_heads(w, c % 2)
                    if c >= 1:
                        q = (c - 1) // 2 % 2
                        weights_low(w - 1, xa[q], xa_hi[q], xa_lo[q], slice(64 * ((c - 1) % 2), 64 * ((c - 1) % 2) + 64))
                weights_low(8 * b + UL + 7, xa[1], xa_hi[1], xa_lo[1], slice(64, 128))

        @block.scalar
        def _(act):
            act.wait_ge(setup, 4)
            act.wait_ge(loaded_w, 16 * W_LOADS)

            def norm_scale(n, pe_s, act_s, centred, variance):
                act.wait_ge(pe_s, 2 * n + 1)
                act.activation(ln_sq[:, :], centred, ACT.Square).then_inc(act_s, 1)
                act.wait_ge(pe_s, 2 * n + 2)
                act.activation(ln_lg[:, :], variance, ACT.Ln, bias=eps[:, :]).then_inc(act_s, 1)
                act.wait_ge(act_s, 3 * n + 2)
                act.activation(ln_rs[:, :], ln_lg[:, :], ACT.Exp, scale=-0.5).then_inc(act_s, 1)

            for b in range(B):
                if b < 3:
                    act.activation(w_hi[:, b, :], w_raw[:, b, :], ACT.Copy).then_inc(w_hi_done, 1)
                else:
                    act.activation(wo_hi[:, :, :], wo_raw, ACT.Copy).then_inc(w_hi_done, 1)
                if b >= 1:
                    act.wait_ge(dve_ln, 3 * b)
                norm_scale(b, pe_ln, act_ln, bank_p, bank_s[0])

            act.wait_ge(ctx_k, 1)
            act.activation(kT_hi[:, 0:512], ps[:, 0, :], ACT.Identity, bias=xbias[:, 1:2]).then_inc(key_hi_done, 1)
            act.activation(kT_hi[:, 512:640], ps[:, 1, 0:128], ACT.Identity, bias=xbias[:, 1:2]).then_inc(key_hi_done, 1)
            act.wait_ge(ctx_v, 1)
            act.activation(xv_hi[:, :, :].rearrange("p b n -> p (b n)"), ps[:, 2, :], ACT.Copy).then_inc(val_hi_done, 1)
            for b in range(B):
                act.activation(xvl_hi[:, b, :], ps[:, 3, 0:128], ACT.Copy, scale=batch_mask[:, b:b + 1]).then_inc(val_hi_done, 1)

            def q_high(n, slot, first=False):
                act.wait_ge(q_proj, n + 1)
                act.wait_ge(bias_done, n + 1)
                if not first:
                    act.wait_ge(stacked, 16 * DMAS * n)
                act.activation(q_hi_t, bank_p, ACT.Identity, bias=bias_now[:, slot, 0:1]).then_inc(q_hi, 1)

            def k_high(n, slot):
                act.wait_ge(k_proj, n + 1)
                act.activation(k_hi_t, bank_p, ACT.Identity, bias=bias_now[:, slot, 1:2]).then_inc(k_hi, 1)

            def v_high(n, slot, free):
                act.wait_ge(v_proj, n + 1)
                if free is not None:
                    act.wait_ge(pv_done, free)
                act.activation(v_hi_t[:, slot, :, :, 0:DH],
                               bank_p.rearrange("p (k h d) -> p k h d", k=KT, h=2), ACT.Copy).then_inc(v_hi, 1)

            def exp_half(i, h, half, first=False):
                u = 4 * i + 2 * h + half
                act.wait_ge(st_done, u + 1)
                if not first:
                    act.wait_ge(pv_done, 2 * i - 1 + h)
                act.activation(prob[:, h, 2 * half:2 * half + 2, :], st[half], ACT.Exp,
                               scale=DH ** -0.5).then_inc(exp_done, 1)

            def m_rows(n, first=False):
                act.wait_ge(m_turned, n + 1)
                if not first:
                    act.wait_ge(m_placed, 16 * n)
                act.activation(m_row[:, :], bank_p[0:2, :], ACT.Copy, scale=-1.0 / MS).then_inc(m_out, 1)

            def step(i, slot, first=False, maxima=True, projected=True):
                if projected:
                    q_high(i + 2, slot)
                exp_half(i, 0, 0, first)
                exp_half(i, 0, 1, first)
                if projected:
                    k_high(i + 2, slot)
                exp_half(i, 1, 0, first)
                if maxima:
                    v_high(i + 1, 1 - slot, None if first else 2 * i)
                exp_half(i, 1, 1, first)
                if maxima:
                    m_rows(i + 1)

            for n in range(2):
                q_high(n, n, first=n == 0)
                k_high(n, n)
            v_high(0, 0, None)
            m_rows(0, first=True)
            step(0, 0, first=True)
            with act.Fori(0, (NP - 4) // 2) as it:
                step(2 * it + 1, 1)
                step(2 * it + 2, 0)
            step(NP - 3, 1)
            step(NP - 2, 0, projected=False)
            step(NP - 1, 1, maxima=False, projected=False)

            for b in range(B):
                if b:
                    act.wait_ge(normed, b)
                norm_scale(b, pe_ln2, act_ln2, ps[:, 1, :], ps[:, 2, :])
            act.wait_ge(key_parts, 2)
            act.wait_ge(pv_done, 2 * NP)
            for h in range(XH):
                act.activation(keys_lo[:, h, :], kT_lo[:, :], ACT.Copy, scale=head_mask[:, h:h + 1]).then_inc(masked, 1)

            def exp_unit(w, slot, first=False):
                act.wait_ge(x_shift, w + 1)
                if not first:
                    act.wait_ge(x_norm, w - 1)
                act.activation(xe[:, slot, :, :], ps[:, 2 * slot:2 * slot + 2, :].rearrange(
                    "p a (h q) -> p (a h) q", q=64), ACT.Exp, scale=XD ** -0.5).then_inc(x_exp, 1)

            for w in range(2):
                exp_unit(w, w, first=True)
            with act.Fori(0, UL // 2 - 1) as it:
                for j in range(2):
                    exp_unit(2 * it + 2 + j, j)
            with act.Fori(0, B) as b:
                for c in range(8):
                    exp_unit(8 * b + UL + c, c % 2)
                    if c in (2, 4, 6):
                        act.wait_ge(x_pv, 4 * b + c // 2)
                        act.activation(xo[:, :], ps[:, 6, 0:128], ACT.Copy).then_inc(x_out, 1)
                act.wait_ge(x_pv, 4 * b + 4)
                act.activation(xo[:, :], ps[:, 6, 0:128], ACT.Copy).then_inc(x_out, 1)
                act.wait_ge(x_turned, 4 * b + 4)
                act.activation(xoT[:, :], ps[:, 7, :], ACT.Copy).then_inc(x_T, 1)
                norm_scale(b, pe_ln3, act_ln3, ps[:, 7, :], ps[:, 6, :])

            act.wait_ge(g_step, 4)
            act.activation(g1[:, :], g1[:, :], ACT.Ln, bias=eps[:, :], scale=1.0 / E).then_inc(g_act, 1)
            act.wait_ge(g_act, 1)
            act.activation(g1[:, :], g1[:, :], ACT.Exp, scale=-0.5).then_inc(g_act, 1)
            act.wait_ge(g_step, GSQRT)
            act.activation(gs, gs, ACT.Sqrt).then_inc(g_act, 1)
            for b in range(B):
                act.wait_ge(aT_turned, b + 1)
                if b:
                    act.wait_ge(g_done, b)
                act.activation(aT, ps[0:E, 1, :], ACT.Copy).then_inc(aT_out, 1)
                act.wait_ge(g_done, b + 1)
                if b:
                    act.wait_ge(z2_out, b)
                act.activation(gates, ps[:, 0, :], ACT.Copy).then_inc(g_out, 1)
                for m in range(4):
                    act.wait_ge(h_done, 4 * b + m + 1)
                    if b:
                        act.wait_ge(z2_done, b)
                    act.activation(hid[:, m, :], ps[:, 2 + m, :], ACT.Gelu).then_inc(h_out, 1)

        @block.vector
        def _(dve):
            dve.wait_ge(loaded_x, 16 * (B + 1))
            dve.wait_ge(loaded, 16 * OTHER_LOADS)
            dve.tensor_scalar(minus_ident[:, :], ident, -1.0, None, ALU.mult).then_inc(w_lo_done, 1)
            for b in range(B):
                dve.wait_ge(w_hi_done, b + 1)
                if b < 3:
                    dve.tensor_tensor(w_lo[:, b, :], w_raw[:, b, :], w_hi[:, b, :], ALU.subtract).then_inc(w_lo_done, 1)
                else:
                    dve.tensor_tensor(wo_lo[:, :, :], wo_raw, wo_hi[:, :, :], ALU.subtract).then_inc(w_lo_done, 1)
                dve.wait_ge(act_ln, 3 * b + 3)
                if b >= 1:
                    dve.wait_ge(dve_ln, 3 * b)
                dve.tensor_tensor(ln_out[:, :], bank_p, ln_rs[:, :], ALU.mult).then_inc(dve_ln, 1)
                dve.wait_ge(dve_ln, 3 * b + 1)
                dve.tensor_copy(xn_hi[:, b, :], ln_out[:, :]).then_inc(dve_ln, 1)
                dve.wait_ge(dve_ln, 3 * b + 2)
                dve.tensor_tensor(xn_lo[:, b, :], ln_out[:, :], xn_hi[:, b, :], ALU.subtract).then_inc(dve_ln, 1)

            dve.wait_ge(key_hi_done, 2)
            dve.scalar_tensor_tensor(kT_lo[:, 0:512], ps[:, 0, :], xbias[:, 1:2], kT_hi[:, 0:512],
                                     ALU.add, ALU.subtract).then_inc(key_parts, 1)
            dve.scalar_tensor_tensor(kT_lo[:, 512:640], ps[:, 1, 0:128], xbias[:, 1:2], kT_hi[:, 512:640],
                                     ALU.add, ALU.subtract).then_inc(key_parts, 1)
            dve.wait_ge(val_hi_done, B + 1)
            dve.tensor_tensor(xv_lo[:, :, :].rearrange("p b n -> p (b n)"), ps[:, 2, :],
                              xv_hi[:, :, :].rearrange("p b n -> p (b n)"), ALU.subtract).then_inc(val_parts, 1)
            for b in range(B):
                dve.scalar_tensor_tensor(xvl_lo[:, b, :], ps[:, 3, 0:128], batch_mask[:, b:b + 1], xvl_hi[:, b, :],
                                         ALU.mult, ALU.subtract).then_inc(val_parts, 1)

            def bias_copy(n, pair, slot, first=False):
                dve.tensor_copy(bias_now[:, slot, :], biases[:, 0:2, bass.ds(pair, 1)].rearrange("p a b -> p (a b)")).then_inc(bias_done, 1)

            def q_low(n, slot, first=False):
                dve.wait_ge(q_hi, n + 1)
                if not first:
                    dve.wait_ge(stacked, 16 * DMAS * n)
                dve.scalar_tensor_tensor(q_lo_t, bank_p, bias_now[:, slot, 0:1], q_hi_t,
                                         ALU.add, ALU.subtract).then_inc(q_lo, 1)

            def k_low(n, slot):
                dve.wait_ge(k_hi, n + 1)
                dve.scalar_tensor_tensor(k_lo_t, bank_p, bias_now[:, slot, 1:2], k_hi_t,
                                         ALU.add, ALU.subtract).then_inc(k_lo, 1)
                dve.tensor_copy(k_hi_2, k_hi_t).then_inc(k_hi2, 1)

            def v_low(n, slot):
                dve.wait_ge(v_hi, n + 1)
                dve.tensor_tensor(v_lo_t[:, slot, :, :, :], bank_p.rearrange("p (k h d) -> p k h d", k=KT, h=2),
                                  v_hi_t[:, slot, :, :, 0:DH], ALU.subtract).then_inc(v_lo, 1)

            def low_parts(g, h):
                dve.wait_ge(exp_done, 2 * g + 1)
                dve.tensor_tensor(prob_lo[:, h, 0, :], prob[:, h, 0, :], prob_hi[:, h, 0, :],
                                  ALU.subtract).then_inc(lo_dve, 1)

            o_view = bank_o[:, 0:KT * (DH + 1)].rearrange("p (q d) -> p q d", q=KT)

            def normalise(g, h, turned):
                dve.wait_ge(pv_done, g + 1)
                dve.reciprocal(rsum[:, h, :], o_view[:, :, DH]).then_inc(r_done, 1)
                dve.wait_ge(r_done, g + 1)
                if turned is not None:
                    dve.wait_ge(oT_turned, turned)
                dve.tensor_tensor(o_n[:, :, h, :], o_view[:, :, 0:DH],
                                  rsum[:, h, :].unsqueeze(2).broadcast_to([128, KT, DH]), ALU.mult).then_inc(o_done, 1)

            def out_parts(n, pair):
                dve.wait_ge(oT_turned, n + 1)
                bv = biases[:, 2, bass.ds(pair, 1)]
                dve.tensor_scalar(oT_hi[:, bass.ds(n, 1), :].rearrange("p a t -> p (a t)"), bank_o, bv, None, ALU.add).then_inc(oT_hi_done, 1)
                dve.wait_ge(oT_hi_done, n + 1)
                dve.scalar_tensor_tensor(oT_lo[:, bass.ds(n, 1), :].rearrange("p a t -> p (a t)"), bank_o, bv,
                                         oT_hi[:, bass.ds(n, 1), :].rearrange("p a t -> p (a t)"),
                                         ALU.add, ALU.subtract).then_inc(oT_done, 1)

            def maxima(n, slot, c):
                h, q = c // KT, c % KT
                dve.wait_ge(s_done, 8 * n + c + 1)
                dve.reduce_max(m_q[:, slot, q, h:h + 1], bank_s[c % 2], AX_X).then_inc(max_done, 1)

            def step(i, slot, prev, nxt, first=False, maxima_=True, projected=True):
                def some(*cs):
                    if maxima_:
                        for c in cs:
                            maxima(i + 1, 1 - slot, c)

                if not first:
                    normalise(2 * i - 1, 1, None)
                if projected:
                    bias_copy(i + 2, nxt, slot)
                    q_low(i + 2, slot)
                some(0, 1)
                if projected:
                    k_low(i + 2, slot)
                low_parts(2 * i, 0)
                if not first:
                    out_parts(i - 1, prev)
                some(2, 3)
                if maxima_:
                    v_low(i + 1, 1 - slot)
                some(4, 5)
                low_parts(2 * i + 1, 1)
                some(6, 7)
                normalise(2 * i, 0, None if first else i)

            for n in range(2):
                bias_copy(n, n, n)
            dve.wait_ge(bias_done, 2)
            for n in range(2):
                q_low(n, n, first=n == 0)
                k_low(n, n)
            v_low(0, 0)
            for c in range(8):
                maxima(0, 0, c)
            step(0, 0, None, 2, first=True)
            with dve.Fori(0, (NP - 4) // 2) as it:
                i = 2 * it + 1
                step(i, 1, (i - 1) % PAIRS, (i + 2) % PAIRS)
                i = 2 * it + 2
                step(i, 0, (i - 1) % PAIRS, (i + 2) % PAIRS)
            step(NP - 3, 1, PAIRS - 4, PAIRS - 1)
            step(NP - 2, 0, PAIRS - 3, None, projected=False)
            step(NP - 1, 1, PAIRS - 2, None, maxima_=False, projected=False)
            normalise(2 * NP - 1, 1, None)
            out_parts(NP - 1, PAIRS - 1)

            def resid_sum(b, bias, bank, done):
                dve.scalar_tensor_tensor(xT[:, b * T:(b + 1) * T], bank, bias, xT[:, b * T:(b + 1) * T],
                                         ALU.add, ALU.add).then_inc(done, 1)

            for b in range(B):
                dve.wait_ge(proj_o, b + 1)
                resid_sum(b, bo[:, :], ps[:, 0, :], resid)
                dve.wait_ge(act_ln2, 3 * b + 3)
                if b:
                    dve.wait_ge(xq_done, b)
                dve.tensor_tensor(ln_out[:, :], ps[:, 1, :], ln_rs[:, :], ALU.mult).then_inc(normed, 1)
                dve.wait_ge(xq_done, b + 1)
                dve.tensor_scalar(xq_hi[:, b, :], ps[:, 3, :], xbias[:, 0:1], None, ALU.add).then_inc(xq_parts, 1)
                dve.wait_ge(xq_parts, 2 * b + 1)
                dve.scalar_tensor_tensor(xq_lo[:, b, :], ps[:, 3, :], xbias[:, 0:1], xq_hi[:, b, :],
                                         ALU.add, ALU.subtract).then_inc(xq_parts, 1)
            dve.wait_ge(pv_done, 2 * NP)
            for h in range(XH):
                dve.tensor_scalar(keys_hi[:, h, :], kT_hi[:, :], head_mask[:, h:h + 1], None, ALU.mult).then_inc(masked, 1)

            def max_heads(w, slot, first=False):
                dve.wait_ge(e_done, w + 1)
                if not first:
                    dve.wait_ge(x_shift, w - 1)
                dve.tensor_reduce(xm[:, slot, :], ps[:, 2 * slot:2 * slot + 2, :].rearrange(
                    "p a (h q) -> p q (a h)", q=64), AX_X, ALU.max).then_inc(x_max, 1)

            def weights(w, slot, a, hi, lo, cols, free=None):
                dve.wait_ge(x_sum, w + 1)
                dve.reciprocal(xrec[:, slot, :], xsum[:, slot, :]).then_inc(x_rec, 1)
                dve.wait_ge(x_rec, w + 1)
                if free is not None:
                    dve.wait_ge(x_pv, free)
                dve.tensor_tensor(a[:, :, cols], xe[:, slot, :, :],
                                  xrec[:, slot, :].unsqueeze(1).broadcast_to([128, XH, 64]), ALU.mult).then_inc(x_norm, 1)
                dve.wait_ge(x_norm, w + 1)
                dve.tensor_tensor(lo[:, 0:8, cols], a[:, 0:8, cols], hi[:, 0:8, cols],
                                  ALU.subtract).then_inc(x_lo_d, 1)

            max_heads(0, 0, first=True)
            max_heads(1, 1, first=True)
            weights(0, 0, left, left_hi, left_lo, slice(0, 64))
            with dve.Fori(0, UL // 2 - 1) as it:
                for j in range(2):
                    w = 2 * it + 2 + j
                    max_heads(w, j)
                    weights(w - 1, 1 - j, left, left_hi, left_lo, bass.ds((w - 1) * 64, 64))
            max_heads(UL, 0)
            weights(UL - 1, 1, left, left_hi, left_lo, slice((UL - 1) * 64, UL * 64))

            def main_batch(b, static):
                for c in range(8):
                    w = 8 * b + UL + c
                    if c < 7 or not static:
                        max_heads(w + 1, (c + 1) % 2)
                    q = c // 2 % 2
                    free = None
                    if c >= 4:
                        free = 4 * b + c // 2 - 1
                    elif not isinstance(b, int) or b > 0:
                        free = 4 * b + c // 2 - 1
                    weights(w, c % 2, xa[q], xa_hi[q], xa_lo[q], slice(64 * (c % 2), 64 * (c % 2) + 64), free)
                dve.wait_ge(x_proj, b + 1)
                xTb = xT[:, bass.ds(b * T, T)]
                dve.scalar_tensor_tensor(xTb, ps[:, 6, :], xbias[:, 2:3], xTb, ALU.add, ALU.add).then_inc(resid2, 1)
                dve.wait_ge(act_ln3, 3 * b + 3)
                dve.tensor_tensor(ln_out[:, :], ps[:, 7, :], ln_rs[:, :], ALU.mult).then_inc(normed3, 1)
                dve.wait_ge(normed3, 2 * b + 1)
                dve.tensor_copy(xn3[:, bass.ds(b, 1), :].rearrange("p a t -> p (a t)"), ln_out[:, :]).then_inc(normed3, 1)

            main_batch(0, False)
            with dve.Fori(1, B - 1) as b:
                main_batch(b, False)
            main_batch(B - 1, True)

            steps = [0]

            def g(ins, wait=True):
                ins.then_inc(g_step, 1)
                steps[0] += 1
                if wait:
                    dve.wait_ge(g_step, steps[0])

            def over(a):
                return a.unsqueeze(2).broadcast_to([128, TT, E])

            dve.wait_ge(scored, B)
            score = ps[:, 5, 0:TT * E].rearrange("p (t e) -> p t e", t=TT)
            g(dve.tensor_reduce(g1[:, :], score, AX_X, ALU.add))
            g(dve.scalar_tensor_tensor(gz, over(g1[:, :]), -1.0 / E, score, ALU.mult, ALU.add))
            g(dve.tensor_tensor(gq, gz, gz, ALU.mult))
            g(dve.tensor_reduce(g1[:, :], gq, AX_X, ALU.add))
            dve.wait_ge(g_act, 2)
            g(dve.scalar_tensor_tensor(gz, gz, 0.5, over(g1[:, :]), ALU.mult, ALU.mult))
            g(dve.tensor_reduce(g1[:, :], gz, AX_X, ALU.max))
            g(dve.tensor_tensor(gz, gz, over(g1[:, :]), ALU.subtract))
            for t in range(TT):
                g(dve.max(c_a[:, 0, t, 0:8], gz[:, t, :]), wait=t == TT - 1)
            for t in range(TT):
                g(dve.match_replace(gq[:, t, :], c_a[:, 0, t, 0:8], gz[:, t, :], -1e30), wait=t == TT - 1)
            for t in range(TT):
                g(dve.max(c_a[:, 0, t, 8:16], gq[:, t, :]), wait=t == TT - 1)
            g(dve.tensor_tensor(c_a[:, 1, :, :], c_a[:, 0, :, :], c_a[:, 0, :, :], ALU.mult), wait=False)
            g(dve.tensor_copy(gq, c_a[:, 0, :, :]))
            old, new = c_a, c_b
            for k in (1, 2, 4, 8):
                o = old[:, :, :, :].rearrange("p a t e -> p (a t) e")
                n = new[:, :, :, :].rearrange("p a t e -> p (a t) e")
                g(dve.tensor_copy(n[:, :, 0:k], o[:, :, 0:k]), wait=False)
                g(dve.tensor_tensor(n[:, :, k:E], o[:, :, k:E], o[:, :, 0:E - k], ALU.add))
                old, new = new, old
            ks = inv_k.unsqueeze(1).broadcast_to([128, TT, E])
            mean_k, meansq_k = c_b[:, 0, :, :], c_b[:, 1, :, :]
            g(dve.tensor_tensor(mean_k, c_a[:, 0, :, :], ks, ALU.mult), wait=False)
            g(dve.tensor_tensor(meansq_k, c_a[:, 1, :, :], ks, ALU.mult))
            g(dve.tensor_tensor(gs, mean_k, mean_k, ALU.mult))
            g(dve.tensor_tensor(gs, gs, meansq_k, ALU.subtract))
            g(dve.tensor_tensor(gs, gs, ks, ALU.add))
            g(dve.tensor_scalar(gs, gs, 0.0, None, ALU.max))
            assert steps[0] == GSQRT
            dve.wait_ge(g_act, 3)
            g(dve.tensor_tensor(gs, mean_k, gs, ALU.subtract))
            g(dve.tensor_tensor(gq, gs, gq, ALU.is_le))
            g(dve.tensor_scalar(gq, gq, 1e30, -1e30, ALU.mult, ALU.add))
            g(dve.tensor_tensor(gs, gs, gq, ALU.add))
            g(dve.tensor_reduce(g1[:, :], gs, AX_X, ALU.max))
            g(dve.tensor_tensor(gz, gz, over(g1[:, :]), ALU.subtract))
            g(dve.tensor_scalar(gz, gz, 0.0, None, ALU.max))
            dve.tensor_tensor(gq, gz, gz, ALU.mult).then_inc(a_done, 1)

            for b in range(B):
                dve.wait_ge(z1_done, b + 1)
                dve.wait_ge(g_out, b + 1)
                if b:
                    dve.wait_ge(h_done, 4 * b)
                dve.scalar_tensor_tensor(z1, ps[0:R, 1, :], bin_sb[0:R, :], gates[0:R, :],
                                         ALU.add, ALU.mult).then_inc(z1_out, 1)
                dve.wait_ge(z2_done, b + 1)
                if b:
                    dve.wait_ge(y_done, b)
                dve.scalar_tensor_tensor(z2[R:2 * R, :], ps[R:2 * R, 6, :], bin_sb[R:2 * R, :], gates[R:2 * R, :],
                                         ALU.add, ALU.mult).then_inc(z2_out, 1)
                dve.wait_ge(y_done, b + 1)
                dve.tensor_tensor(xT[:, b * T:(b + 1) * T], ps[:, 7, :], xT[:, b * T:(b + 1) * T], ALU.add).then_inc(stored, 1)

        @block.tensor
        def _(pe):
            def mm(o, lhsT, rhs, start, stop):
                return pe.matmul(o, lhsT, rhs, start=start, stop=stop, skip_group_check=True)

            pe.wait_ge(loaded_x, 16 * (B + 1))
            for b in range(B):
                if b >= 1:
                    pe.wait_ge(dve_ln, 3 * b)
                mm(bank_p, centre, xT[:, b * T:(b + 1) * T], True, True).then_inc(pe_ln, 1)
                pe.wait_ge(act_ln, 3 * b + 1)
                mm(bank_s[0], mean, ln_sq[:, :], True, True).then_inc(pe_ln, 1)
            pe.wait_ge(dve_ln, 3 * B)
            pe.wait_ge(w_lo_done, 5)
            pe.wait_ge(setup, 4)

            mm(ps[:, 0, :], xw[:, 1, :], ctx_sb[:, 0:512], True, True)
            mm(ps[:, 1, 0:128], xw[:, 1, :], ctx_sb[:, 512:640], True, True).then_inc(ctx_k, 1)
            for t in range(XT):
                o = ps[:, 2 + t // 4, 128 * (t % 4):128 * (t % 4) + 128]
                mm(o, ctx_sb[:, t * 128:(t + 1) * 128], xw[:, 2, :], True, False)
                last = mm(o, ones_row[0:1, :], xbv_row[:, :], False, True)
            last.then_inc(ctx_v, 1)
            pe.wait_ge(key_parts, 2)
            pe.wait_ge(val_parts, B + 1)

            def project(n, batch, pair, j, bank, done):
                cols = bass.ds(pair * 128, 128)
                xb = bass.ds(batch, 1)
                xh = xn_hi[:, xb, :].rearrange("p a t -> p (a t)")
                xl = xn_lo[:, xb, :].rearrange("p a t -> p (a t)")
                mm(bank, w_hi[:, j, cols], xh, True, False)
                mm(bank, w_lo[:, j, cols], xh, False, False)
                mm(bank, w_hi[:, j, cols], xl, False, True).then_inc(done, 1)

            def project_v(n, batch, pair):
                cols = bass.ds(pair * 128, 128)
                for t in range(KT):
                    toks = bass.ds(batch * T + t * 128, 128)
                    xh = xn_hi[:, :, :].rearrange("p a t -> p (a t)")[:, toks]
                    xl = xn_lo[:, :, :].rearrange("p a t -> p (a t)")[:, toks]
                    o = bank_p[:, t * 128:(t + 1) * 128]
                    mm(o, xh, w_hi[:, 2, cols], True, False)
                    mm(o, xh, w_lo[:, 2, cols], False, False)
                    last = mm(o, xl, w_hi[:, 2, cols], False, True)
                last.then_inc(v_proj, 1)

            def scores_for_max(n, slot, c):
                h, q = c // KT, c % KT
                if c == 0:
                    pe.wait_ge(stacked, 16 * DMAS * (n + 1))
                if c >= 2 or not isinstance(n, int) or n >= 1:
                    pe.wait_ge(max_done, 8 * n + c - 1)
                mm(bank_s[c % 2], qa[:, slot, h, q * 128:(q + 1) * 128],
                   ka[:, slot, h, :], True, True).then_inc(s_done, 1)

            def turn_maxima(n, slot):
                pe.wait_ge(max_done, 8 * n + 8)
                for q in range(KT):
                    last = pe.transpose(bank_p[0:2, q * 128:(q + 1) * 128], m_q[:, slot, q, :], ident)
                last.then_inc(m_turned, 1)

            def scores(i, slot, h, half, first=False):
                u = 4 * i + 2 * h + half
                if not (first and h == 0):
                    pe.wait_ge(exp_done, u - 1)
                for t in range(2):
                    cols = slice((2 * half + t) * 128, (2 * half + t + 1) * 128)
                    mm(st[half][:, t, :], ka[:, slot, h, cols], qa[:, slot, h, :], True, False)
                    last = mm(st[half][:, t, :], kb[0:DH + 1, slot, h, cols], qb[0:DH + 1, slot, h, :], False, True)
                last.then_inc(st_done, 1)

            def values(g, slot, h, qs):
                if 0 in qs:
                    pe.wait_ge(lo_dve, g + 1)
                    pe.wait_ge(lo_pool, g + 1)
                for q in qs:
                    cols = slice(q * 128, (q + 1) * 128)
                    o = bank_o[:, q * (DH + 1):(q + 1) * (DH + 1)]
                    for k in range(KT):
                        mm(o, prob_hi[:, h, k, cols], v_hi_t[:, slot, k, h, :], k == 0, False)
                        mm(o[:, 0:DH], prob_hi[:, h, k, cols], v_lo_t[:, slot, k, h, :], False, False)
                        last = mm(o, prob_lo[:, h, k, cols], v_hi_t[:, slot, k, h, :], False, k == KT - 1)
                if KT - 1 in qs:
                    last.then_inc(pv_done, 1)

            def turn_outputs(n):
                pe.wait_ge(o_done, 2 * n + 2)
                for q in range(KT):
                    last = pe.transpose(bank_o[:, q * 128:(q + 1) * 128],
                                        o_n[:, q, :, :].rearrange("p h d -> p (h d)"), ident)
                last.then_inc(oT_turned, 1)

            def step(i, slot, batch2, pair2, batch1, pair1, first=False, maxima=True, projected=True):
                def some(*cs):
                    if maxima:
                        for c in cs:
                            scores_for_max(i + 1, 1 - slot, c)

                if not first:
                    pe.wait_ge(o_done, 2 * i - 1)
                    values(2 * i - 1, 1 - slot, 1, range(KT))
                if projected:
                    pe.wait_ge(m_out, i + 1)
                    project(i + 2, batch2, pair2, 0, bank_p, q_proj)
                pe.wait_ge(m_placed, 16 * (i + 1))
                scores(i, slot, 0, 0, first)
                some(0)
                scores(i, slot, 0, 1, first)
                some(1)
                if projected:
                    pe.wait_ge(q_lo, i + 3)
                    project(i + 2, batch2, pair2, 1, bank_p, k_proj)
                if not first:
                    turn_outputs(i - 1)
                some(2)
                scores(i, slot, 1, 0)
                some(3)
                if maxima:
                    pe.wait_ge(k_lo, i + 3 if projected else i + 2)
                    project_v(i + 1, batch1, pair1)
                scores(i, slot, 1, 1)
                some(4, 5)
                if not first:
                    pe.wait_ge(oT_done, i)
                values(2 * i, slot, 0, [0, 1])
                some(6)
                values(2 * i, slot, 0, [2, 3])
                some(7)
                if maxima:
                    pe.wait_ge(v_lo, i + 2)
                    turn_maxima(i + 1, 1 - slot)

            for n in range(2):
                if n:
                    pe.wait_ge(k_lo, n)
                project(n, 0, n, 0, bank_p, q_proj)
                pe.wait_ge(q_lo, n + 1)
                project(n, 0, n, 1, bank_p, k_proj)
            pe.wait_ge(k_lo, 2)
            project_v(0, 0, 0)
            for c in range(8):
                scores_for_max(0, 0, c)
            pe.wait_ge(v_lo, 1)
            turn_maxima(0, 0)
            step(0, 0, 0, 2, 0, 1, first=True)
            with pe.Fori(0, (NP - 4) // 2) as it:
                i = 2 * it + 1
                step(i, 1, (i + 2) // PAIRS, (i + 2) % PAIRS, (i + 1) // PAIRS, (i + 1) % PAIRS)
                i = 2 * it + 2
                step(i, 0, (i + 2) // PAIRS, (i + 2) % PAIRS, (i + 1) // PAIRS, (i + 1) % PAIRS)
            step(NP - 3, 1, B - 1, PAIRS - 1, B - 1, PAIRS - 2)
            step(NP - 2, 0, None, None, B - 1, PAIRS - 1, projected=False)
            step(NP - 1, 1, None, None, None, None, maxima=False, projected=False)
            pe.wait_ge(o_done, 2 * NP - 1)
            values(2 * NP - 1, 1, 1, range(KT))
            turn_outputs(NP - 1)

            def out_proj(b):
                for p in range(PAIRS):
                    n = b * PAIRS + p
                    mm(ps[:, 0, :], wo_hi[:, p, :], oT_hi[:, n, :], p == 0, False)
                    mm(ps[:, 0, :], wo_lo[:, p, :], oT_hi[:, n, :], False, False)
                    last = mm(ps[:, 0, :], wo_hi[:, p, :], oT_lo[:, n, :], False, p == PAIRS - 1)
                last.then_inc(proj_o, 1)

            pe.wait_ge(oT_done, NP)
            out_proj(0)
            for b in range(B):
                pe.wait_ge(resid, b + 1)
                if b:
                    pe.wait_ge(normed, b)
                mm(ps[:, 1, :], centre, xT[:, b * T:(b + 1) * T], True, True).then_inc(pe_ln2, 1)
                if b + 1 < B:
                    out_proj(b + 1)
                pe.wait_ge(act_ln2, 3 * b + 1)
                mm(ps[:, 2, :], mean, ln_sq[:, :], True, True).then_inc(pe_ln2, 1)
                pe.wait_ge(normed, b + 1)
                if b:
                    pe.wait_ge(xq_parts, 2 * b)
                mm(ps[:, 3, :], xw[:, 0, :], ln_out[:, :], True, True).then_inc(xq_done, 1)
            pe.wait_ge(xq_parts, 2 * B)
            pe.wait_ge(masked, 2 * XH)

            def energies_left(w, slot, cols, first=False):
                if not first:
                    pe.wait_ge(x_exp, w - 1)
                for h in range(XH):
                    for b in range(B):
                        o = ps[SLP * b:SLP * b + SLP, 2 * slot + h // 8, 64 * (h % 8):64 * (h % 8) + 64]
                        ks = slice(B * 128 + SLP * b, B * 128 + SLP * b + SLP)
                        mm(o, keys_hi[:, h, ks], xq_hi[:, b, cols], h % 8 == 0, False)
                        mm(o, keys_lo[:, h, ks], xq_hi[:, b, cols], False, False)
                        last = mm(o, keys_hi[:, h, ks], xq_lo[:, b, cols], False, False)
                last.then_inc(e_done, 1)

            def energies(w, slot, b, cols):
                pe.wait_ge(x_exp, w - 1)
                keys = bass.ds(b * 128, 128)
                qh, ql = (a.rearrange("p b t -> p (b t)")[:, bass.ds(b * T + cols, 64)]
                          for a in (xq_hi[:, :, :], xq_lo[:, :, :]))
                for h in range(XH):
                    o = ps[:, 2 * slot + h // 8, 64 * (h % 8):64 * (h % 8) + 64]
                    mm(o, keys_hi[:, h, keys], qh, h % 8 == 0, False)
                    mm(o, keys_lo[:, h, keys], qh, False, False)
                    last = mm(o, keys_hi[:, h, keys], ql, False, False)
                last.then_inc(e_done, 1)

            def shift(w, slot):
                pe.wait_ge(x_max, w + 1)
                for half in range(2):
                    last = mm(ps[:, 2 * slot + half, :].rearrange("p (h q) -> p h q", q=64), minus_ident[:, :],
                              xm[:, slot, :].unsqueeze(1).broadcast_to([128, 8, 64]), False, True)
                last.then_inc(x_shift, 1)

            energies_left(0, 0, slice(0, 64), first=True)
            energies_left(1, 1, slice(64, 128), first=True)
            shift(0, 0)
            for w in range(2, UL):
                energies_left(w, w % 2, slice(64 * w, 64 * w + 64))
                shift(w - 1, (w - 1) % 2)
            energies(UL, 0, 0, 0)
            shift(UL - 1, 1)

            def weighted(b, q):
                n = 4 * b + q
                pe.wait_ge(x_lo_d, 2 * n + UL + 2)
                pe.wait_ge(x_lo_p, 2 * n + UL + 2)
                if q or not isinstance(b, int) or b > 0:
                    pe.wait_ge(x_out if q else resid2, n if q else b)
                s, cols = q % 2, slice(128 * q, 128 * q + 128)
                vals = [a[:, :, :].rearrange("p b n -> p (b n)") for a in (xv_hi, xv_lo, xvl_hi, xvl_lo)]
                for h in range(XH):
                    o = ps[:, 6, XD * h:XD * h + XD]
                    v_h, v_l, l_h, l_l = (a[:, bass.ds(b * 128 + XD * h, XD)] for a in vals)
                    mm(o, xa_hi[s][:, h, :], v_h, h == 0, False)
                    mm(o, xa_hi[s][:, h, :], v_l, False, False)
                    mm(o, xa_lo[s][:, h, :], v_h, False, False)
                    mm(o, left_hi[:, h, cols], l_h, False, False)
                    mm(o, left_hi[:, h, cols], l_l, False, False)
                    last = mm(o, left_lo[:, h, cols], l_h, False, True)
                last.then_inc(x_pv, 1)

            def turn_tile(b, q):
                pe.wait_ge(x_out, 4 * b + q + 1)
                pe.transpose(ps[:, 7, 128 * q:128 * q + 128], xo[:, :], ident).then_inc(x_turned, 1)

            def main_batch(b, static=False):
                for c in range(8):
                    w = 8 * b + UL + c
                    if c < 7:
                        energies(w + 1, (c + 1) % 2, b, 64 * (c + 1))
                    elif not static:
                        energies(w + 1, 0, b + 1, 0)
                    shift(w, c % 2)
                    if c in (2, 4, 6):
                        weighted(b, c // 2 - 1)
                    if c in (3, 5, 7):
                        if c == 3 and (not isinstance(b, int) or b > 0):
                            pe.wait_ge(normed3, 2 * b)
                        turn_tile(b, c // 2 - 1)
                weighted(b, 3)
                turn_tile(b, 3)
                pe.wait_ge(x_T, b + 1)
                mm(ps[:, 6, :], xw[:, 3, :], xoT[:, :], True, True).then_inc(x_proj, 1)
                pe.wait_ge(resid2, b + 1)
                mm(ps[:, 7, :], centre, xT[:, bass.ds(b * T, T)], True, True).then_inc(pe_ln3, 1)
                pe.wait_ge(act_ln3, 3 * b + 1)
                mm(ps[:, 6, :], mean, ln_sq[:, :], True, True).then_inc(pe_ln3, 1)
                pe.wait_ge(normed3, 2 * b + 2)
                for t in range(KT):
                    last = mm(ps[:, 5, bass.ds((b * KT + t) * E, E)], ln_out[:, t * 128:(t + 1) * 128],
                              proj_sb[:, :], True, True)
                last.then_inc(scored, 1)

            for b in range(B):
                main_batch(b, static=b == B - 1)

            def gates_in(b):
                if b:
                    pe.wait_ge(z1_out, b)
                else:
                    pe.wait_ge(a_done, 1)
                for t in range(KT):
                    last = pe.transpose(ps[0:E, 1, t * 128:(t + 1) * 128], gq[:, KT * b + t, :], ident)
                last.then_inc(aT_turned, 1)
                pe.wait_ge(aT_out, b + 1)
                if b:
                    pe.wait_ge(g_out, b)
                mm(ps[:, 0, :], c12_sb[:, :], aT, True, True).then_inc(g_done, 1)
                mm(ps[0:R, 1, :], win1_sb[:, :], xn3[:, b, :], True, True).then_inc(z1_done, 1)

            gates_in(0)
            for b in range(B):
                pe.wait_ge(z1_out, b + 1)
                for m in range(4):
                    if b:
                        pe.wait_ge(h_out, 4 * (b - 1) + m + 1)
                    mm(ps[:, 2 + m, :], wout1_sb[:, m * 128:(m + 1) * 128], z1, True, True).then_inc(h_done, 1)
                if b + 1 < B:
                    gates_in(b + 1)
                for m in range(4):
                    pe.wait_ge(h_out, 4 * b + m + 1)
                    last = mm(ps[R:2 * R, 6, :], win2_sb[:, m, :], hid[:, m, :], m == 0, m == 3)
                last.then_inc(z2_done, 1)
                pe.wait_ge(z2_out, b + 1)
                if b:
                    pe.wait_ge(stored, b)
                mm(ps[:, 7, :], wout2_sb[R:2 * R, :], z2[R:2 * R, :], True, True).then_inc(y_done, 1)


def kernel(**inputs):
    import concourse.bacc as bacc
    from concourse.bass_utils import run_bass_kernel_spmd

    def t(a, *axes):
        return np.ascontiguousarray(np.transpose(np.asarray(a), axes))

    g = {k: np.asarray(v) for k, v in inputs.items()}
    eye = np.eye(128, dtype=np.float32)
    heads = np.repeat(np.eye(XH, dtype=np.float32), XD, axis=0)
    left = np.zeros((128, B), np.float32)
    for b in range(B):
        left[SLP * b:SLP * b + SL, b] = 1.0
    full = np.full((128, 128), 1.0 / 128, np.float32)
    consts = np.concatenate([eye - full, full, eye, np.ones((128, 256), np.float32), heads, left,
                             np.tile(1.0 / np.arange(1, E + 1, dtype=np.float32), (128, 1))], axis=1)
    ctxT = t(g["ctx_1024"], 2, 0, 1)

    def col(a):
        return np.ascontiguousarray(a.reshape(-1, 1))

    arrays = {
        "x": t(g["x"], 2, 0, 1).reshape(D, B * T),
        "ctx_main": np.ascontiguousarray(ctxT[:, :, 0:128]).reshape(D, B * 128),
        "ctx_left": np.ascontiguousarray(ctxT[:, :, 128:]),
        "wq": t(g["L0_attn_W_Q"], 2, 0, 1).reshape(D, H * DH),
        "wk": t(g["L0_attn_W_K"], 2, 0, 1).reshape(D, H * DH),
        "wv": t(g["L0_attn_W_V"], 2, 0, 1).reshape(D, H * DH),
        "wo": t(g["L0_attn_W_O"].reshape(PAIRS, 2, D, DH), 1, 3, 0, 2).reshape(128, PAIRS, D),
        "bias_qkv": t(np.stack([g["L0_attn_b_Q"], g["L0_attn_b_K"], g["L0_attn_b_V"]]).reshape(3, PAIRS, 128), 2, 0, 1),
        "b_o": col(g["L0_attn_b_O"]),
        "xwq": t(g["L0_xattn_Wq_w"], 1, 0), "xwk": t(g["L0_xattn_Wk_w"], 1, 0),
        "xwv": t(g["L0_xattn_Wv_w"], 1, 0), "xwo": t(g["L0_xattn_Wo_w"], 1, 0),
        "xb": t(np.stack([g["L0_xattn_Wq_b"], g["L0_xattn_Wk_b"], g["L0_xattn_Wo_b"]]), 1, 0),
        "xbv": g["L0_xattn_Wv_b"].reshape(1, 128),
        "proj": g["L0_ffn_proj"],
        "c12": np.concatenate([g["L0_ffn_C1"], g["L0_ffn_C2"]], axis=1),
        "win1": np.ascontiguousarray(g["L0_ffn_Win1"][0:D]), "bin1": col(g["L0_ffn_Win1"][D]),
        "wout1": t(g["L0_ffn_Wout1"], 1, 0),
        "win2": t(g["L0_ffn_Win2"][0:O].reshape(O // 128, 128, R), 1, 0, 2), "bin2": col(g["L0_ffn_Win2"][O]),
        "wout2": t(g["L0_ffn_Wout2"], 1, 0),
        "consts": consts,
    }
    nc = bacc.Bacc("TRN2", target_bir_lowering=False, num_devices=1)
    args = [nc.dram_tensor(f"in_{k}", a.shape, mybir.dt.from_np(a.dtype), kind="ExternalInput").ap()
            for k, a in arrays.items()]
    out = nc.dram_tensor("out_T", (D, B * T), F32, kind="ExternalOutput").ap()
    decoder(nc, **dict(zip(arrays, args)), out=out)
    r = run_bass_kernel_spmd(nc, [{f"in_{k}": a for k, a in arrays.items()}], core_ids=[0])
    return t(r.results[0]["out_T"].reshape(D, B, T), 1, 2, 0)
```

```python
from contextlib import ExitStack

import numpy as np

import concourse.bass as bass
from concourse import mybir

F32 = mybir.dt.float32
F16 = mybir.dt.float16
BF16 = mybir.dt.bfloat16
ALU = mybir.AluOpType
ACT = mybir.ActivationFunctionType
AX_X = mybir.AxisListType.X

B, T, D = 4, 512, 128
H, DH = 16, 64
PAIRS = H // 2
NP = B * PAIRS
KT = T // 128
S = 154
SL = S - 128
SLP = 32
XH, XD = 16, 8
XT = B + 1
E, R, O = 16, 64, 512
TT = B * KT
EPS = 1e-5
MS = 64.0
DMAS = 4
LEAD, LAG, LOOP_FROM, LOOP_TO = 3, 1, 3, NP - 3


def late(n, first):
    return not isinstance(n, int) or n >= first


def absent(n):
    return isinstance(n, int) and not 0 <= n < NP


def decoder(nc, x, ctx_main, ctx_left, wq, wk, wv, wo, bias_qkv, b_o, xwq, xwk, xwv, xwo, xb, xbv,
            proj, c12, win1, bin1, wout1, win2, bin2, wout2, consts, out):
    with ExitStack() as stack:
        def sb(name, shape, dt):
            return stack.enter_context(nc.sbuf_tensor(name, shape, dt))

        def sem(name):
            return stack.enter_context(nc.semaphore(name))

        cst = sb("cst", [128, 5 * 128 + 16 + B + 16], F32)
        centre, mean, ident = cst[:, 0:128], cst[:, 128:256], cst[:, 256:384]
        head_mask = cst[:, 640:656]
        batch_mask = cst[:, 656:660]
        inv_k = cst[:, 660:676]
        minus_ident = sb("minus_ident", [128, 128], BF16)
        ones_row = cst[:, 384:512]
        xT = sb("xT", [128, B * T], F32)
        biases = sb("biases", [128, 3, PAIRS], F32)
        w_split = sb("w_split", [128, 2 * 3 * H * DH], F16)
        w_hi = w_split[:, 0:3 * H * DH].rearrange("p (a n) -> p a n", a=3)
        w_lo = w_split[:, 3 * H * DH:].rearrange("p (a n) -> p a n", a=3)
        xn3 = w_split[:, 0:2 * B * T].bitcast(F32).rearrange("p (b t) -> p b t", b=B)
        wo_hi = sb("wo_hi", [128, PAIRS, D], F16)
        wo_lo = sb("wo_lo", [128, PAIRS, D], F16)
        bo = sb("bo", [128, 1], F32)
        xw = sb("xw", [128, 4, 128], F32)
        xbias = sb("xbias", [128, 3], F32)
        xbv_row = sb("xbv_row", [1, 128], F32)
        proj_sb = sb("proj_sb", [128, E], F32)
        c12_sb = sb("c12_sb", [E, 2 * R], F32)
        win1_sb = sb("win1_sb", [128, R], F32)
        wout1_sb = sb("wout1_sb", [R, O], F32)
        win2_sb = sb("win2_sb", [128, O // 128, R], F32)
        wout2_sb = sb("wout2_sb", [128, D], F32)
        bin_sb = sb("bin_sb", [128, 1], F32)
        eps = sb("eps", [128, 1], F32)
        xn_hi = sb("xn_hi", [128, B, T], F16)
        xn_lo = sb("xn_lo", [128, B, T], F16)

        r1 = sb("r1", [128, 64 * 1024 // 4], F32)
        w_raw = r1[:, 0:3 * 1024].rearrange("p (a n) -> p a n", a=3)
        wo_raw = r1[:, 3 * 1024:4 * 1024].rearrange("p (a n) -> p a n", a=PAIRS)
        r1h = r1[:, :].bitcast(F16)
        oT_hi = r1h[:, 0:NP * T].rearrange("p (n t) -> p n t", n=NP)
        oT_lo = r1h[:, NP * T:2 * NP * T].rearrange("p (n t) -> p n t", n=NP)
        left = r1[:, 0:XH * T].rearrange("p (h t) -> p h t", h=XH)
        left_hi = left.bitcast(BF16).rearrange("p h (t two) -> p h t two", two=2)[:, :, :, 1]
        left_lo = r1h[:, 2 * XH * T:3 * XH * T].rearrange("p (h t) -> p h t", h=XH)

        r2 = sb("r2", [128, 40 * 1024 // 4], F32)
        r2h = r2[:, :].bitcast(F16)

        def r2_f16(start, n):
            return r2h[:, start:start + n]
        prob = r2[:, 0:2 * KT * T].rearrange("p (h k t) -> p h k t", h=2, k=KT)
        prob_hi = prob.bitcast(BF16).rearrange("p h k (t two) -> p h k t two", two=2)[:, :, :, :, 1]
        base = 4 * KT * T
        prob_lo = r2_f16(base, 2 * KT * T).rearrange("p (h k t) -> p h k t", h=2, k=KT)
        base += 2 * KT * T
        stacks = r2_f16(base, 16 * T).rearrange("p (s h j t) -> p s h j t", s=2, h=2, j=4)
        qa, kb, qb, ka = (stacks[:, :, :, j, :] for j in range(4))
        keys_hi = r2_f16(0, XH * XT * 128).rearrange("p (h k) -> p h k", h=XH)
        keys_lo = r2_f16(XH * XT * 128, XH * XT * 128).rearrange("p (h k) -> p h k", h=XH)

        xe_f32 = sb("xe", [128, 2 * XH * 64], F32)
        parts_0 = sb("parts", [128, 5 * T], F16)
        parts = [parts_0[:, :].rearrange("p (j t) -> p j t", j=5),
                 xe_f32[:, :].bitcast(F16)[:, 0:5 * T]]
        parts[1] = parts[1].rearrange("p (j t) -> p j t", j=5)
        v_hi_t = sb("v_hi", [128, 2, KT, 2, DH + 1], F16)
        v_lo_t = sb("v_lo", [128, 2, KT, 2, DH], F16)
        bias_now = sb("bias_now", [128, 2, 2], F32)
        m_q = sb("m_q", [128, 2, KT, 2], F32)
        m_row = sb("m_row", [2, T], F16)
        rsum = sb("rsum", [128, 2, KT], F32)
        o_hi = sb("o_hi", [128, T], F16)
        o_n = sb("o_n", [128, KT, 2, DH], F32)
        ln_sq = sb("ln_sq", [128, T], F32)
        ln_lg = sb("ln_lg", [128, T], F32)
        ln_rs = sb("ln_rs", [128, T], F32)
        ln_out = sb("ln_out", [128, T], F32)
        ctx_sb = sb("ctx_sb", [128, XT * 128], F32)
        kT_hi = sb("kT_hi", [128, XT * 128], F16)
        kT_lo = sb("kT_lo", [128, XT * 128], F16)
        xv_hi = sb("xv_hi", [128, B, 128], F16)
        xv_lo = sb("xv_lo", [128, B, 128], F16)
        xvl_hi = sb("xvl_hi", [128, B, 128], F16)
        xvl_lo = sb("xvl_lo", [128, B, 128], F16)
        xq_hi, xq_lo = xn_hi, xn_lo
        xm = sb("xm", [128, 2, 64], BF16)
        xe = xe_f32[:, 0:2 * XH * 64].rearrange("p (s h q) -> p s h q", s=2, h=XH)
        xs8 = sb("xs8", [128, 8, 64], F32)
        xs4 = sb("xs4", [128, 4, 64], F32)
        xs2 = sb("xs2", [128, 2, 2, 64], F32)
        xsum = sb("xsum", [128, 64], F32)
        xrec = sb("xrec", [128, 2, 64], F32)
        xa0 = sb("xa0", [128, XH, 128], F32)
        xal0 = sb("xal0", [128, XH, 128], F16)
        free1 = XH * T + XH * T // 2
        xa1 = r1[:, free1:free1 + XH * 128].rearrange("p (h t) -> p h t", h=XH)
        free1 = 2 * (free1 + XH * 128)
        xal1 = r1h[:, free1:free1 + XH * 128].rearrange("p (h t) -> p h t", h=XH)
        xa, xa_lo = [xa0[:, :, :], xa1], [xal0[:, :, :], xal1]
        xa_hi = [a.bitcast(BF16).rearrange("p h (t two) -> p h t two", two=2)[:, :, :, 1] for a in xa]
        xo = sb("xo", [128, KT, 128], F32)
        xoT = sb("xoT", [128, T], F32)
        hid = r2[:, 0:O // 128 * T].rearrange("p (m t) -> p m t", m=O // 128)
        gates, z2 = r2[:, 2048:2560], r2[:, 3072:3584]
        z1, aT = r2[0:R, 2560:3072], r2[0:E, 3584:4096]
        c_a, c_b = (r2[:, n:n + 512].rearrange("p (a t e) -> p a t e", a=2, t=TT) for n in (4096, 4608))
        gz, gs, gq = (r2[:, n:n + 256].rearrange("p (t e) -> p t e", t=TT) for n in (5120, 5376, 5632))
        g1 = sb("g1", [128, TT], F32)

        ps = stack.enter_context(nc.psum_tensor("ps", [128, 8, 512], F32))
        st = [ps[:, 0:2, :], ps[:, 2:4, :]]
        bank_p, bank_s, bank_o = ps[:, 4, :], [ps[:, 5, :], ps[:, 6, :]], ps[:, 7, :]

        loaded = sem("loaded")
        loaded_x = sem("loaded_x")
        loaded_w = sem("loaded_w")
        stored = sem("stored")
        setup = sem("setup")
        w_hi_done = sem("w_hi_done")
        w_lo_done = sem("w_lo_done")
        pe_ln = sem("pe_ln")
        act_ln = sem("act_ln")
        dve_ln = sem("dve_ln")
        bias_done = sem("bias_done")
        q_proj, k_proj, v_proj = sem("q_proj"), sem("k_proj"), sem("v_proj")
        k_hi2 = sem("k_hi2")
        q_hi, k_hi, v_hi = sem("q_hi_done"), sem("k_hi_done"), sem("v_hi_done")
        q_lo, k_lo, v_lo = sem("q_lo_done"), sem("k_lo_done"), sem("v_lo_done")
        stacked, m_placed = sem("stacked"), sem("m_placed")
        s_done, max_done = sem("s_done"), sem("max_done")
        m_turned, m_out = sem("m_turned"), sem("m_out")
        st_done = [sem("st_done_0"), sem("st_done_1")]
        exp_done = [sem("exp_done_0"), sem("exp_done_1")]
        lo_dve, lo_pool = sem("lo_dve"), sem("lo_pool")
        pv_done, r_done, o_done = sem("pv_done"), sem("r_done"), sem("o_done")
        oT_turned, oT_hi_done, oT_done = sem("oT_turned"), sem("oT_hi_done"), sem("oT_done")
        oT_kept = sem("oT_kept")
        bo_done, bo_added = sem("bo_done"), sem("bo_added")
        minus_done, ctx_k, ctx_v, key_parts, val_parts = (sem(n) for n in (
            "minus_done", "ctx_k", "ctx_v", "key_parts", "val_parts"))
        key_hi_done, val_hi_done, masked = (sem(n) for n in ("key_hi_done", "val_hi_done", "masked"))
        proj_o, resid, pe_ln2, act_ln2, normed, xq_done, xq_parts = (sem(n) for n in (
            "proj_o", "resid", "pe_ln2", "act_ln2", "normed", "xq_done", "xq_parts"))
        e_done, x_max, x_shift, x_exp, x_tree, x_sum, x_rec, x_norm, x_lo_d, x_lo_p = (sem(n) for n in (
            "e_done", "x_max", "x_shift", "x_exp", "x_tree", "x_sum", "x_rec", "x_norm", "x_lo_d", "x_lo_p"))
        x_add = sem("x_add")
        x_pv, x_out, x_turned, x_T, x_proj, resid2, pe_ln3, act_ln3, normed3, scored = (sem(n) for n in (
            "x_pv", "x_out", "x_turned", "x_T", "x_proj", "resid2", "pe_ln3", "act_ln3", "normed3", "scored"))
        g_step, g_act, a_done, aT_turned, aT_out, g_done, g_out = (sem(n) for n in (
            "g_step", "g_act", "a_done", "aT_turned", "aT_out", "g_done", "g_out"))
        z1_done, z1_out, h_done, h_out, z2_done, z2_out, y_done = (sem(n) for n in (
            "z1_done", "z1_out", "h_done", "h_out", "z2_done", "z2_out", "y_done"))

        W_LOADS = 4
        X_LOADS = 3
        OTHER_LOADS = 18
        GSQRT = 7 + 3 * TT + 2 + 8 + 6
        UL, UM = T // 64, B * T // 64

        block = stack.enter_context(nc.Block())

        @block.sync
        def _(sp):
            for b in range(B):
                sp.dma_start(xT[:, b * T:(b + 1) * T], x[:, b * T:(b + 1) * T]).then_inc(loaded_x, 16)
                if b == 0:
                    sp.dma_start(cst[:, :], consts).then_inc(loaded_x, 16)
            for j, w in enumerate((wq, wk, wv)):
                sp.dma_start(w_raw[:, j, :], w).then_inc(loaded_w, 16)
            sp.dma_start(wo_raw, wo).then_inc(loaded_w, 16)
            sp.dma_start(biases[:, :, :], bias_qkv).then_inc(loaded, 16)
            sp.dma_start(bo[:, :], b_o).then_inc(loaded, 16)
            for j, w in enumerate((xwq, xwk, xwv, xwo)):
                sp.dma_start(xw[:, j, :], w).then_inc(loaded, 16)
            sp.dma_start(xbias[:, :], xb).then_inc(loaded, 16)
            sp.dma_start(xbv_row[:, :], xbv).then_inc(loaded, 16)
            sp.dma_start(proj_sb[:, :], proj).then_inc(loaded, 16)
            sp.dma_start(c12_sb[:, :], c12).then_inc(loaded, 16)
            sp.dma_start(win1_sb[:, :], win1).then_inc(loaded, 16)
            sp.dma_start(wout1_sb[:, :], wout1).then_inc(loaded, 16)
            sp.dma_start(win2_sb[:, :, :], win2).then_inc(loaded, 16)
            sp.dma_start(wout2_sb[R:2 * R, :], wout2).then_inc(loaded, 16)
            sp.dma_start(bin_sb[0:R, :], bin1).then_inc(loaded, 16)
            sp.dma_start(bin_sb[R:2 * R, :], bin2).then_inc(loaded, 16)
            sp.dma_start(ctx_sb[:, 0:B * 128], ctx_main).then_inc(loaded, 16)
            sp.wait_ge(setup, 1)
            sp.dma_start(ctx_sb[:, B * 128:].rearrange("p (b k) -> p b k", b=B)[:, :, 0:SL],
                         ctx_left).then_inc(loaded, 16)

            def reg(n):
                return n if isinstance(n, int) else sp.to_reg(n)

            def stack_pair(n, slot):
                if absent(n):
                    return
                pairs, used, placed = reg(n + 1), reg(2 * n - 2), reg(16 * DMAS * n)
                if late(n, 2):
                    sp.wait_ge(st_done[0], used)
                    sp.wait_ge(st_done[1], used)
                if late(n, 1):
                    sp.wait_ge(stacked, placed)
                sp.wait_ge(q_hi, pairs)
                sp.wait_ge(k_hi, pairs)
                sp.wait_ge(q_lo, pairs)
                sp.wait_ge(k_lo, pairs)
                sp.wait_ge(k_hi2, pairs)
                for h in range(2):
                    rows = slice(DH * h, DH * h + DH)
                    sp.dma_start(stacks[0:DH, slot, h, :, :], parts[slot][rows, 0:4, :]).then_inc(stacked, 16)
                    sp.dma_start(stacks[DH:128, slot, h, 0:4:3, :], parts[slot][rows, 0:5:4, :]).then_inc(stacked, 16)

            def place_maxima(n, slot):
                sp.wait_ge(m_out, reg(n + 1))
                sp.dma_start(qb[DH:DH + 1, slot, :, :], m_row[:, :]).then_inc(m_placed, 16)

            stack_pair(0, 0)
            stack_pair(1, 1)
            place_maxima(0, 0)
            stack_pair(2, 0)
            place_maxima(1, 1)
            with sp.Fori(0, (NP - 4) // 2) as it:
                stack_pair(2 * it + 3, 1)
                place_maxima(2 * it + 2, 0)
                stack_pair(2 * it + 4, 0)
                place_maxima(2 * it + 3, 1)
            stack_pair(NP - 1, 1)
            place_maxima(NP - 2, 0)
            place_maxima(NP - 1, 1)
            for b in range(B):
                sp.wait_ge(stored, b + 1)
                sp.dma_start(out[:, b * T:(b + 1) * T], xT[:, b * T:(b + 1) * T]).then_inc(m_placed, 16)
            sp.wait_ge(m_placed, 16 * (NP + B))

        @block.gpsimd
        def _(pool):
            pool.memset(ctx_sb[:, B * 128:], 0.0).then_inc(setup, 1)
            pool.wait_ge(setup, 1)
            pool.memset(kb[DH:DH + 1, :, :, :], MS).then_inc(setup, 1)
            pool.wait_ge(setup, 2)
            pool.memset(v_hi_t[:, :, :, :, DH:DH + 1], 1.0).then_inc(setup, 1)
            pool.wait_ge(setup, 3)
            pool.memset(eps[:, :], EPS).then_inc(setup, 1)

            def low_parts(g, h):
                for half, tiles in enumerate((slice(1, 2), slice(2, 4))):
                    pool.wait_ge(exp_done[half], g + 1)
                    pool.tensor_tensor(prob_lo[:, h, tiles, :], prob[:, h, tiles, :], prob_hi[:, h, tiles, :],
                                       ALU.subtract).then_inc(lo_pool, 1)

            with pool.Fori(0, NP) as i:
                low_parts(2 * i, 0)
                low_parts(2 * i + 1, 1)

            def sum_heads(w, slot, first=False):
                pool.wait_ge(x_exp, w + 1)
                e = xe[:, slot, :, :]
                pool.tensor_tensor(xs8[:, :, :], e[:, 0:8, :], e[:, 8:16, :], ALU.add).then_inc(x_tree, 1)
                pool.wait_ge(x_tree, 2 * w + 1)
                pool.tensor_tensor(xs4[:, :, :], xs8[:, 0:4, :], xs8[:, 4:8, :], ALU.add).then_inc(x_tree, 1)
                pool.wait_ge(x_tree, 2 * w + 2)
                if not first:
                    pool.wait_ge(x_add, w - 1)
                pool.tensor_tensor(xs2[:, slot, :, :], xs4[:, 0:2, :], xs4[:, 2:4, :], ALU.add).then_inc(x_sum, 1)

            def weights_low(w, a, hi, lo, cols):
                pool.wait_ge(x_norm, w + 1)
                pool.tensor_tensor(lo[:, 8:16, cols], a[:, 8:16, cols], hi[:, 8:16, cols],
                                   ALU.subtract).then_inc(x_lo_p, 1)

            for u in range(2):
                sum_heads(u, u, first=True)
                if u:
                    weights_low(0, left, left_hi, left_lo, slice(0, 64))
            with pool.Fori(0, UL // 2 - 1) as it:
                for j in range(2):
                    w = 2 * it + 2 + j
                    sum_heads(w, j)
                    weights_low(w - 1, left, left_hi, left_lo, bass.ds((w - 1) * 64, 64))

            def main_low(w, c):
                q, cols = c // 2 % 2, slice(64 * (c % 2), 64 * (c % 2) + 64)
                weights_low(w, xa[q], xa_hi[q], xa_lo[q], cols)

            sum_heads(UL, 0)
            weights_low(UL - 1, left, left_hi, left_lo, slice((UL - 1) * 64, UL * 64))
            for c in range(1, 8):
                sum_heads(UL + c, c % 2)
                main_low(UL + c - 1, c - 1)
            with pool.Fori(1, B) as b:
                for c in range(8):
                    w = 8 * b + UL + c
                    sum_heads(w, c % 2)
                    main_low(w - 1, (c - 1) % 8)
            main_low(UL + UM - 1, 7)

        @block.scalar
        def _(act):
            act.wait_ge(setup, 4)
            act.wait_ge(loaded_w, 16 * W_LOADS)

            def norm_scale(n, pe_s, act_s, centred, variance):
                act.wait_ge(pe_s, 2 * n + 1)
                act.activation(ln_sq[:, :], centred, ACT.Square).then_inc(act_s, 1)
                act.wait_ge(pe_s, 2 * n + 2)
                act.activation(ln_lg[:, :], variance, ACT.Ln, bias=eps[:, :]).then_inc(act_s, 1)
                act.wait_ge(act_s, 3 * n + 2)
                act.activation(ln_rs[:, :], ln_lg[:, :], ACT.Exp, scale=-0.5).then_inc(act_s, 1)

            for b in range(B):
                if b < 3:
                    act.activation(w_hi[:, b, :], w_raw[:, b, :], ACT.Copy).then_inc(w_hi_done, 1)
                else:
                    act.activation(wo_hi[:, :, :], wo_raw, ACT.Copy).then_inc(w_hi_done, 1)
                if b >= 1:
                    act.wait_ge(dve_ln, 3 * b)
                norm_scale(b, pe_ln, act_ln, bank_p, bank_s[0])

            act.wait_ge(ctx_k, 1)
            act.activation(kT_hi[:, 0:512], ps[:, 0, :], ACT.Identity, bias=xbias[:, 1:2]).then_inc(key_hi_done, 1)
            act.activation(kT_hi[:, 512:640], ps[:, 1, 0:128], ACT.Identity, bias=xbias[:, 1:2]).then_inc(key_hi_done, 1)
            act.wait_ge(ctx_v, 1)
            act.activation(xv_hi[:, :, :].rearrange("p b n -> p (b n)"), ps[:, 2, :], ACT.Copy).then_inc(val_hi_done, 1)
            for b in range(B):
                act.activation(xvl_hi[:, b, :], ps[:, 3, 0:128], ACT.Copy, scale=batch_mask[:, b:b + 1]).then_inc(val_hi_done, 1)

            def q_high(n, slot):
                if absent(n):
                    return
                act.wait_ge(q_proj, n + 1)
                act.wait_ge(bias_done, n + 1)
                if late(n, 2):
                    act.wait_ge(stacked, 16 * DMAS * (n - 1))
                act.activation(parts[slot][:, 0, :], bank_p, ACT.Identity, bias=bias_now[:, slot, 0:1]).then_inc(q_hi, 1)

            def k_high(n, slot):
                if absent(n):
                    return
                act.wait_ge(k_proj, n + 1)
                act.activation(parts[slot][:, 1, :], bank_p, ACT.Identity, bias=bias_now[:, slot, 1:2]).then_inc(k_hi, 1)

            def v_high(n, slot):
                if absent(n):
                    return
                act.wait_ge(v_proj, n + 1)
                if late(n, 2):
                    act.wait_ge(pv_done, 2 * n - 2)
                act.activation(v_hi_t[:, slot, :, :, 0:DH],
                               bank_p.rearrange("p (k h d) -> p k h d", k=KT, h=2), ACT.Copy).then_inc(v_hi, 1)

            def exp_half(n, h, half):
                if absent(n):
                    return
                act.wait_ge(st_done[half], 2 * n + h + 1)
                if late(n, 1):
                    act.wait_ge(pv_done, 2 * n - 1 + h)
                act.activation(prob[:, h, 2 * half:2 * half + 2, :], st[half], ACT.Exp,
                               scale=DH ** -0.5).then_inc(exp_done[half], 1)

            def m_rows(n):
                if absent(n):
                    return
                act.wait_ge(m_turned, n + 1)
                if late(n, 1):
                    act.wait_ge(m_placed, 16 * n)
                act.activation(m_row[:, :], bank_s[0][0:2, :], ACT.Copy, scale=-1.0 / MS).then_inc(m_out, 1)

            def out_high(n):
                if absent(n):
                    return
                act.wait_ge(oT_turned, n + 1)
                if late(n, 1):
                    act.wait_ge(oT_done, n)
                    act.wait_ge(oT_kept, n)
                act.activation(o_hi[:, :], bank_o, ACT.Copy).then_inc(oT_hi_done, 1)

            def step(i, s):
                exp_half(i, 0, 0)
                out_high(i - 1)
                exp_half(i, 0, 1)
                v_high(i + 1, 1 - s)
                exp_half(i, 1, 0)
                exp_half(i, 1, 1)
                q_high(i + 3, 1 - s)
                m_rows(i + 1)
                k_high(i + 3, 1 - s)

            for i in range(-LEAD, LOOP_FROM):
                step(i, i % 2)
            with act.Fori(LOOP_FROM // 2, LOOP_TO // 2) as it:
                step(2 * it + 1, 1)
                step(2 * it + 2, 0)
            for i in range(LOOP_TO, NP + LAG):
                step(i, i % 2)

            for b in range(B):
                if b:
                    act.wait_ge(normed, b)
                norm_scale(b, pe_ln2, act_ln2, ps[:, 1, :], ps[:, 2, :])
            act.wait_ge(key_parts, 2)
            act.wait_ge(pv_done, 2 * NP)
            for h in range(XH):
                act.activation(keys_lo[:, h, :], kT_lo[:, :], ACT.Copy, scale=head_mask[:, h:h + 1]).then_inc(masked, 1)

            def exp_unit(w, slot, first=False):
                act.wait_ge(x_shift, w + 1)
                if not first:
                    act.wait_ge(x_norm, w - 1)
                act.activation(xe[:, slot, :, :], ps[:, 2 * slot:2 * slot + 2, :].rearrange(
                    "p a (h q) -> p (a h) q", q=64), ACT.Exp, scale=XD ** -0.5).then_inc(x_exp, 1)

            for w in range(2):
                exp_unit(w, w, first=True)
            with act.Fori(0, UL // 2 - 1) as it:
                for j in range(2):
                    exp_unit(2 * it + 2 + j, j)

            def out_tile(b, q):
                act.wait_ge(x_pv, 4 * b + q + 1)
                act.activation(xo[:, q, :], ps[:, 6, 128 * q:128 * q + 128], ACT.Copy).then_inc(x_out, 1)

            def turned_out(b):
                act.wait_ge(x_turned, b + 1)
                if late(b, 1):
                    act.wait_ge(x_proj, b)
                act.activation(xoT[:, :], ps[:, 7, :], ACT.Copy).then_inc(x_T, 1)

            def main_batch(b, prev):
                for c in range(8):
                    exp_unit(8 * b + UL + c, c % 2)
                    if prev is not None:
                        if c == 0:
                            out_tile(prev, 2)
                        if c == 2:
                            out_tile(prev, 3)
                        if c == 3:
                            turned_out(prev)
                        if c == 5:
                            norm_scale(prev, pe_ln3, act_ln3, ps[:, 4, :], ps[:, 7, :])
                    if c in (4, 6):
                        if c == 4 and prev is not None:
                            act.wait_ge(x_turned, b)
                        out_tile(b, c // 2 - 2)

            main_batch(0, None)
            main_batch(1, 0)
            with act.Fori(2, B) as b:
                main_batch(b, b - 1)
            out_tile(B - 1, 2)
            out_tile(B - 1, 3)
            turned_out(B - 1)
            norm_scale(B - 1, pe_ln3, act_ln3, ps[:, 4, :], ps[:, 7, :])

            act.wait_ge(g_step, 4)
            act.activation(g1[:, :], g1[:, :], ACT.Ln, bias=eps[:, :], scale=1.0 / E).then_inc(g_act, 1)
            act.wait_ge(g_act, 1)
            act.activation(g1[:, :], g1[:, :], ACT.Exp, scale=-0.5).then_inc(g_act, 1)
            act.wait_ge(g_step, GSQRT)
            act.activation(gs, gs, ACT.Sqrt).then_inc(g_act, 1)
            for b in range(B):
                act.wait_ge(aT_turned, b + 1)
                if b:
                    act.wait_ge(g_done, b)
                act.activation(aT, ps[0:E, 1, :], ACT.Copy).then_inc(aT_out, 1)
                act.wait_ge(g_done, b + 1)
                if b:
                    act.wait_ge(z2_out, b)
                act.activation(gates, ps[:, 0, :], ACT.Copy).then_inc(g_out, 1)
                for m in range(4):
                    act.wait_ge(h_done, 4 * b + m + 1)
                    if b:
                        act.wait_ge(z2_done, b)
                    act.activation(hid[:, m, :], ps[:, 2 + m, :], ACT.Gelu).then_inc(h_out, 1)

        @block.vector
        def _(dve):
            dve.wait_ge(loaded_x, 16 * (B + 1))
            dve.wait_ge(loaded, 16 * OTHER_LOADS)
            dve.tensor_scalar(minus_ident[:, :], ident, -1.0, None, ALU.mult).then_inc(w_lo_done, 1)
            for b in range(B):
                dve.wait_ge(w_hi_done, b + 1)
                if b < 3:
                    dve.tensor_tensor(w_lo[:, b, :], w_raw[:, b, :], w_hi[:, b, :], ALU.subtract).then_inc(w_lo_done, 1)
                else:
                    dve.tensor_tensor(wo_lo[:, :, :], wo_raw, wo_hi[:, :, :], ALU.subtract).then_inc(w_lo_done, 1)
                dve.wait_ge(act_ln, 3 * b + 3)
                if b >= 1:
                    dve.wait_ge(dve_ln, 3 * b)
                dve.tensor_tensor(ln_out[:, :], bank_p, ln_rs[:, :], ALU.mult).then_inc(dve_ln, 1)
                dve.wait_ge(dve_ln, 3 * b + 1)
                dve.tensor_copy(xn_hi[:, b, :], ln_out[:, :]).then_inc(dve_ln, 1)
                dve.wait_ge(dve_ln, 3 * b + 2)
                dve.tensor_tensor(xn_lo[:, b, :], ln_out[:, :], xn_hi[:, b, :], ALU.subtract).then_inc(dve_ln, 1)

            dve.wait_ge(bo_done, 1)
            dve.tensor_tensor(bo[:, :], ps[:, 7, 0:1], bo[:, :], ALU.add).then_inc(bo_added, 1)
            dve.wait_ge(key_hi_done, 2)
            dve.scalar_tensor_tensor(kT_lo[:, 0:512], ps[:, 0, :], xbias[:, 1:2], kT_hi[:, 0:512],
                                     ALU.add, ALU.subtract).then_inc(key_parts, 1)
            dve.scalar_tensor_tensor(kT_lo[:, 512:640], ps[:, 1, 0:128], xbias[:, 1:2], kT_hi[:, 512:640],
                                     ALU.add, ALU.subtract).then_inc(key_parts, 1)
            dve.wait_ge(val_hi_done, B + 1)
            dve.tensor_tensor(xv_lo[:, :, :].rearrange("p b n -> p (b n)"), ps[:, 2, :],
                              xv_hi[:, :, :].rearrange("p b n -> p (b n)"), ALU.subtract).then_inc(val_parts, 1)
            for b in range(B):
                dve.scalar_tensor_tensor(xvl_lo[:, b, :], ps[:, 3, 0:128], batch_mask[:, b:b + 1], xvl_hi[:, b, :],
                                         ALU.mult, ALU.subtract).then_inc(val_parts, 1)

            def bias_copy(n, slot):
                if absent(n):
                    return
                if late(n, 2):
                    dve.wait_ge(k_lo, n - 1)
                dve.tensor_copy(bias_now[:, slot, :], biases[:, 0:2, bass.ds(n % PAIRS, 1)].rearrange("p a b -> p (a b)")).then_inc(bias_done, 1)

            def q_low(n, slot):
                if absent(n):
                    return
                dve.wait_ge(bias_done, n + 1)
                dve.wait_ge(q_hi, n + 1)
                if late(n, 2):
                    dve.wait_ge(stacked, 16 * DMAS * (n - 1))
                dve.scalar_tensor_tensor(parts[slot][:, 2, :], bank_p, bias_now[:, slot, 0:1], parts[slot][:, 0, :],
                                         ALU.add, ALU.subtract).then_inc(q_lo, 1)

            def k_low(n, slot):
                if absent(n):
                    return
                dve.wait_ge(k_hi, n + 1)
                dve.scalar_tensor_tensor(parts[slot][:, 4, :], bank_p, bias_now[:, slot, 1:2], parts[slot][:, 1, :],
                                         ALU.add, ALU.subtract).then_inc(k_lo, 1)

            def k_again(n, slot):
                if absent(n):
                    return
                dve.wait_ge(k_hi, n + 1)
                dve.tensor_copy(parts[slot][:, 3, :], parts[slot][:, 1, :]).then_inc(k_hi2, 1)

            def v_low(n, slot):
                if absent(n):
                    return
                dve.wait_ge(v_hi, n + 1)
                dve.tensor_tensor(v_lo_t[:, slot, :, :, :], bank_p.rearrange("p (k h d) -> p k h d", k=KT, h=2),
                                  v_hi_t[:, slot, :, :, 0:DH], ALU.subtract).then_inc(v_lo, 1)

            def low_parts(n, h):
                if absent(n):
                    return
                dve.wait_ge(exp_done[0], 2 * n + h + 1)
                dve.tensor_tensor(prob_lo[:, h, 0, :], prob[:, h, 0, :], prob_hi[:, h, 0, :],
                                  ALU.subtract).then_inc(lo_dve, 1)

            o_view = bank_o[:, 0:KT * (DH + 1)].rearrange("p (q d) -> p q d", q=KT)

            def normalise(n, h):
                if absent(n):
                    return
                dve.wait_ge(pv_done, 2 * n + h + 1)
                dve.reciprocal(rsum[:, h, :], o_view[:, :, DH]).then_inc(r_done, 1)
                dve.wait_ge(r_done, 2 * n + h + 1)
                if late(n, 1):
                    dve.wait_ge(oT_turned, n)
                dve.tensor_tensor(o_n[:, :, h, :], o_view[:, :, 0:DH],
                                  rsum[:, h, :].unsqueeze(2).broadcast_to([128, KT, DH]), ALU.mult).then_inc(o_done, 1)

            def out_low(n):
                if absent(n):
                    return
                dve.wait_ge(oT_hi_done, n + 1)
                dve.tensor_tensor(oT_lo[:, bass.ds(n, 1), :].rearrange("p a t -> p (a t)"), bank_o, o_hi[:, :],
                                  ALU.subtract).then_inc(oT_done, 1)

            def out_keep(n):
                if absent(n):
                    return
                dve.tensor_copy(oT_hi[:, bass.ds(n, 1), :].rearrange("p a t -> p (a t)"), o_hi[:, :]).then_inc(oT_kept, 1)

            def maximum(n, slot, c):
                if absent(n):
                    return
                h, q = c // KT, c % KT
                dve.wait_ge(s_done, 8 * n + c + 1)
                dve.reduce_max(m_q[:, slot, q, h:h + 1], bank_s[c % 2], AX_X).then_inc(max_done, 1)

            def step(i, s):
                maximum(i + 1, 1 - s, 2)
                k_again(i + 2, s)
                out_low(i - 1)
                maximum(i + 1, 1 - s, 3)
                v_low(i + 1, 1 - s)
                low_parts(i, 0)
                maximum(i + 1, 1 - s, 4)
                bias_copy(i + 3, 1 - s)
                maximum(i + 1, 1 - s, 5)
                maximum(i + 1, 1 - s, 6)
                maximum(i + 1, 1 - s, 7)
                q_low(i + 3, 1 - s)
                normalise(i, 0)
                out_keep(i - 1)
                low_parts(i, 1)
                maximum(i + 2, s, 0)
                maximum(i + 2, s, 1)
                k_low(i + 3, 1 - s)
                normalise(i, 1)

            for i in range(-LEAD, LOOP_FROM):
                step(i, i % 2)
            with dve.Fori(LOOP_FROM // 2, LOOP_TO // 2) as it:
                step(2 * it + 1, 1)
                step(2 * it + 2, 0)
            for i in range(LOOP_TO, NP + LAG):
                step(i, i % 2)

            def resid_sum(b, bias, bank, done):
                dve.scalar_tensor_tensor(xT[:, b * T:(b + 1) * T], bank, bias, xT[:, b * T:(b + 1) * T],
                                         ALU.add, ALU.add).then_inc(done, 1)

            dve.wait_ge(bo_added, 1)
            for b in range(B):
                dve.wait_ge(proj_o, b + 1)
                resid_sum(b, bo[:, :], ps[:, 0, :], resid)
                dve.wait_ge(act_ln2, 3 * b + 3)
                if b:
                    dve.wait_ge(xq_done, b)
                dve.tensor_tensor(ln_out[:, :], ps[:, 1, :], ln_rs[:, :], ALU.mult).then_inc(normed, 1)
                dve.wait_ge(xq_done, b + 1)
                dve.tensor_scalar(xq_hi[:, b, :], ps[:, 3, :], xbias[:, 0:1], None, ALU.add).then_inc(xq_parts, 1)
                dve.wait_ge(xq_parts, 2 * b + 1)
                dve.scalar_tensor_tensor(xq_lo[:, b, :], ps[:, 3, :], xbias[:, 0:1], xq_hi[:, b, :],
                                         ALU.add, ALU.subtract).then_inc(xq_parts, 1)
            dve.wait_ge(pv_done, 2 * NP)
            for h in range(XH):
                dve.tensor_scalar(keys_hi[:, h, :], kT_hi[:, :], head_mask[:, h:h + 1], None, ALU.mult).then_inc(masked, 1)

            def max_heads(w, slot, first=False):
                dve.wait_ge(e_done, w + 1)
                if not first:
                    dve.wait_ge(x_shift, w - 1)
                dve.tensor_reduce(xm[:, slot, :], ps[:, 2 * slot:2 * slot + 2, :].rearrange(
                    "p a (h q) -> p q (a h)", q=64), AX_X, ALU.max).then_inc(x_max, 1)

            def weights(w, slot, a, hi, lo, cols, free=None):
                dve.wait_ge(x_sum, w + 1)
                dve.tensor_tensor(xsum[:, :], xs2[:, slot, 0, :], xs2[:, slot, 1, :], ALU.add).then_inc(x_add, 1)
                dve.wait_ge(x_add, w + 1)
                dve.reciprocal(xrec[:, slot, :], xsum[:, :]).then_inc(x_rec, 1)
                dve.wait_ge(x_rec, w + 1)
                if free is not None:
                    dve.wait_ge(x_pv, free)
                dve.tensor_tensor(a[:, :, cols], xe[:, slot, :, :],
                                  xrec[:, slot, :].unsqueeze(1).broadcast_to([128, XH, 64]), ALU.mult).then_inc(x_norm, 1)
                dve.wait_ge(x_norm, w + 1)
                dve.tensor_tensor(lo[:, 0:8, cols], a[:, 0:8, cols], hi[:, 0:8, cols],
                                  ALU.subtract).then_inc(x_lo_d, 1)

            max_heads(0, 0, first=True)
            max_heads(1, 1, first=True)
            weights(0, 0, left, left_hi, left_lo, slice(0, 64))
            with dve.Fori(0, UL // 2 - 1) as it:
                for j in range(2):
                    w = 2 * it + 2 + j
                    max_heads(w, j)
                    weights(w - 1, 1 - j, left, left_hi, left_lo, bass.ds((w - 1) * 64, 64))
            max_heads(UL, 0)
            weights(UL - 1, 1, left, left_hi, left_lo, slice((UL - 1) * 64, UL * 64))

            def resid_3(b):
                dve.wait_ge(x_proj, b + 1)
                xTb = xT[:, bass.ds(b * T, T)]
                dve.scalar_tensor_tensor(xTb, ps[:, 4, :], xbias[:, 2:3], xTb, ALU.add, ALU.add).then_inc(resid2, 1)

            def norm_3(b):
                dve.wait_ge(act_ln3, 3 * b + 3)
                dve.tensor_tensor(xn3[:, bass.ds(b, 1), :].rearrange("p a t -> p (a t)"), ps[:, 4, :], ln_rs[:, :],
                                  ALU.mult).then_inc(normed3, 1)

            def main_batch(b, prev):
                for c in range(8):
                    w = 8 * b + UL + c
                    if c < 7 or not isinstance(b, int) or b < B - 1:
                        max_heads(w + 1, (c + 1) % 2)
                    q = c // 2 % 2
                    free = 4 * b + c // 2 - 1 if late(b, 1) or c >= 4 else None
                    weights(w, c % 2, xa[q], xa_hi[q], xa_lo[q], slice(64 * (c % 2), 64 * (c % 2) + 64), free)
                    if c == 3 and prev is not None:
                        resid_3(prev)
                    if c == 6 and prev is not None:
                        norm_3(prev)

            main_batch(0, None)
            with dve.Fori(1, B - 1) as b:
                main_batch(b, b - 1)
            main_batch(B - 1, B - 2)
            resid_3(B - 1)
            norm_3(B - 1)

            steps = [0]

            def g(ins, wait=True):
                ins.then_inc(g_step, 1)
                steps[0] += 1
                if wait:
                    dve.wait_ge(g_step, steps[0])

            def over(a):
                return a.unsqueeze(2).broadcast_to([128, TT, E])

            dve.wait_ge(scored, B)
            score = ps[:, 5, 0:TT * E].rearrange("p (t e) -> p t e", t=TT)
            g(dve.tensor_reduce(g1[:, :], score, AX_X, ALU.add))
            g(dve.scalar_tensor_tensor(gz, over(g1[:, :]), -1.0 / E, score, ALU.mult, ALU.add))
            g(dve.tensor_tensor(gq, gz, gz, ALU.mult))
            g(dve.tensor_reduce(g1[:, :], gq, AX_X, ALU.add))
            dve.wait_ge(g_act, 2)
            g(dve.scalar_tensor_tensor(gz, gz, 0.5, over(g1[:, :]), ALU.mult, ALU.mult))
            g(dve.tensor_reduce(g1[:, :], gz, AX_X, ALU.max))
            g(dve.tensor_tensor(gz, gz, over(g1[:, :]), ALU.subtract))
            for t in range(TT):
                g(dve.max(c_a[:, 0, t, 0:8], gz[:, t, :]), wait=t == TT - 1)
            for t in range(TT):
                g(dve.match_replace(gq[:, t, :], c_a[:, 0, t, 0:8], gz[:, t, :], -1e30), wait=t == TT - 1)
            for t in range(TT):
                g(dve.max(c_a[:, 0, t, 8:16], gq[:, t, :]), wait=t == TT - 1)
            g(dve.tensor_tensor(c_a[:, 1, :, :], c_a[:, 0, :, :], c_a[:, 0, :, :], ALU.mult), wait=False)
            g(dve.tensor_copy(gq, c_a[:, 0, :, :]))
            old, new = c_a, c_b
            for k in (1, 2, 4, 8):
                o = old[:, :, :, :].rearrange("p a t e -> p (a t) e")
                n = new[:, :, :, :].rearrange("p a t e -> p (a t) e")
                g(dve.tensor_copy(n[:, :, 0:k], o[:, :, 0:k]), wait=False)
                g(dve.tensor_tensor(n[:, :, k:E], o[:, :, k:E], o[:, :, 0:E - k], ALU.add))
                old, new = new, old
            ks = inv_k.unsqueeze(1).broadcast_to([128, TT, E])
            mean_k, meansq_k = c_b[:, 0, :, :], c_b[:, 1, :, :]
            g(dve.tensor_tensor(mean_k, c_a[:, 0, :, :], ks, ALU.mult), wait=False)
            g(dve.tensor_tensor(meansq_k, c_a[:, 1, :, :], ks, ALU.mult))
            g(dve.tensor_tensor(gs, mean_k, mean_k, ALU.mult))
            g(dve.tensor_tensor(gs, gs, meansq_k, ALU.subtract))
            g(dve.tensor_tensor(gs, gs, ks, ALU.add))
            g(dve.tensor_scalar(gs, gs, 0.0, None, ALU.max))
            assert steps[0] == GSQRT
            dve.wait_ge(g_act, 3)
            g(dve.tensor_tensor(gs, mean_k, gs, ALU.subtract))
            g(dve.tensor_tensor(gq, gs, gq, ALU.is_le))
            g(dve.tensor_scalar(gq, gq, 1e30, -1e30, ALU.mult, ALU.add))
            g(dve.tensor_tensor(gs, gs, gq, ALU.add))
            g(dve.tensor_reduce(g1[:, :], gs, AX_X, ALU.max))
            g(dve.tensor_tensor(gz, gz, over(g1[:, :]), ALU.subtract))
            g(dve.tensor_scalar(gz, gz, 0.0, None, ALU.max))
            dve.tensor_tensor(gq, gz, gz, ALU.mult).then_inc(a_done, 1)

            for b in range(B):
                dve.wait_ge(z1_done, b + 1)
                dve.wait_ge(g_out, b + 1)
                if b:
                    dve.wait_ge(h_done, 4 * b)
                dve.scalar_tensor_tensor(z1, ps[0:R, 1, :], bin_sb[0:R, :], gates[0:R, :],
                                         ALU.add, ALU.mult).then_inc(z1_out, 1)
                dve.wait_ge(z2_done, b + 1)
                if b:
                    dve.wait_ge(y_done, b)
                dve.scalar_tensor_tensor(z2[R:2 * R, :], ps[R:2 * R, 6, :], bin_sb[R:2 * R, :], gates[R:2 * R, :],
                                         ALU.add, ALU.mult).then_inc(z2_out, 1)
                dve.wait_ge(y_done, b + 1)
                dve.tensor_tensor(xT[:, b * T:(b + 1) * T], ps[:, 7, :], xT[:, b * T:(b + 1) * T], ALU.add).then_inc(stored, 1)

        @block.tensor
        def _(pe):
            def mm(o, lhsT, rhs, start, stop):
                return pe.matmul(o, lhsT, rhs, start=start, stop=stop, skip_group_check=True)

            pe.wait_ge(loaded_x, 16 * (B + 1))
            pe.wait_ge(loaded_w, 16 * W_LOADS)
            pe.wait_ge(loaded, 16 * OTHER_LOADS)
            for b in range(B):
                if b >= 1:
                    pe.wait_ge(dve_ln, 3 * b)
                mm(bank_p, centre, xT[:, b * T:(b + 1) * T], True, True).then_inc(pe_ln, 1)
                pe.wait_ge(act_ln, 3 * b + 1)
                mm(bank_s[0], mean, ln_sq[:, :], True, True).then_inc(pe_ln, 1)
            pe.wait_ge(dve_ln, 3 * B)
            pe.wait_ge(w_lo_done, 5)
            pe.wait_ge(setup, 4)

            mm(ps[:, 0, :], xw[:, 1, :], ctx_sb[:, 0:512], True, True)
            mm(ps[:, 1, 0:128], xw[:, 1, :], ctx_sb[:, 512:640], True, True).then_inc(ctx_k, 1)
            for t in range(XT):
                o = ps[:, 2 + t // 4, 128 * (t % 4):128 * (t % 4) + 128]
                mm(o, ctx_sb[:, t * 128:(t + 1) * 128], xw[:, 2, :], True, False)
                last = mm(o, ones_row[0:1, :], xbv_row[:, :], False, True)
            last.then_inc(ctx_v, 1)
            for p in range(PAIRS):
                last = mm(ps[:, 7, 0:1], wo_raw[:, p, :], biases[:, 2, p:p + 1], p == 0, p == PAIRS - 1)
            last.then_inc(bo_done, 1)
            pe.wait_ge(bo_added, 1)
            pe.wait_ge(key_parts, 2)
            pe.wait_ge(val_parts, B + 1)

            def project(n, j, done):
                cols = bass.ds(n % PAIRS * 128, 128)
                xb = bass.ds(n // PAIRS, 1)
                xh = xn_hi[:, xb, :].rearrange("p a t -> p (a t)")
                xl = xn_lo[:, xb, :].rearrange("p a t -> p (a t)")
                mm(bank_p, w_hi[:, j, cols], xh, True, False)
                mm(bank_p, w_lo[:, j, cols], xh, False, False)
                mm(bank_p, w_hi[:, j, cols], xl, False, True).then_inc(done, 1)

            def project_q(n):
                if absent(n):
                    return
                if late(n, 2):
                    pe.wait_ge(v_lo, n - 1)
                elif n == 1:
                    pe.wait_ge(k_lo, n)
                project(n, 0, q_proj)

            def project_k(n):
                if absent(n):
                    return
                pe.wait_ge(q_lo, n + 1)
                project(n, 1, k_proj)

            def project_v(n):
                if absent(n):
                    return
                if isinstance(n, int) and n == NP - 1:
                    pe.wait_ge(v_lo, n)
                else:
                    pe.wait_ge(k_lo, n + 2)
                cols = bass.ds(n % PAIRS * 128, 128)
                for t in range(KT):
                    toks = bass.ds(n // PAIRS * T + t * 128, 128)
                    xh = xn_hi[:, :, :].rearrange("p a t -> p (a t)")[:, toks]
                    xl = xn_lo[:, :, :].rearrange("p a t -> p (a t)")[:, toks]
                    o = bank_p[:, t * 128:(t + 1) * 128]
                    mm(o, xh, w_hi[:, 2, cols], True, False)
                    mm(o, xh, w_lo[:, 2, cols], False, False)
                    last = mm(o, xl, w_hi[:, 2, cols], False, True)
                last.then_inc(v_proj, 1)

            def scores_for_max(n, slot, c):
                if absent(n):
                    return
                h, q = c // KT, c % KT
                if c == 0:
                    pe.wait_ge(stacked, 16 * DMAS * (n + 1))
                    if late(n, 1):
                        pe.wait_ge(m_out, n)
                elif c >= 2 or late(n, 1):
                    pe.wait_ge(max_done, 8 * n + c - 1)
                mm(bank_s[c % 2], qa[:, slot, h, q * 128:(q + 1) * 128],
                   ka[:, slot, h, :], True, True).then_inc(s_done, 1)

            def turn_maxima(n, slot):
                if absent(n):
                    return
                pe.wait_ge(max_done, 8 * n + 8)
                for q in range(KT):
                    last = pe.transpose(bank_s[0][0:2, q * 128:(q + 1) * 128], m_q[:, slot, q, :], ident)
                last.then_inc(m_turned, 1)

            def scores(n, slot, h, half):
                if absent(n):
                    return
                if h == 0 and half == 0:
                    pe.wait_ge(m_placed, 16 * (n + 1))
                if h == 1 or late(n, 1):
                    pe.wait_ge(exp_done[half], 2 * n + h)
                for t in range(2):
                    cols = slice((2 * half + t) * 128, (2 * half + t + 1) * 128)
                    mm(st[half][:, t, :], ka[:, slot, h, cols], qa[:, slot, h, :], True, False)
                    last = mm(st[half][:, t, :], kb[0:DH + 1, slot, h, cols], qb[0:DH + 1, slot, h, :], False, True)
                last.then_inc(st_done[half], 1)

            def values(n, slot, h, part):
                if absent(n):
                    return
                if part == 0:
                    pe.wait_ge(lo_dve, 2 * n + h + 1)
                    pe.wait_ge(lo_pool, 4 * n + 2 * h + 2)
                    if h == 0:
                        pe.wait_ge(v_lo, n + 1)
                    if h == 1:
                        pe.wait_ge(o_done, 2 * n + 1)
                    elif late(n, 1):
                        pe.wait_ge(oT_done, n)
                for q in (2 * part, 2 * part + 1):
                    cols = slice(q * 128, (q + 1) * 128)
                    o = bank_o[:, q * (DH + 1):(q + 1) * (DH + 1)]
                    for k in range(KT):
                        mm(o, prob_hi[:, h, k, cols], v_hi_t[:, slot, k, h, :], k == 0, False)
                        mm(o[:, 0:DH], prob_hi[:, h, k, cols], v_lo_t[:, slot, k, h, :], False, False)
                        last = mm(o, prob_lo[:, h, k, cols], v_hi_t[:, slot, k, h, :], False, k == KT - 1)
                if part == 1:
                    last.then_inc(pv_done, 1)

            def turn_outputs(n):
                if absent(n):
                    return
                pe.wait_ge(o_done, 2 * n + 2)
                for q in range(KT):
                    last = pe.transpose(bank_o[:, q * 128:(q + 1) * 128],
                                        o_n[:, q, :, :].rearrange("p h d -> p (h d)"), ident)
                last.then_inc(oT_turned, 1)

            def step(i, s):
                scores(i, s, 0, 0)
                turn_outputs(i - 1)
                scores(i, s, 0, 1)
                project_v(i + 1)
                scores(i, s, 1, 0)
                scores(i, s, 1, 1)
                scores_for_max(i + 1, 1 - s, 4)
                project_q(i + 3)
                scores_for_max(i + 1, 1 - s, 5)
                scores_for_max(i + 1, 1 - s, 6)
                values(i, s, 0, 0)
                scores_for_max(i + 1, 1 - s, 7)
                values(i, s, 0, 1)
                turn_maxima(i + 1, 1 - s)
                project_k(i + 3)
                scores_for_max(i + 2, s, 0)
                scores_for_max(i + 2, s, 1)
                values(i, s, 1, 0)
                scores_for_max(i + 2, s, 2)
                values(i, s, 1, 1)
                scores_for_max(i + 2, s, 3)

            for i in range(-LEAD, LOOP_FROM):
                step(i, i % 2)
            with pe.Fori(LOOP_FROM // 2, LOOP_TO // 2) as it:
                step(2 * it + 1, 1)
                step(2 * it + 2, 0)
            for i in range(LOOP_TO, NP + LAG):
                step(i, i % 2)

            def out_proj(b):
                for p in range(PAIRS):
                    n = b * PAIRS + p
                    mm(ps[:, 0, :], wo_hi[:, p, :], oT_hi[:, n, :], p == 0, False)
                    mm(ps[:, 0, :], wo_lo[:, p, :], oT_hi[:, n, :], False, False)
                    last = mm(ps[:, 0, :], wo_hi[:, p, :], oT_lo[:, n, :], False, p == PAIRS - 1)
                last.then_inc(proj_o, 1)

            pe.wait_ge(oT_done, NP)
            pe.wait_ge(oT_kept, NP)
            out_proj(0)
            for b in range(B):
                pe.wait_ge(resid, b + 1)
                if b:
                    pe.wait_ge(normed, b)
                mm(ps[:, 1, :], centre, xT[:, b * T:(b + 1) * T], True, True).then_inc(pe_ln2, 1)
                if b + 1 < B:
                    out_proj(b + 1)
                pe.wait_ge(act_ln2, 3 * b + 1)
                mm(ps[:, 2, :], mean, ln_sq[:, :], True, True).then_inc(pe_ln2, 1)
                pe.wait_ge(normed, b + 1)
                if b:
                    pe.wait_ge(xq_parts, 2 * b)
                mm(ps[:, 3, :], xw[:, 0, :], ln_out[:, :], True, True).then_inc(xq_done, 1)
            pe.wait_ge(xq_parts, 2 * B)
            pe.wait_ge(masked, 2 * XH)

            def energies_left(w, slot, cols, first=False):
                if not first:
                    pe.wait_ge(x_exp, w - 1)
                for h in range(XH):
                    for b in range(B):
                        o = ps[SLP * b:SLP * b + SLP, 2 * slot + h // 8, 64 * (h % 8):64 * (h % 8) + 64]
                        ks = slice(B * 128 + SLP * b, B * 128 + SLP * b + SLP)
                        mm(o, keys_hi[:, h, ks], xq_hi[:, b, cols], h % 8 == 0, False)
                        mm(o, keys_lo[:, h, ks], xq_hi[:, b, cols], False, False)
                        last = mm(o, keys_hi[:, h, ks], xq_lo[:, b, cols], False, False)
                last.then_inc(e_done, 1)

            def energies(w, slot, b, cols):
                pe.wait_ge(x_exp, w - 1)
                keys = bass.ds(b * 128, 128)
                qh, ql = (a.rearrange("p b t -> p (b t)")[:, bass.ds(b * T + cols, 64)]
                          for a in (xq_hi[:, :, :], xq_lo[:, :, :]))
                for h in range(XH):
                    o = ps[:, 2 * slot + h // 8, 64 * (h % 8):64 * (h % 8) + 64]
                    mm(o, keys_hi[:, h, keys], qh, h % 8 == 0, False)
                    mm(o, keys_lo[:, h, keys], qh, False, False)
                    last = mm(o, keys_hi[:, h, keys], ql, False, False)
                last.then_inc(e_done, 1)

            def shift(w, slot):
                pe.wait_ge(x_max, w + 1)
                for half in range(2):
                    last = mm(ps[:, 2 * slot + half, :].rearrange("p (h q) -> p h q", q=64), minus_ident[:, :],
                              xm[:, slot, :].unsqueeze(1).broadcast_to([128, 8, 64]), False, True)
                last.then_inc(x_shift, 1)

            energies_left(0, 0, slice(0, 64), first=True)
            energies_left(1, 1, slice(64, 128), first=True)
            shift(0, 0)
            for w in range(2, UL):
                energies_left(w, w % 2, slice(64 * w, 64 * w + 64))
                shift(w - 1, (w - 1) % 2)
            energies(UL, 0, 0, 0)
            shift(UL - 1, 1)

            def weighted(b, q):
                n = 4 * b + q
                pe.wait_ge(x_lo_d, 2 * n + UL + 2)
                pe.wait_ge(x_lo_p, 2 * n + UL + 2)
                if n:
                    pe.wait_ge(x_out, n)
                s, cols = q % 2, slice(128 * q, 128 * q + 128)
                vals = [a[:, :, :].rearrange("p b n -> p (b n)") for a in (xv_hi, xv_lo, xvl_hi, xvl_lo)]
                for h in range(XH):
                    o = ps[:, 6, 128 * q + XD * h:128 * q + XD * h + XD]
                    v_h, v_l, l_h, l_l = (a[:, bass.ds(b * 128 + XD * h, XD)] for a in vals)
                    mm(o, xa_hi[s][:, h, :], v_h, h == 0, False)
                    mm(o, xa_hi[s][:, h, :], v_l, False, False)
                    mm(o, xa_lo[s][:, h, :], v_h, False, False)
                    mm(o, left_hi[:, h, cols], l_h, False, False)
                    mm(o, left_hi[:, h, cols], l_l, False, False)
                    last = mm(o, left_lo[:, h, cols], l_h, False, True)
                last.then_inc(x_pv, 1)

            def turn_tiles(b):
                pe.wait_ge(x_out, 4 * b + 4)
                if b:
                    pe.wait_ge(act_ln3, 3 * b - 1)
                for q in range(KT):
                    last = pe.transpose(ps[:, 7, 128 * q:128 * q + 128], xo[:, q, :], ident)
                last.then_inc(x_turned, 1)

            def out_proj_3(b):
                pe.wait_ge(x_T, b + 1)
                if b:
                    pe.wait_ge(normed3, b)
                mm(ps[:, 4, :], xw[:, 3, :], xoT[:, :], True, True).then_inc(x_proj, 1)

            def centre_3(b):
                pe.wait_ge(resid2, b + 1)
                mm(ps[:, 4, :], centre, xT[:, b * T:(b + 1) * T], True, True).then_inc(pe_ln3, 1)

            def variance_3(b):
                pe.wait_ge(act_ln3, 3 * b + 1)
                mm(ps[:, 7, :], mean, ln_sq[:, :], True, True).then_inc(pe_ln3, 1)

            def expert_scores(b):
                pe.wait_ge(normed3, b + 1)
                for t in range(KT):
                    last = mm(ps[:, 5, (b * KT + t) * E:(b * KT + t + 1) * E], xn3[:, b, t * 128:(t + 1) * 128],
                              proj_sb[:, :], True, True)
                last.then_inc(scored, 1)

            for u in range(UM):
                b, c = divmod(u, 8)
                if u + 1 < UM:
                    energies(UL + u + 1, (u + 1) % 2, (u + 1) // 8, 64 * ((u + 1) % 8))
                shift(UL + u, u % 2)
                if c == 1 and b:
                    weighted(b - 1, 3)
                if c == 2 and b:
                    turn_tiles(b - 1)
                if c == 3 and b:
                    out_proj_3(b - 1)
                if c == 4 and b:
                    centre_3(b - 1)
                if c == 5 and b:
                    variance_3(b - 1)
                if c in (3, 5, 7):
                    weighted(b, (c - 3) // 2)
                if c == 7 and b:
                    expert_scores(b - 1)
            weighted(B - 1, 3)
            turn_tiles(B - 1)
            out_proj_3(B - 1)
            centre_3(B - 1)
            variance_3(B - 1)
            expert_scores(B - 1)

            def gates_in(b):
                if b:
                    pe.wait_ge(z1_out, b)
                else:
                    pe.wait_ge(a_done, 1)
                for t in range(KT):
                    last = pe.transpose(ps[0:E, 1, t * 128:(t + 1) * 128], gq[:, KT * b + t, :], ident)
                last.then_inc(aT_turned, 1)
                pe.wait_ge(aT_out, b + 1)
                if b:
                    pe.wait_ge(g_out, b)
                mm(ps[:, 0, :], c12_sb[:, :], aT, True, True).then_inc(g_done, 1)
                mm(ps[0:R, 1, :], win1_sb[:, :], xn3[:, b, :], True, True).then_inc(z1_done, 1)

            gates_in(0)
            for b in range(B):
                pe.wait_ge(z1_out, b + 1)
                for m in range(4):
                    if b:
                        pe.wait_ge(h_out, 4 * (b - 1) + m + 1)
                    mm(ps[:, 2 + m, :], wout1_sb[:, m * 128:(m + 1) * 128], z1, True, True).then_inc(h_done, 1)
                if b + 1 < B:
                    gates_in(b + 1)
                for m in range(4):
                    pe.wait_ge(h_out, 4 * b + m + 1)
                    last = mm(ps[R:2 * R, 6, :], win2_sb[:, m, :], hid[:, m, :], m == 0, m == 3)
                last.then_inc(z2_done, 1)
                pe.wait_ge(z2_out, b + 1)
                if b:
                    pe.wait_ge(stored, b)
                mm(ps[:, 7, :], wout2_sb[R:2 * R, :], z2[R:2 * R, :], True, True).then_inc(y_done, 1)


def kernel(**inputs):
    import concourse.bacc as bacc
    from concourse.bass_utils import run_bass_kernel_spmd

    def t(a, *axes):
        return np.ascontiguousarray(np.transpose(np.asarray(a), axes))

    g = {k: np.asarray(v) for k, v in inputs.items()}
    eye = np.eye(128, dtype=np.float32)
    heads = np.repeat(np.eye(XH, dtype=np.float32), XD, axis=0)
    left = np.zeros((128, B), np.float32)
    for b in range(B):
        left[SLP * b:SLP * b + SL, b] = 1.0
    full = np.full((128, 128), 1.0 / 128, np.float32)
    consts = np.concatenate([eye - full, full, eye, np.ones((128, 256), np.float32), heads, left,
                             np.tile(1.0 / np.arange(1, E + 1, dtype=np.float32), (128, 1))], axis=1)
    ctxT = t(g["ctx_1024"], 2, 0, 1)

    def col(a):
        return np.ascontiguousarray(a.reshape(-1, 1))

    arrays = {
        "x": t(g["x"], 2, 0, 1).reshape(D, B * T),
        "ctx_main": np.ascontiguousarray(ctxT[:, :, 0:128]).reshape(D, B * 128),
        "ctx_left": np.ascontiguousarray(ctxT[:, :, 128:]),
        "wq": t(g["L0_attn_W_Q"], 2, 0, 1).reshape(D, H * DH),
        "wk": t(g["L0_attn_W_K"], 2, 0, 1).reshape(D, H * DH),
        "wv": t(g["L0_attn_W_V"], 2, 0, 1).reshape(D, H * DH),
        "wo": t(g["L0_attn_W_O"].reshape(PAIRS, 2, D, DH), 1, 3, 0, 2).reshape(128, PAIRS, D),
        "bias_qkv": t(np.stack([g["L0_attn_b_Q"], g["L0_attn_b_K"], g["L0_attn_b_V"]]).reshape(3, PAIRS, 128), 2, 0, 1),
        "b_o": col(g["L0_attn_b_O"]),
        "xwq": t(g["L0_xattn_Wq_w"], 1, 0), "xwk": t(g["L0_xattn_Wk_w"], 1, 0),
        "xwv": t(g["L0_xattn_Wv_w"], 1, 0), "xwo": t(g["L0_xattn_Wo_w"], 1, 0),
        "xb": t(np.stack([g["L0_xattn_Wq_b"], g["L0_xattn_Wk_b"], g["L0_xattn_Wo_b"]]), 1, 0),
        "xbv": g["L0_xattn_Wv_b"].reshape(1, 128),
        "proj": g["L0_ffn_proj"],
        "c12": np.concatenate([g["L0_ffn_C1"], g["L0_ffn_C2"]], axis=1),
        "win1": np.ascontiguousarray(g["L0_ffn_Win1"][0:D]), "bin1": col(g["L0_ffn_Win1"][D]),
        "wout1": t(g["L0_ffn_Wout1"], 1, 0),
        "win2": t(g["L0_ffn_Win2"][0:O].reshape(O // 128, 128, R), 1, 0, 2), "bin2": col(g["L0_ffn_Win2"][O]),
        "wout2": t(g["L0_ffn_Wout2"], 1, 0),
        "consts": consts,
    }
    nc = bacc.Bacc("TRN2", target_bir_lowering=False, num_devices=1)
    args = [nc.dram_tensor(f"in_{k}", a.shape, mybir.dt.from_np(a.dtype), kind="ExternalInput").ap()
            for k, a in arrays.items()]
    out = nc.dram_tensor("out_T", (D, B * T), F32, kind="ExternalOutput").ap()
    decoder(nc, **dict(zip(arrays, args)), out=out)
    r = run_bass_kernel_spmd(nc, [{f"in_{k}": a for k, a in arrays.items()}], core_ids=[0])
    return t(r.results[0]["out_T"].reshape(D, B, T), 1, 2, 0)
```

```python
from contextlib import ExitStack

import numpy as np

import concourse.bass as bass
from concourse import mybir

F32 = mybir.dt.float32
F16 = mybir.dt.float16
BF16 = mybir.dt.bfloat16
ALU = mybir.AluOpType
ACT = mybir.ActivationFunctionType
AX_X = mybir.AxisListType.X

B, T, D = 4, 512, 128
H, DH = 16, 64
PAIRS = H // 2
NP = B * PAIRS
KT = T // 128
S = 154
SL = S - 128
SLP = 32
XH, XD = 16, 8
XG = XH // 4
XR = 3 * 4 * XD
XT = B + 1
E, R, O = 16, 64, 512
ER = 3 * 32
TT = B * KT
EPS = 1e-5
MS = 64.0
DMAS = 4
LEAD, LAG, LOOP_FROM, LOOP_TO = 3, 1, 3, NP - 3


def late(n, first):
    return not isinstance(n, int) or n >= first


def absent(n):
    return isinstance(n, int) and not 0 <= n < NP


def decoder(nc, x, ctx_main, ctx_left, wq, wk, wv, wo, bias_qkv, b_o, xwq, xwk, xwv, xwo, xbqk, xbo, xbv,
            proj, c12, win1, wout1, win2, wout2, bins, consts, out):
    with ExitStack() as stack:
        def sb(name, shape, dt):
            return stack.enter_context(nc.sbuf_tensor(name, shape, dt))

        def sem(name):
            return stack.enter_context(nc.semaphore(name))

        cst = sb("cst", [128, 4 * 128 + 4 + B + 16], F32)
        centre, mean, ident = cst[:, 0:128], cst[:, 128:256], cst[:, 256:384]
        head_mask = cst[0:XR, 512:516]
        batch_mask = cst[:, 516:520]
        inv_k = cst[:, 520:536]
        minus_ident = sb("minus_ident", [128, 128], BF16)
        ones_row = cst[:, 384:512]
        xT = sb("xT", [128, B * T], F32)
        biases = sb("biases", [128, 3, PAIRS], F32)
        w_split = sb("w_split", [128, 2 * 3 * H * DH], F16)
        w_hi = w_split[:, 0:3 * H * DH].rearrange("p (a n) -> p a n", a=3)
        w_lo = w_split[:, 3 * H * DH:].rearrange("p (a n) -> p a n", a=3)
        xn3 = w_split[:, 0:2 * B * T].bitcast(F32).rearrange("p (b t) -> p b t", b=B)
        wo_hi = sb("wo_hi", [128, PAIRS, D], F16)
        wo_lo = sb("wo_lo", [128, PAIRS, D], F16)
        bo = sb("bo", [128, 1], F32)
        xw = sb("xw", [128, 2, 128], F32)
        xw_q = sb("xw_q", [128, XG, XR], F32)
        xw_k = sb("xw_k", [128, XG, XR], F32)
        xb_qk = sb("xb_qk", [XR, 2, XG], F32)
        xb_o = sb("xb_o", [128, 1], F32)
        xbv_row = sb("xbv_row", [1, 128], F32)
        proj_sb = sb("proj_sb", [128, E], F32)
        c_sb = sb("c_sb", [ER, 2, 2 * R], F32)
        c_split = sb("c_split", [ER, 2, 2 * R], F16)
        win1_sb = sb("win1_sb", [128, 2 * R], F32)
        wout1_sb = sb("wout1_sb", [2 * R, O], F32)
        wout1_hi = sb("wout1_hi", [2 * R, O], F16)
        wout1_lo = sb("wout1_lo", [R, O], F16)
        win2_sb = sb("win2_sb", [128, O // 128, 2 * R], F32)
        wout2_sb = sb("wout2_sb", [2 * R, D], F32)
        wout2_hi = sb("wout2_hi", [2 * R, D], F16)
        wout2_lo = sb("wout2_lo", [R, D], F16)
        bin_sb = sb("bin_sb", [2 * R, 2], F32)
        eps = sb("eps", [128, 1], F32)
        xn_hi = sb("xn_hi", [128, B, T], F16)
        xn_lo = sb("xn_lo", [128, B, T], F16)

        r1 = sb("r1", [128, 64 * 1024 // 4], F32)
        w_raw = r1[:, 0:3 * 1024].rearrange("p (a n) -> p a n", a=3)
        wo_raw = r1[:, 3 * 1024:4 * 1024].rearrange("p (a n) -> p a n", a=PAIRS)
        r1h = r1[:, :].bitcast(F16)
        oT_hi = r1h[:, 0:NP * T].rearrange("p (n t) -> p n t", n=NP)
        oT_lo = r1h[:, NP * T:2 * NP * T].rearrange("p (n t) -> p n t", n=NP)
        left = r1[:, 0:XH * T].rearrange("p (h t) -> p h t", h=XH)
        left_hi = left.bitcast(BF16).rearrange("p h (t two) -> p h t two", two=2)[:, :, :, 1]
        left_lo = r1h[:, 2 * XH * T:3 * XH * T].rearrange("p (h t) -> p h t", h=XH)

        xe_f32 = sb("xe", [128, 2 * XH * 64], F32)
        r2 = sb("r2", [128, 40 * 1024 // 4], F32)
        r2h = r2[:, :].bitcast(F16)

        def r2_f16(start, n):
            return r2h[:, start:start + n]
        prob = r2[:, 0:2 * KT * T].rearrange("p (h k t) -> p h k t", h=2, k=KT)
        prob_hi = prob.bitcast(BF16).rearrange("p h k (t two) -> p h k t two", two=2)[:, :, :, :, 1]
        base = 4 * KT * T
        prob_lo = r2_f16(base, 2 * KT * T).rearrange("p (h k t) -> p h k t", h=2, k=KT)
        base += 2 * KT * T
        stacks = r2_f16(base, 16 * T).rearrange("p (s h j t) -> p s h j t", s=2, h=2, j=4)
        qa, kb, qb, ka = (stacks[:, :, :, j, :] for j in range(4))
        keys = r2_f16(0, XH * XT * 128)[0:XR].rearrange("p (h k) -> p h k", h=XH)
        queries = r2_f16(XH * XT * 128, XG * B * T)[0:XR].rearrange("p (g t) -> p g t", g=XG)
        ln2_sq, ln2_rs = (xe_f32[:, n * 2 * T:(n + 1) * 2 * T].rearrange("p (b t) -> p b t", b=2) for n in range(2))
        ln2_lg = r2[:, 9216:9216 + 2 * T].rearrange("p (b t) -> p b t", b=2)
        ln1_sq, ln1_lg, ln1_rs = (r2[:, n * B * T:(n + 1) * B * T].rearrange("p (b t) -> p b t", b=B) for n in range(3))
        ln1_out = ln1_sq

        parts_0 = sb("parts", [128, 5 * T], F16)
        parts = [parts_0[:, :].rearrange("p (j t) -> p j t", j=5),
                 xe_f32[:, :].bitcast(F16)[:, 0:5 * T]]
        parts[1] = parts[1].rearrange("p (j t) -> p j t", j=5)
        v_hi_t = sb("v_hi", [128, 2, KT, 2, DH + 1], F16)
        v_lo_t = sb("v_lo", [128, 2, KT, 2, DH], F16)
        bias_now = sb("bias_now", [128, 2, 2], F32)
        m_q = sb("m_q", [128, 2, KT, 2], F32)
        m_row = sb("m_row", [2, T], F16)
        rsum = sb("rsum", [128, 2, KT], F32)
        o_hi = sb("o_hi", [128, T], F16)
        o_n = sb("o_n", [128, KT, 2, DH], F32)
        ln_sq = sb("ln_sq", [128, T], F32)
        ln_lg = sb("ln_lg", [128, T], F32)
        ln_rs = sb("ln_rs", [128, T], F32)
        ctx_sb = sb("ctx_sb", [128, XT * 128], F32)
        k_stack = sb("k_stack", [XR, XG, XT * 128], F16)
        xv_hi = sb("xv_hi", [128, B, 128], F16)
        xv_lo = sb("xv_lo", [128, B, 128], F16)
        xvl_hi = sb("xvl_hi", [128, B, 128], F16)
        xvl_lo = sb("xvl_lo", [128, B, 128], F16)
        xm = sb("xm", [128, 2, 64], BF16)
        xe = xe_f32[:, 0:2 * XH * 64].rearrange("p (s h q) -> p s h q", s=2, h=XH)
        xs8 = xn_hi[:, 0:2, :].rearrange("p b t -> p (b t)").bitcast(F32).rearrange("p (h q) -> p h q", h=8)
        xs4 = sb("xs4", [128, 4, 64], F32)
        xs2 = sb("xs2", [128, 2, 2, 64], F32)
        xsum = sb("xsum", [128, 64], F32)
        xrec = sb("xrec", [128, 2, 64], F32)
        xa0 = sb("xa0", [128, XH, 128], F32)
        xal0 = xn_lo[:, :, :].rearrange("p b t -> p (b t)").rearrange("p (h q) -> p h q", h=XH)
        free1 = XH * T + XH * T // 2
        xa1 = r1[:, free1:free1 + XH * 128].rearrange("p (h t) -> p h t", h=XH)
        free1 = 2 * (free1 + XH * 128)
        xal1 = r1h[:, free1:free1 + XH * 128].rearrange("p (h t) -> p h t", h=XH)
        xa, xa_lo = [xa0[:, :, :], xa1], [xal0, xal1]
        xa_hi = [a.bitcast(BF16).rearrange("p h (t two) -> p h t two", two=2)[:, :, :, 1] for a in xa]
        xo = sb("xo", [128, KT, 128], F32)
        xoT = sb("xoT", [128, T], F32)
        def r2_f32(start, n):
            return r2[:, start:start + n]
        hid = r2_f32(0, 2 * O // 128 * T).rearrange("p (s m t) -> p s m t", s=2, m=O // 128)
        gates_2 = r2_f32(4096, 2 * T).rearrange("p (s t) -> p s t", s=2)
        gates_1 = xe_f32[:, 0:T]
        z1, z2 = r2_f32(5120, T), r2_f32(5632, T)
        z1_split, z2_split, aT = (r2h[:, 2 * n:2 * n + T] for n in (6144, 6400, 6656))
        a_stack = r2_f32(6912, TT * ER).rearrange("p (t j e) -> p t j e", t=TT, j=3)
        c_a, c_b = (r2_f32(n, 512).rearrange("p (a t e) -> p a t e", a=2, t=TT) for n in (8448, 8960))
        gz, gs, gq = (r2_f32(n, 256).rearrange("p (t e) -> p t e", t=TT) for n in (9472, 9728, 9984))
        a_hi = sb("a_hi", [128, TT, E], F16)
        g1 = sb("g1", [128, TT], F32)

        ps = stack.enter_context(nc.psum_tensor("ps", [128, 8, 512], F32))
        st = [ps[:, 0:2, :], ps[:, 2:4, :]]
        bank_p, bank_s, bank_o = ps[:, 4, :], [ps[:, 5, :], ps[:, 6, :]], ps[:, 7, :]

        loaded = sem("loaded")
        loaded_x = sem("loaded_x")
        loaded_x0 = sem("loaded_x0")
        loaded_w = sem("loaded_w")
        stored = sem("stored")
        setup = sem("setup")
        w_hi_done = sem("w_hi_done")
        w_lo_done = sem("w_lo_done")
        w_pool = sem("w_pool")
        pe_ln = sem("pe_ln")
        act_ln = sem("act_ln")
        dve_ln = sem("dve_ln")
        xn_done = sem("xn_done")
        bias_done = sem("bias_done")
        q_proj, k_proj, v_proj = sem("q_proj"), sem("k_proj"), sem("v_proj")
        k_hi2 = sem("k_hi2")
        q_hi, k_hi, v_hi = sem("q_hi_done"), sem("k_hi_done"), sem("v_hi_done")
        q_lo, k_lo, v_lo = sem("q_lo_done"), sem("k_lo_done"), sem("v_lo_done")
        stacked, m_placed = sem("stacked"), sem("m_placed")
        s_done, max_done = sem("s_done"), sem("max_done")
        m_turned, m_out = sem("m_turned"), sem("m_out")
        st_done = [sem("st_done_0"), sem("st_done_1")]
        exp_done = [sem("exp_done_0"), sem("exp_done_1")]
        lo_dve, lo_pool = sem("lo_dve"), sem("lo_pool")
        pv_done, r_done, o_done = sem("pv_done"), sem("r_done"), sem("o_done")
        oT_turned, oT_hi_done, oT_done = sem("oT_turned"), sem("oT_hi_done"), sem("oT_done")
        oT_kept = sem("oT_kept")
        bo_done, bo_added = sem("bo_done"), sem("bo_added")
        ctx_k, ctx_v, key_parts, val_parts = (sem(n) for n in (
            "ctx_k", "ctx_v", "key_parts", "val_parts"))
        key_hi_done, val_hi_done, masked = (sem(n) for n in ("key_hi_done", "val_hi_done", "masked"))
        proj_o, resid, pe_ln2, act_ln2, normed, xq_done, xq_parts = (sem(n) for n in (
            "proj_o", "resid", "pe_ln2", "act_ln2", "normed", "xq_done", "xq_parts"))
        xq_high, xq_high_dve = sem("xq_high"), sem("xq_high_dve")
        e_done, x_max, x_shift, x_exp, x_tree, x_sum, x_rec, x_norm, x_lo_d, x_lo_p = (sem(n) for n in (
            "e_done", "x_max", "x_shift", "x_exp", "x_tree", "x_sum", "x_rec", "x_norm", "x_lo_d", "x_lo_p"))
        x_add = sem("x_add")
        x_pv, x_out, x_turned, x_T, x_proj, resid2, pe_ln3, act_ln3, normed3, scored = (sem(n) for n in (
            "x_pv", "x_out", "x_turned", "x_T", "x_proj", "resid2", "pe_ln3", "act_ln3", "normed3", "scored"))
        g1_out = sem("g1_out")
        w_mix, z1_hi, z2_hi, z1_lo, z2_lo = (sem(n) for n in ("w_mix", "z1_hi", "z2_hi", "z1_lo", "z2_lo"))
        g_step, g_act, a_done, aT_turned, aT_out, g_done, g_out = (sem(n) for n in (
            "g_step", "g_act", "a_done", "aT_turned", "aT_out", "g_done", "g_out"))
        z1_done, z1_out, h_done, h_out, z2_done, z2_out, y_done = (sem(n) for n in (
            "z1_done", "z1_out", "h_done", "h_out", "z2_done", "z2_out", "y_done"))

        W_LOADS = 4
        X_LOADS = 3
        OTHER_LOADS = 18
        G_TILES = ((0, TT - KT), (TT - KT, TT))
        G_BEFORE = (0, 32 + 3 * (TT - KT))
        G_SQRT = tuple(n + 23 + 3 * (t1 - t0) for n, (t0, t1) in zip(G_BEFORE, G_TILES))
        XQ_ACT = (0, 1, 2) + tuple(range(XG * B // 2, XG * B))
        XQ_DVE = tuple(j for j in range(XG * B) if j not in XQ_ACT)
        OUT_BANK = (0, 1, 6, 0)
        UL, UM = T // 64, B * T // 64

        block = stack.enter_context(nc.Block())

        @block.sync
        def _(sp):
            for b in range(B):
                sp.dma_start(xT[:, b * T:(b + 1) * T], x[:, b * T:(b + 1) * T]).then_inc(loaded_x if b else loaded_x0, 16)
                if b == 0:
                    sp.dma_start(cst[:, :], consts).then_inc(loaded_x0, 16)
            for j, w in enumerate((wq, wk, wv)):
                sp.dma_start(w_raw[:, j, :], w).then_inc(loaded_w, 16)
            sp.dma_start(wo_raw, wo).then_inc(loaded_w, 16)
            sp.dma_start(biases[:, :, :], bias_qkv).then_inc(loaded, 16)
            sp.dma_start(bo[:, :], b_o).then_inc(loaded, 16)
            sp.dma_start(xw_q[:, :, :], xwq).then_inc(loaded, 16)
            sp.dma_start(xw_k[:, :, :], xwk).then_inc(loaded, 16)
            for j, w in enumerate((xwv, xwo)):
                sp.dma_start(xw[:, j, :], w).then_inc(loaded, 16)
            sp.dma_start(xb_qk[:, :, :], xbqk).then_inc(loaded, 16)
            sp.dma_start(xb_o[:, :], xbo).then_inc(loaded, 16)
            sp.dma_start(xbv_row[:, :], xbv).then_inc(loaded, 16)
            sp.dma_start(proj_sb[:, :], proj).then_inc(loaded, 16)
            sp.dma_start(c_sb[:, :, :], c12).then_inc(loaded, 16)
            sp.dma_start(win1_sb[:, :], win1).then_inc(loaded, 16)
            sp.dma_start(wout1_sb[:, :], wout1).then_inc(loaded, 16)
            sp.dma_start(win2_sb[:, :, :], win2).then_inc(loaded, 16)
            sp.dma_start(wout2_sb[:, :], wout2).then_inc(loaded, 16)
            sp.dma_start(bin_sb[:, :], bins).then_inc(loaded, 16)
            sp.dma_start(ctx_sb[:, 0:B * 128], ctx_main).then_inc(loaded, 16)
            sp.wait_ge(setup, 1)
            sp.dma_start(ctx_sb[:, B * 128:].rearrange("p (b k) -> p b k", b=B)[:, :, 0:SL],
                         ctx_left).then_inc(loaded, 16)

            def reg(n):
                return n if isinstance(n, int) else sp.to_reg(n)

            def stack_pair(n, slot):
                if absent(n):
                    return
                pairs, used, placed = reg(n + 1), reg(2 * n - 2), reg(16 * DMAS * n)
                if late(n, 2):
                    sp.wait_ge(st_done[0], used)
                    sp.wait_ge(st_done[1], used)
                if late(n, 1):
                    sp.wait_ge(stacked, placed)
                sp.wait_ge(q_hi, pairs)
                sp.wait_ge(k_hi, pairs)
                sp.wait_ge(q_lo, pairs)
                sp.wait_ge(k_lo, pairs)
                sp.wait_ge(k_hi2, pairs)
                for h in range(2):
                    rows = slice(DH * h, DH * h + DH)
                    sp.dma_start(stacks[0:DH, slot, h, :, :], parts[slot][rows, 0:4, :]).then_inc(stacked, 16)
                    sp.dma_start(stacks[DH:128, slot, h, 0:4:3, :], parts[slot][rows, 0:5:4, :]).then_inc(stacked, 16)

            def place_maxima(n, slot):
                sp.wait_ge(m_out, reg(n + 1))
                sp.dma_start(qb[DH:DH + 1, slot, :, :], m_row[:, :]).then_inc(m_placed, 16)

            stack_pair(0, 0)
            stack_pair(1, 1)
            place_maxima(0, 0)
            stack_pair(2, 0)
            place_maxima(1, 1)
            with sp.Fori(0, (NP - 4) // 2) as it:
                stack_pair(2 * it + 3, 1)
                place_maxima(2 * it + 2, 0)
                stack_pair(2 * it + 4, 0)
                place_maxima(2 * it + 3, 1)
            stack_pair(NP - 1, 1)
            place_maxima(NP - 2, 0)
            place_maxima(NP - 1, 1)
            for b in range(B):
                sp.wait_ge(stored, b + 1)
                sp.dma_start(out[:, b * T:(b + 1) * T], xT[:, b * T:(b + 1) * T]).then_inc(m_placed, 16)
            sp.wait_ge(m_placed, 16 * (NP + B))

        @block.gpsimd
        def _(pool):
            pool.memset(ctx_sb[:, B * 128:], 0.0).then_inc(setup, 1)
            pool.wait_ge(setup, 1)
            pool.memset(kb[DH:DH + 1, :, :, :], MS).then_inc(setup, 1)
            pool.wait_ge(setup, 2)
            pool.memset(v_hi_t[:, :, :, :, DH:DH + 1], 1.0).then_inc(setup, 1)
            pool.wait_ge(setup, 3)
            pool.memset(eps[:, :], EPS).then_inc(setup, 1)

            pool.wait_ge(loaded_w, 16 * W_LOADS)
            pool.wait_ge(setup, 4)
            pool.tensor_copy(w_hi[:, 2, :], w_raw[:, 2, :]).then_inc(w_pool, 1)
            pool.wait_ge(w_pool, 1)
            pool.tensor_tensor(w_lo[:, 2, :], w_raw[:, 2, :], w_hi[:, 2, :], ALU.subtract).then_inc(w_pool, 1)
            pool.wait_ge(w_pool, 2)
            pool.tensor_copy(wo_hi[:, :, :], wo_raw).then_inc(w_pool, 1)
            pool.wait_ge(w_pool, 3)
            pool.tensor_tensor(wo_lo[:, :, :], wo_raw, wo_hi[:, :, :], ALU.subtract).then_inc(w_pool, 1)

            def low_parts(g, h):
                for half, tiles in enumerate((slice(1, 2), slice(2, 4))):
                    pool.wait_ge(exp_done[half], g + 1)
                    pool.tensor_tensor(prob_lo[:, h, tiles, :], prob[:, h, tiles, :], prob_hi[:, h, tiles, :],
                                       ALU.subtract).then_inc(lo_pool, 1)

            with pool.Fori(0, NP) as i:
                low_parts(2 * i, 0)
                low_parts(2 * i + 1, 1)

            pool.wait_ge(loaded, 16 * OTHER_LOADS)
            pool.tensor_copy(c_split[:, :, :], c_sb[:, :, :]).then_inc(w_mix, 1)
            pool.tensor_copy(wout1_hi[:, :], wout1_sb[:, :]).then_inc(w_mix, 1)
            pool.tensor_copy(wout2_hi[:, :], wout2_sb[:, :]).then_inc(w_mix, 1)
            pool.wait_ge(w_mix, 3)
            pool.tensor_tensor(c_split[32:64, :, :], c_sb[32:64, :, :], c_split[32:64, :, :], ALU.subtract).then_inc(w_mix, 1)
            pool.wait_ge(w_mix, 4)
            pool.tensor_tensor(wout1_lo[:, :], wout1_sb[0:R, :], wout1_hi[0:R, :], ALU.subtract).then_inc(w_mix, 1)
            pool.wait_ge(w_mix, 5)
            pool.tensor_tensor(wout2_lo[:, :], wout2_sb[0:R, :], wout2_hi[0:R, :], ALU.subtract).then_inc(w_mix, 1)

            def sum_heads(w, slot, first=False):
                pool.wait_ge(x_exp, w + 1)
                e = xe[:, slot, :, :]
                pool.tensor_tensor(xs8[:, :, :], e[:, 0:8, :], e[:, 8:16, :], ALU.add).then_inc(x_tree, 1)
                pool.wait_ge(x_tree, 2 * w + 1)
                pool.tensor_tensor(xs4[:, :, :], xs8[:, 0:4, :], xs8[:, 4:8, :], ALU.add).then_inc(x_tree, 1)
                pool.wait_ge(x_tree, 2 * w + 2)
                if not first:
                    pool.wait_ge(x_add, w - 1)
                pool.tensor_tensor(xs2[:, slot, :, :], xs4[:, 0:2, :], xs4[:, 2:4, :], ALU.add).then_inc(x_sum, 1)

            def weights_low(w, a, hi, lo, cols):
                pool.wait_ge(x_norm, w + 1)
                pool.tensor_tensor(lo[:, 8:16, cols], a[:, 8:16, cols], hi[:, 8:16, cols],
                                   ALU.subtract).then_inc(x_lo_p, 1)

            for u in range(2):
                sum_heads(u, u, first=True)
                if u:
                    weights_low(0, left, left_hi, left_lo, slice(0, 64))
            with pool.Fori(0, UL // 2 - 1) as it:
                for j in range(2):
                    w = 2 * it + 2 + j
                    sum_heads(w, j)
                    weights_low(w - 1, left, left_hi, left_lo, bass.ds((w - 1) * 64, 64))

            def main_low(w, c):
                q, cols = c // 2 % 2, slice(64 * (c % 2), 64 * (c % 2) + 64)
                weights_low(w, xa[q], xa_hi[q], xa_lo[q], cols)

            sum_heads(UL, 0)
            weights_low(UL - 1, left, left_hi, left_lo, slice((UL - 1) * 64, UL * 64))
            for c in range(1, 8):
                sum_heads(UL + c, c % 2)
                main_low(UL + c - 1, c - 1)
            with pool.Fori(1, B) as b:
                for c in range(8):
                    w = 8 * b + UL + c
                    sum_heads(w, c % 2)
                    main_low(w - 1, (c - 1) % 8)
            main_low(UL + UM - 1, 7)
            pool.wait_ge(e_done, UL + UM)
            pool.memset(a_stack, 0.0).then_inc(w_mix, 1)

        @block.scalar
        def _(act):
            def squares_3(b):
                act.wait_ge(pe_ln3, 2 * b + 1)
                act.activation(ln_sq[:, :], ps[:, 4, :], ACT.Square).then_inc(act_ln3, 1)

            def logs_3(n):
                act.wait_ge(pe_ln3, 2 * n + 2)
                act.activation(ln_lg[:, :], ps[:, 7, :], ACT.Ln, bias=eps[:, :]).then_inc(act_ln3, 1)

            def scale_3(n):
                act.wait_ge(act_ln3, 3 * n + 2)
                act.activation(ln_rs[:, :], ln_lg[:, :], ACT.Exp, scale=-0.5).then_inc(act_ln3, 1)

            def weight_high(j):
                act.activation(w_hi[:, j, :], w_raw[:, j, :], ACT.Copy).then_inc(w_hi_done, 1)

            for b in range(B):
                act.wait_ge(pe_ln, b + 1)
                act.activation(ln1_sq[:, b, :], ps[:, b, :], ACT.Square).then_inc(act_ln, 1)
            act.wait_ge(loaded_w, 16 * W_LOADS)
            weight_high(0)
            weight_high(1)
            act.wait_ge(setup, 4)
            act.wait_ge(pe_ln, 2 * B)
            act.activation(ln1_lg, ps[:, 4:8, :], ACT.Ln, bias=eps[:, :]).then_inc(act_ln, 1)
            act.wait_ge(act_ln, B + 1)
            for b in range(B):
                act.activation(ln1_rs[:, b, :], ln1_lg[:, b, :], ACT.Exp, scale=-0.5).then_inc(act_ln, 1)

            act.wait_ge(loaded, 16 * OTHER_LOADS)
            for g in range(XG):
                act.wait_ge(ctx_k, g + 1)
                act.activation(k_stack[:, g, 0:512], ps[0:XR, 4 + g, :], ACT.Identity,
                               bias=xb_qk[:, 1, g:g + 1]).then_inc(key_hi_done, 1)
            act.wait_ge(ctx_k, XG + 1)
            for g in range(XG):
                act.activation(k_stack[:, g, 512:640], ps[0:XR, 0, 128 * g:128 * g + 128], ACT.Identity,
                               bias=xb_qk[:, 1, g:g + 1]).then_inc(key_hi_done, 1)
            act.wait_ge(ctx_v, 1)
            act.activation(xv_hi[:, :, :].rearrange("p b n -> p (b n)"), ps[:, 1, :], ACT.Copy).then_inc(val_hi_done, 1)
            for b in range(B):
                act.activation(xvl_hi[:, b, :], ps[:, 2, 0:128], ACT.Copy, scale=batch_mask[:, b:b + 1]).then_inc(val_hi_done, 1)

            def q_high(n, slot):
                if absent(n):
                    return
                act.wait_ge(q_proj, n + 1)
                act.wait_ge(bias_done, n + 1)
                if late(n, 2):
                    act.wait_ge(stacked, 16 * DMAS * (n - 1))
                act.activation(parts[slot][:, 0, :], bank_p, ACT.Identity, bias=bias_now[:, slot, 0:1]).then_inc(q_hi, 1)

            def k_high(n, slot):
                if absent(n):
                    return
                act.wait_ge(k_proj, n + 1)
                act.activation(parts[slot][:, 1, :], bank_p, ACT.Identity, bias=bias_now[:, slot, 1:2]).then_inc(k_hi, 1)

            def v_high(n, slot):
                if absent(n):
                    return
                act.wait_ge(v_proj, n + 1)
                if late(n, 2):
                    act.wait_ge(pv_done, 2 * n - 2)
                act.activation(v_hi_t[:, slot, :, :, 0:DH],
                               bank_p.rearrange("p (k h d) -> p k h d", k=KT, h=2), ACT.Copy).then_inc(v_hi, 1)

            def exp_half(n, h, half):
                if absent(n):
                    return
                act.wait_ge(st_done[half], 2 * n + h + 1)
                if late(n, 1):
                    act.wait_ge(pv_done, 2 * n - 1 + h)
                act.activation(prob[:, h, 2 * half:2 * half + 2, :], st[half], ACT.Exp,
                               scale=DH ** -0.5).then_inc(exp_done[half], 1)

            def m_rows(n):
                if absent(n):
                    return
                act.wait_ge(m_turned, n + 1)
                if late(n, 1):
                    act.wait_ge(m_placed, 16 * n)
                act.activation(m_row[:, :], bank_s[0][0:2, :], ACT.Copy, scale=-1.0 / MS).then_inc(m_out, 1)

            def out_high(n):
                if absent(n):
                    return
                act.wait_ge(oT_turned, n + 1)
                if late(n, 1):
                    act.wait_ge(oT_done, n)
                    act.wait_ge(oT_kept, n)
                act.activation(o_hi[:, :], bank_o, ACT.Copy).then_inc(oT_hi_done, 1)

            def step(i, s):
                exp_half(i, 0, 0)
                exp_half(i, 0, 1)
                v_high(i + 1, 1 - s)
                out_high(i - 1)
                exp_half(i, 1, 0)
                exp_half(i, 1, 1)
                q_high(i + 3, 1 - s)
                m_rows(i + 1)
                k_high(i + 3, 1 - s)

            for i in range(-LEAD, LOOP_FROM):
                step(i, i % 2)
            with act.Fori(LOOP_FROM // 2, LOOP_TO // 2) as it:
                step(2 * it + 1, 1)
                step(2 * it + 2, 0)
            for i in range(LOOP_TO, NP + LAG):
                step(i, i % 2)

            def squares_2(b):
                act.wait_ge(pe_ln2, 4 * (b // 2) + b % 2 + 1)
                act.activation(ln2_sq[:, b % 2, :], ps[:, 2 + b % 2, :], ACT.Square).then_inc(act_ln2, 1)

            def norm_2(half):
                act.wait_ge(pe_ln2, 4 * half + 4)
                variance = ps[:, 0:2, :] if half else ps[:, 4:6, :]
                act.activation(ln2_lg, variance, ACT.Ln, bias=eps[:, :]).then_inc(act_ln2, 1)
                act.wait_ge(act_ln2, 4 * half + 3)
                if half:
                    act.wait_ge(normed, 2)
                act.activation(ln2_rs, ln2_lg, ACT.Exp, scale=-0.5).then_inc(act_ln2, 1)

            def query_high(j):
                b, g = divmod(j, XG)
                act.wait_ge(xq_done, j + 1)
                act.activation(queries[:, g, b * T:(b + 1) * T], ps[0:XR, 5 + j % 3, :], ACT.Identity,
                               bias=xb_qk[:, 0, g:g + 1]).then_inc(xq_high, 1)

            squares_2(0)
            squares_2(1)
            norm_2(0)
            squares_2(2)
            squares_2(3)
            for j in XQ_ACT[0:3]:
                query_high(j)
            norm_2(1)
            for j in XQ_ACT[3:]:
                query_high(j)

            def exp_unit(w, slot, first=False):
                act.wait_ge(x_shift, w + 1)
                if not first:
                    act.wait_ge(x_norm, w - 1)
                act.activation(xe[:, slot, :, :], ps[:, 2 * slot:2 * slot + 2, :].rearrange(
                    "p a (h q) -> p (a h) q", q=64), ACT.Exp, scale=XD ** -0.5).then_inc(x_exp, 1)

            for w in range(2):
                exp_unit(w, w, first=True)
            with act.Fori(0, UL // 2 - 1) as it:
                for j in range(2):
                    exp_unit(2 * it + 2 + j, j)

            def out_tile(b, q):
                act.wait_ge(x_pv, 4 * b + q + 1)
                act.activation(xo[:, q, :], ps[:, 6, 128 * q:128 * q + 128], ACT.Copy).then_inc(x_out, 1)

            def turned_out(b):
                act.wait_ge(x_turned, b + 1)
                if late(b, 1):
                    act.wait_ge(x_proj, b)
                act.activation(xoT[:, :], ps[:, 7, :], ACT.Copy).then_inc(x_T, 1)

            def main_batch(b, prev, prev2):
                for c in range(8):
                    exp_unit(8 * b + UL + c, c % 2)
                    if c == 0 and prev2 is not None:
                        scale_3(prev2)
                    if prev is not None:
                        if c == 0:
                            out_tile(prev, 2)
                        if c == 2:
                            out_tile(prev, 3)
                        if c == 4:
                            turned_out(prev)
                        if c == 6:
                            squares_3(prev)
                        if c == 7:
                            logs_3(prev)
                    if c in (4, 6):
                        if c == 4 and prev is not None:
                            act.wait_ge(x_turned, b)
                        out_tile(b, c // 2 - 2)

            main_batch(0, None, None)
            main_batch(1, 0, None)
            with act.Fori(2, B) as b:
                main_batch(b, b - 1, b - 2)
            scale_3(B - 2)
            def gate_scale(part):
                t = slice(*G_TILES[part])
                act.wait_ge(g_step, G_BEFORE[part] + 4)
                act.activation(g1[:, t], g1[:, t], ACT.Ln, bias=eps[:, :], scale=1.0 / E).then_inc(g_act, 1)
                act.wait_ge(g_act, 3 * part + 1)
                act.activation(g1[:, t], g1[:, t], ACT.Exp, scale=-0.5).then_inc(g_act, 1)

            def gate_root(part):
                t = slice(*G_TILES[part])
                act.wait_ge(g_step, G_SQRT[part])
                act.activation(gs[:, t, :], gs[:, t, :], ACT.Sqrt).then_inc(g_act, 1)

            out_tile(B - 1, 2)
            gate_scale(0)
            out_tile(B - 1, 3)
            turned_out(B - 1)
            squares_3(B - 1)
            logs_3(B - 1)
            scale_3(B - 1)

            gate_root(0)

            def gates_turned(b):
                act.wait_ge(aT_turned, b + 1)
                if b:
                    act.wait_ge(g_done, 2 * b)
                act.activation(aT[0:ER, :], ps[0:ER, 0, :], ACT.Copy).then_inc(aT_out, 1)

            def gates_1_out(b):
                act.wait_ge(g_done, 2 * b + 1)
                if b:
                    act.wait_ge(z1_out, b)
                act.activation(gates_1, ps[:, 1, :], ACT.Copy).then_inc(g1_out, 1)

            def gates_out(b):
                act.wait_ge(g_done, 2 * b + 2)
                if b >= 2:
                    act.wait_ge(z2_out, b - 1)
                act.activation(gates_2[:, b % 2, :], ps[:, 2, :], ACT.Copy).then_inc(g_out, 1)

            def hidden(b):
                for m in range(4):
                    act.wait_ge(h_done, 4 * b + m + 1)
                    if b >= 2:
                        act.wait_ge(z2_done, b - 1)
                    act.activation(hid[:, b % 2, m, :], ps[:, 3 + (4 * b + m) % 3, :], ACT.Gelu).then_inc(h_out, 1)

            def high(b, z, split, ready, used, done):
                act.wait_ge(ready, b + 1)
                if b:
                    act.wait_ge(*used)
                act.activation(split, z, ACT.Copy).then_inc(done, 1)

            gates_turned(0)
            gate_scale(1)
            gates_1_out(0)
            gates_out(0)
            for b in range(B + 1):
                if b < B:
                    high(b, z1, z1_split, z1_out, (h_done, 4 * b), z1_hi)
                    if b:
                        gates_out(b)
                    if b == 1:
                        gate_root(1)
                if b + 1 < B:
                    gates_turned(b + 1)
                if b >= 2:
                    high(b - 2, z2, z2_split, z2_out, (y_done, b - 2), z2_hi)
                if b < B:
                    hidden(b)
                if b + 1 < B:
                    gates_1_out(b + 1)
            high(B - 1, z2, z2_split, z2_out, (y_done, B - 1), z2_hi)

        @block.vector
        def _(dve):
            dve.wait_ge(loaded_x0, 16 * 2)
            dve.tensor_scalar(minus_ident[:, :], ident, -1.0, None, ALU.mult).then_inc(w_lo_done, 1)

            def weight_low(j):
                dve.wait_ge(w_hi_done, j + 1)
                dve.tensor_tensor(w_lo[:, j, :], w_raw[:, j, :], w_hi[:, j, :], ALU.subtract).then_inc(w_lo_done, 1)

            weight_low(0)
            weight_low(1)
            for b in range(B):
                dve.wait_ge(act_ln, B + 2 + b)
                dve.tensor_tensor(ln1_out[:, b, :], ps[:, b, :], ln1_rs[:, b, :], ALU.mult).then_inc(dve_ln, 1)
            for b in range(B):
                dve.wait_ge(dve_ln, b + 1)
                dve.tensor_copy(xn_hi[:, b, :], ln1_out[:, b, :]).then_inc(xn_done, 1)
                dve.wait_ge(xn_done, 2 * b + 1)
                dve.tensor_tensor(xn_lo[:, b, :], ln1_out[:, b, :], xn_hi[:, b, :], ALU.subtract).then_inc(xn_done, 1)

            dve.wait_ge(loaded, 16 * OTHER_LOADS)
            low = slice(4 * XD, 8 * XD)
            dve.wait_ge(key_hi_done, 2 * XG)
            for g in range(XG):
                dve.scalar_tensor_tensor(k_stack[low, g, 0:512], ps[low, 4 + g, :], xb_qk[low, 1, g:g + 1],
                                         k_stack[low, g, 0:512], ALU.add, ALU.subtract).then_inc(key_parts, 1)
                dve.scalar_tensor_tensor(k_stack[low, g, 512:640], ps[low, 0, 128 * g:128 * g + 128],
                                         xb_qk[low, 1, g:g + 1], k_stack[low, g, 512:640],
                                         ALU.add, ALU.subtract).then_inc(key_parts, 1)
            dve.wait_ge(val_hi_done, B + 1)
            dve.tensor_tensor(xv_lo[:, :, :].rearrange("p b n -> p (b n)"), ps[:, 1, :],
                              xv_hi[:, :, :].rearrange("p b n -> p (b n)"), ALU.subtract).then_inc(val_parts, 1)
            for b in range(B):
                dve.scalar_tensor_tensor(xvl_lo[:, b, :], ps[:, 2, 0:128], batch_mask[:, b:b + 1], xvl_hi[:, b, :],
                                         ALU.mult, ALU.subtract).then_inc(val_parts, 1)

            dve.wait_ge(bo_done, 1)
            dve.tensor_tensor(bo[:, :], ps[:, 3, 0:1], bo[:, :], ALU.add).then_inc(bo_added, 1)

            def bias_copy(n, slot):
                if absent(n):
                    return
                if late(n, 2):
                    dve.wait_ge(k_lo, n - 1)
                dve.tensor_copy(bias_now[:, slot, :], biases[:, 0:2, bass.ds(n % PAIRS, 1)].rearrange("p a b -> p (a b)")).then_inc(bias_done, 1)

            def q_low(n, slot):
                if absent(n):
                    return
                dve.wait_ge(bias_done, n + 1)
                dve.wait_ge(q_hi, n + 1)
                if late(n, 2):
                    dve.wait_ge(stacked, 16 * DMAS * (n - 1))
                dve.scalar_tensor_tensor(parts[slot][:, 2, :], bank_p, bias_now[:, slot, 0:1], parts[slot][:, 0, :],
                                         ALU.add, ALU.subtract).then_inc(q_lo, 1)

            def k_low(n, slot):
                if absent(n):
                    return
                dve.wait_ge(k_hi, n + 1)
                dve.scalar_tensor_tensor(parts[slot][:, 4, :], bank_p, bias_now[:, slot, 1:2], parts[slot][:, 1, :],
                                         ALU.add, ALU.subtract).then_inc(k_lo, 1)

            def k_again(n, slot):
                if absent(n):
                    return
                dve.wait_ge(k_hi, n + 1)
                dve.tensor_copy(parts[slot][:, 3, :], parts[slot][:, 1, :]).then_inc(k_hi2, 1)

            def v_low(n, slot):
                if absent(n):
                    return
                dve.wait_ge(v_hi, n + 1)
                dve.tensor_tensor(v_lo_t[:, slot, :, :, :], bank_p.rearrange("p (k h d) -> p k h d", k=KT, h=2),
                                  v_hi_t[:, slot, :, :, 0:DH], ALU.subtract).then_inc(v_lo, 1)

            def low_parts(n, h):
                if absent(n):
                    return
                dve.wait_ge(exp_done[0], 2 * n + h + 1)
                dve.tensor_tensor(prob_lo[:, h, 0, :], prob[:, h, 0, :], prob_hi[:, h, 0, :],
                                  ALU.subtract).then_inc(lo_dve, 1)

            o_view = bank_o[:, 0:KT * (DH + 1)].rearrange("p (q d) -> p q d", q=KT)

            def normalise(n, h):
                if absent(n):
                    return
                dve.wait_ge(pv_done, 2 * n + h + 1)
                dve.reciprocal(rsum[:, h, :], o_view[:, :, DH]).then_inc(r_done, 1)
                dve.wait_ge(r_done, 2 * n + h + 1)
                if late(n, 1):
                    dve.wait_ge(oT_turned, n)
                dve.tensor_tensor(o_n[:, :, h, :], o_view[:, :, 0:DH],
                                  rsum[:, h, :].unsqueeze(2).broadcast_to([128, KT, DH]), ALU.mult).then_inc(o_done, 1)

            def out_low(n):
                if absent(n):
                    return
                dve.wait_ge(oT_hi_done, n + 1)
                dve.tensor_tensor(oT_lo[:, bass.ds(n, 1), :].rearrange("p a t -> p (a t)"), bank_o, o_hi[:, :],
                                  ALU.subtract).then_inc(oT_done, 1)

            def out_keep(n):
                if absent(n):
                    return
                dve.tensor_copy(oT_hi[:, bass.ds(n, 1), :].rearrange("p a t -> p (a t)"), o_hi[:, :]).then_inc(oT_kept, 1)

            def maximum(n, slot, c):
                if absent(n):
                    return
                h, q = c // KT, c % KT
                dve.wait_ge(s_done, 8 * n + c + 1)
                dve.reduce_max(m_q[:, slot, q, h:h + 1], bank_s[c % 2], AX_X).then_inc(max_done, 1)

            def step(i, s):
                maximum(i + 1, 1 - s, 1)
                normalise(i - 1, 1)
                maximum(i + 1, 1 - s, 2)
                low_parts(i, 0)
                maximum(i + 1, 1 - s, 3)
                maximum(i + 1, 1 - s, 4)
                v_low(i + 1, 1 - s)
                maximum(i + 1, 1 - s, 5)
                bias_copy(i + 3, 1 - s)
                out_low(i - 1)
                maximum(i + 1, 1 - s, 6)
                maximum(i + 1, 1 - s, 7)
                low_parts(i, 1)
                q_low(i + 3, 1 - s)
                normalise(i, 0)
                out_keep(i - 1)
                k_again(i + 3, 1 - s)
                k_low(i + 3, 1 - s)
                maximum(i + 2, s, 0)

            for i in range(-LEAD, LOOP_FROM):
                step(i, i % 2)
            with dve.Fori(LOOP_FROM // 2, LOOP_TO // 2) as it:
                step(2 * it + 1, 1)
                step(2 * it + 2, 0)
            for i in range(LOOP_TO, NP + LAG):
                step(i, i % 2)

            def resid_2(b):
                dve.wait_ge(proj_o, b + 1)
                dve.scalar_tensor_tensor(xT[:, b * T:(b + 1) * T], ps[:, OUT_BANK[b], :], bo[:, :], xT[:, b * T:(b + 1) * T],
                                         ALU.add, ALU.add).then_inc(resid, 1)

            def norm_2(b):
                dve.wait_ge(act_ln2, 4 * (b // 2) + 4)
                dve.tensor_tensor(xn3[:, b, :], ps[:, 2 + b % 2, :], ln2_rs[:, b % 2, :], ALU.mult).then_inc(normed, 1)

            def query_parts(j):
                b, g = divmod(j, XG)
                if j in XQ_ACT:
                    dve.wait_ge(xq_high, XQ_ACT.index(j) + 1)
                else:
                    dve.wait_ge(xq_done, j + 1)
                    dve.tensor_scalar(queries[:, g, b * T:(b + 1) * T], ps[0:XR, 5 + j % 3, :],
                                      xb_qk[:, 0, g:g + 1], None, ALU.add).then_inc(xq_high_dve, 1)
                    dve.wait_ge(xq_high_dve, XQ_DVE.index(j) + 1)
                rows = slice(8 * XD, XR)
                q = queries[rows, g, b * T:(b + 1) * T]
                dve.scalar_tensor_tensor(q, ps[rows, 5 + j % 3, :], xb_qk[rows, 0, g:g + 1], q,
                                         ALU.add, ALU.subtract).then_inc(xq_parts, 1)

            dve.wait_ge(bo_added, 1)
            resid_2(0)
            resid_2(1)
            dve.wait_ge(key_parts, 2 * XG)
            dve.wait_ge(pv_done, 2 * NP)
            for h in range(XH):
                dve.tensor_scalar(keys[:, h, :], k_stack[:, h // 4, :], head_mask[:, h % 4:h % 4 + 1], None,
                                  ALU.mult).then_inc(masked, 1)
            resid_2(2)
            norm_2(0)
            norm_2(1)
            resid_2(3)
            for j in range(6):
                query_parts(j)
            norm_2(2)
            norm_2(3)
            for j in range(6, XG * B):
                query_parts(j)

            def max_heads(w, slot, first=False):
                dve.wait_ge(e_done, w + 1)
                if not first:
                    dve.wait_ge(x_shift, w - 1)
                dve.tensor_reduce(xm[:, slot, :], ps[:, 2 * slot:2 * slot + 2, :].rearrange(
                    "p a (h q) -> p q (a h)", q=64), AX_X, ALU.max).then_inc(x_max, 1)

            def weights(w, slot, a, hi, lo, cols, free=None):
                dve.wait_ge(x_sum, w + 1)
                dve.tensor_tensor(xsum[:, :], xs2[:, slot, 0, :], xs2[:, slot, 1, :], ALU.add).then_inc(x_add, 1)
                dve.wait_ge(x_add, w + 1)
                dve.reciprocal(xrec[:, slot, :], xsum[:, :]).then_inc(x_rec, 1)
                dve.wait_ge(x_rec, w + 1)
                if free is not None:
                    dve.wait_ge(x_pv, free)
                dve.tensor_tensor(a[:, :, cols], xe[:, slot, :, :],
                                  xrec[:, slot, :].unsqueeze(1).broadcast_to([128, XH, 64]), ALU.mult).then_inc(x_norm, 1)
                dve.wait_ge(x_norm, w + 1)
                dve.tensor_tensor(lo[:, 0:8, cols], a[:, 0:8, cols], hi[:, 0:8, cols],
                                  ALU.subtract).then_inc(x_lo_d, 1)

            max_heads(0, 0, first=True)
            max_heads(1, 1, first=True)
            with dve.Fori(0, UL // 2 - 1) as it:
                for j in range(2):
                    w = 2 * it + j
                    max_heads(w + 2, j)
                    weights(w, j, left, left_hi, left_lo, bass.ds(w * 64, 64))
            for w in range(UL - 2, UL):
                max_heads(w + 2, w % 2)
                weights(w, w % 2, left, left_hi, left_lo, slice(w * 64, w * 64 + 64))

            def resid_3(b):
                dve.wait_ge(x_proj, b + 1)
                xTb = xT[:, bass.ds(b * T, T)]
                dve.scalar_tensor_tensor(xTb, ps[:, 4, :], xb_o[:, :], xTb, ALU.add, ALU.add).then_inc(resid2, 1)

            def norm_3(b):
                dve.wait_ge(act_ln3, 3 * b + 3)
                dve.tensor_tensor(xn3[:, bass.ds(b, 1), :].rearrange("p a t -> p (a t)"), ps[:, 4, :], ln_rs[:, :],
                                  ALU.mult).then_inc(normed3, 1)

            for b in range(B):
                for c in range(8):
                    w = 8 * b + UL + c
                    if c < 6 or b < B - 1:
                        max_heads(w + 2, c % 2)
                    q = c // 2 % 2
                    free = 4 * b + c // 2 - 1 if b or c >= 4 else None
                    weights(w, c % 2, xa[q], xa_hi[q], xa_lo[q], slice(64 * (c % 2), 64 * (c % 2) + 64), free)
                    if c == 0 and b >= 2:
                        norm_3(b - 2)
                    if c == 3 and b:
                        resid_3(b - 1)
            norm_3(B - 2)

            steps = [0]

            def g(ins, wait=True):
                ins.then_inc(g_step, 1)
                steps[0] += 1
                if wait:
                    dve.wait_ge(g_step, steps[0])

            def over(a):
                return a.unsqueeze(2).broadcast_to([128, a.shape[1], E])

            def sort_gates(part):
                t0, t1 = G_TILES[part]
                ts = slice(t0, t1)
                assert steps[0] == G_BEFORE[part]
                dve.wait_ge(scored, B - 1 + part)
                score = ps[:, 5, 0:TT * E].rearrange("p (t e) -> p t e", t=TT)[:, ts, :]
                z, q, m = gz[:, ts, :], gq[:, ts, :], g1[:, ts]
                g(dve.tensor_reduce(m, score, AX_X, ALU.add))
                g(dve.scalar_tensor_tensor(z, over(m), -1.0 / E, score, ALU.mult, ALU.add))
                g(dve.tensor_tensor(q, z, z, ALU.mult))
                g(dve.tensor_reduce(m, q, AX_X, ALU.add))
                dve.wait_ge(g_act, 3 * part + 2)
                g(dve.scalar_tensor_tensor(z, z, 0.5, over(m), ALU.mult, ALU.mult))
                g(dve.tensor_reduce(m, z, AX_X, ALU.max))
                g(dve.tensor_tensor(z, z, over(m), ALU.subtract))
                for t in range(t0, t1):
                    g(dve.max(c_a[:, 0, t, 0:8], gz[:, t, :]), wait=t == t1 - 1)
                for t in range(t0, t1):
                    g(dve.match_replace(gq[:, t, :], c_a[:, 0, t, 0:8], gz[:, t, :], -1e30), wait=t == t1 - 1)
                for t in range(t0, t1):
                    g(dve.max(c_a[:, 0, t, 8:16], gq[:, t, :]), wait=t == t1 - 1)

            def threshold_roots(part):
                ts = slice(*G_TILES[part])
                g(dve.tensor_tensor(c_a[:, 1, ts, :], c_a[:, 0, ts, :], c_a[:, 0, ts, :], ALU.mult), wait=False)
                g(dve.tensor_copy(gq[:, ts, :], c_a[:, 0, ts, :]))
                old, new = c_a[:, :, ts, :], c_b[:, :, ts, :]
                for k in (1, 2, 4, 8):
                    g(dve.tensor_copy(new[:, :, :, 0:k], old[:, :, :, 0:k]), wait=False)
                    g(dve.tensor_tensor(new[:, :, :, k:E], old[:, :, :, k:E], old[:, :, :, 0:E - k], ALU.add))
                    old, new = new, old
                n = ts.stop - ts.start
                ks = inv_k.unsqueeze(1).broadcast_to([128, n, E])
                mean_k, meansq_k, root = c_b[:, 0, ts, :], c_b[:, 1, ts, :], gs[:, ts, :]
                g(dve.tensor_tensor(mean_k, c_a[:, 0, ts, :], ks, ALU.mult), wait=False)
                g(dve.tensor_tensor(meansq_k, c_a[:, 1, ts, :], ks, ALU.mult))
                g(dve.tensor_tensor(root, mean_k, mean_k, ALU.mult))
                g(dve.tensor_tensor(root, root, meansq_k, ALU.subtract))
                g(dve.tensor_tensor(root, root, ks, ALU.add))
                g(dve.tensor_scalar(root, root, 0.0, None, ALU.max))
                assert steps[0] == G_SQRT[part]

            def gates(part):
                ts = slice(*G_TILES[part])
                z, q, m, tau = gz[:, ts, :], gq[:, ts, :], g1[:, ts], gs[:, ts, :]
                dve.wait_ge(g_act, 3 * part + 3)
                g(dve.tensor_tensor(tau, c_b[:, 0, ts, :], tau, ALU.subtract))
                g(dve.tensor_tensor(q, tau, q, ALU.is_le))
                g(dve.tensor_scalar(q, q, 1e30, -1e30, ALU.mult, ALU.add))
                g(dve.tensor_tensor(tau, tau, q, ALU.add))
                g(dve.tensor_reduce(m, tau, AX_X, ALU.max))
                g(dve.tensor_tensor(z, z, over(m), ALU.subtract))
                g(dve.tensor_scalar(z, z, 0.0, None, ALU.max))
                g(dve.tensor_tensor(q, z, z, ALU.mult))
                g(dve.tensor_copy(a_hi[:, ts, :], q))
                dve.wait_ge(w_mix, 7)
                for j in range(2):
                    dve.tensor_copy(a_stack[:, ts, j, 0:E], a_hi[:, ts, :]).then_inc(a_done, 1)
                dve.tensor_tensor(a_stack[:, ts, 2, 0:E], q, a_hi[:, ts, :], ALU.subtract).then_inc(a_done, 1)

            sort_gates(0)
            resid_3(B - 1)
            threshold_roots(0)
            norm_3(B - 1)
            gates(0)

            def gated(b, bank, col, gate, z, done, lo, out):
                dve.wait_ge(done, b + 1)
                if b:
                    dve.wait_ge(lo, b)
                dve.scalar_tensor_tensor(z, ps[:, bank, :], bin_sb[:, col:col + 1], gate,
                                         ALU.add, ALU.mult).then_inc(out, 1)

            def low(b, z, split, hi, lo):
                rows = slice(R, 2 * R)
                dve.wait_ge(hi, b + 1)
                dve.tensor_tensor(split[rows, :], z[rows, :], split[rows, :], ALU.subtract).then_inc(lo, 1)

            def first(b):
                dve.wait_ge(g1_out, b + 1)
                gated(b, 0, 0, gates_1, z1, z1_done, z1_lo, z1_out)
                low(b, z1, z1_split, z1_hi, z1_lo)

            def second(b):
                dve.wait_ge(g_out, b + 1)
                gated(b, 6, 1, gates_2[:, b % 2, :], z2, z2_done, z2_lo, z2_out)

            def result(b):
                dve.wait_ge(y_done, b + 1)
                dve.tensor_tensor(xT[:, b * T:(b + 1) * T], ps[:, 7, :], xT[:, b * T:(b + 1) * T], ALU.add).then_inc(stored, 1)

            sort_gates(1)
            first(0)
            first(1)
            threshold_roots(1)
            gates(1)
            for b in range(1, B + 1):
                if b >= 2:
                    low(b - 2, z2, z2_split, z2_hi, z2_lo)
                if b + 1 < B:
                    first(b + 1)
                if b >= 2:
                    result(b - 2)
                second(b - 1)
            low(B - 1, z2, z2_split, z2_hi, z2_lo)
            result(B - 1)

        @block.tensor
        def _(pe):
            def mm(o, lhsT, rhs, start, stop):
                return pe.matmul(o, lhsT, rhs, start=start, stop=stop, skip_group_check=True)

            pe.wait_ge(loaded_x0, 16 * 2)
            for b in range(B):
                if b == 1:
                    pe.wait_ge(loaded_x, 16 * (B - 1))
                mm(ps[:, b, :], centre, xT[:, b * T:(b + 1) * T], True, True).then_inc(pe_ln, 1)
            for b in range(B):
                pe.wait_ge(act_ln, b + 1)
                mm(ps[:, 4 + b, :], mean, ln1_sq[:, b, :], True, True).then_inc(pe_ln, 1)

            pe.wait_ge(loaded, 16 * OTHER_LOADS)
            pe.wait_ge(act_ln, B + 1)
            for g in range(XG):
                mm(ps[0:XR, 4 + g, :], xw_k[:, g, :], ctx_sb[:, 0:512], True, True).then_inc(ctx_k, 1)
            pe.wait_ge(dve_ln, B)
            for g in range(XG):
                last = mm(ps[0:XR, 0, 128 * g:128 * g + 128], xw_k[:, g, :], ctx_sb[:, 512:640], True, True)
            last.then_inc(ctx_k, 1)
            for t in range(XT):
                o = ps[:, 1 + t // 4, 128 * (t % 4):128 * (t % 4) + 128]
                mm(o, ctx_sb[:, t * 128:(t + 1) * 128], xw[:, 0, :], True, False)
                last = mm(o, ones_row[0:1, :], xbv_row[:, :], False, True)
            last.then_inc(ctx_v, 1)
            pe.wait_ge(loaded_w, 16 * W_LOADS)
            for p in range(PAIRS):
                last = mm(ps[:, 3, 0:1], wo_raw[:, p, :], biases[:, 2, p:p + 1], p == 0, p == PAIRS - 1)
            last.then_inc(bo_done, 1)
            pe.wait_ge(bo_added, 1)
            pe.wait_ge(xn_done, 2 * B)
            pe.wait_ge(w_lo_done, 3)
            pe.wait_ge(w_pool, 4)
            pe.wait_ge(setup, 4)
            pe.wait_ge(key_parts, 2 * XG)
            pe.wait_ge(val_parts, B + 1)

            def project(n, j, done):
                cols = bass.ds(n % PAIRS * 128, 128)
                xb = bass.ds(n // PAIRS, 1)
                xh = xn_hi[:, xb, :].rearrange("p a t -> p (a t)")
                xl = xn_lo[:, xb, :].rearrange("p a t -> p (a t)")
                mm(bank_p, w_hi[:, j, cols], xh, True, False)
                mm(bank_p, w_lo[:, j, cols], xh, False, False)
                mm(bank_p, w_hi[:, j, cols], xl, False, True).then_inc(done, 1)

            def project_q(n):
                if absent(n):
                    return
                if late(n, 2):
                    pe.wait_ge(v_lo, n - 1)
                elif n == 1:
                    pe.wait_ge(k_lo, n)
                project(n, 0, q_proj)

            def project_k(n):
                if absent(n):
                    return
                pe.wait_ge(q_lo, n + 1)
                project(n, 1, k_proj)

            def project_v(n):
                if absent(n):
                    return
                if isinstance(n, int) and n == NP - 1:
                    pe.wait_ge(v_lo, n)
                else:
                    pe.wait_ge(k_lo, n + 2)
                cols = bass.ds(n % PAIRS * 128, 128)
                for t in range(KT):
                    toks = bass.ds(n // PAIRS * T + t * 128, 128)
                    xh = xn_hi[:, :, :].rearrange("p a t -> p (a t)")[:, toks]
                    xl = xn_lo[:, :, :].rearrange("p a t -> p (a t)")[:, toks]
                    o = bank_p[:, t * 128:(t + 1) * 128]
                    mm(o, xh, w_hi[:, 2, cols], True, False)
                    mm(o, xh, w_lo[:, 2, cols], False, False)
                    last = mm(o, xl, w_hi[:, 2, cols], False, True)
                last.then_inc(v_proj, 1)

            def scores_for_max(n, slot, c):
                if absent(n):
                    return
                h, q = c // KT, c % KT
                if c == 0:
                    pe.wait_ge(stacked, 16 * DMAS * (n + 1))
                    if late(n, 1):
                        pe.wait_ge(m_out, n)
                elif c >= 2 or late(n, 1):
                    pe.wait_ge(max_done, 8 * n + c - 1)
                mm(bank_s[c % 2], qa[:, slot, h, q * 128:(q + 1) * 128],
                   ka[:, slot, h, :], True, True).then_inc(s_done, 1)

            def turn_maxima(n, slot):
                if absent(n):
                    return
                pe.wait_ge(max_done, 8 * n + 8)
                for q in range(KT):
                    last = pe.transpose(bank_s[0][0:2, q * 128:(q + 1) * 128], m_q[:, slot, q, :], ident)
                last.then_inc(m_turned, 1)

            def scores(n, slot, h, half):
                if absent(n):
                    return
                if h == 0 and half == 0:
                    pe.wait_ge(m_placed, 16 * (n + 1))
                if h == 1 or late(n, 1):
                    pe.wait_ge(exp_done[half], 2 * n + h)
                for t in range(2):
                    cols = slice((2 * half + t) * 128, (2 * half + t + 1) * 128)
                    mm(st[half][:, t, :], ka[:, slot, h, cols], qa[:, slot, h, :], True, False)
                    last = mm(st[half][:, t, :], kb[0:DH + 1, slot, h, cols], qb[0:DH + 1, slot, h, :], False, True)
                last.then_inc(st_done[half], 1)

            def values(n, slot, h, part):
                if absent(n):
                    return
                if part == 0:
                    pe.wait_ge(lo_dve, 2 * n + h + 1)
                    pe.wait_ge(lo_pool, 4 * n + 2 * h + 2)
                    if h == 0:
                        pe.wait_ge(v_lo, n + 1)
                    if h == 1:
                        pe.wait_ge(o_done, 2 * n + 1)
                    elif late(n, 1):
                        pe.wait_ge(oT_done, n)
                for q in (2 * part, 2 * part + 1):
                    cols = slice(q * 128, (q + 1) * 128)
                    o = bank_o[:, q * (DH + 1):(q + 1) * (DH + 1)]
                    for k in range(KT):
                        mm(o, prob_hi[:, h, k, cols], v_hi_t[:, slot, k, h, :], k == 0, False)
                        mm(o[:, 0:DH], prob_hi[:, h, k, cols], v_lo_t[:, slot, k, h, :], False, False)
                        last = mm(o, prob_lo[:, h, k, cols], v_hi_t[:, slot, k, h, :], False, k == KT - 1)
                if part == 1:
                    last.then_inc(pv_done, 1)

            def turn_outputs(n):
                if absent(n):
                    return
                pe.wait_ge(o_done, 2 * n + 2)
                for q in range(KT):
                    last = pe.transpose(bank_o[:, q * 128:(q + 1) * 128],
                                        o_n[:, q, :, :].rearrange("p h d -> p (h d)"), ident)
                last.then_inc(oT_turned, 1)

            def out_proj(b):
                pe.wait_ge(oT_done, PAIRS * (b + 1))
                pe.wait_ge(oT_kept, PAIRS * (b + 1))
                if b == 0:
                    pe.wait_ge(exp_done[0], 2 * NP)
                elif b == B - 1:
                    pe.wait_ge(resid, 1)
                for p in range(PAIRS):
                    n, bank = b * PAIRS + p, ps[:, OUT_BANK[b], :]
                    mm(bank, wo_hi[:, p, :], oT_hi[:, n, :], p == 0, False)
                    mm(bank, wo_lo[:, p, :], oT_hi[:, n, :], False, False)
                    last = mm(bank, wo_hi[:, p, :], oT_lo[:, n, :], False, p == PAIRS - 1)
                last.then_inc(proj_o, 1)

            def step(i, s):
                scores(i, s, 0, 0)
                scores_for_max(i + 1, 1 - s, 2)
                scores(i, s, 0, 1)
                scores_for_max(i + 1, 1 - s, 3)
                project_v(i + 1)
                scores_for_max(i + 1, 1 - s, 4)
                turn_outputs(i - 1)
                scores(i, s, 1, 0)
                scores_for_max(i + 1, 1 - s, 5)
                scores(i, s, 1, 1)
                scores_for_max(i + 1, 1 - s, 6)
                scores_for_max(i + 1, 1 - s, 7)
                project_q(i + 3)
                if isinstance(i, int) and i == NP - 1:
                    out_proj(0)
                values(i, s, 0, 0)
                turn_maxima(i + 1, 1 - s)
                values(i, s, 0, 1)
                project_k(i + 3)
                values(i, s, 1, 0)
                values(i, s, 1, 1)
                scores_for_max(i + 2, s, 0)
                scores_for_max(i + 2, s, 1)

            for i in range(-LEAD, LOOP_FROM):
                step(i, i % 2)
            with pe.Fori(LOOP_FROM // 2, LOOP_TO // 2) as it:
                step(2 * it + 1, 1)
                step(2 * it + 2, 0)
            for i in range(LOOP_TO, NP):
                step(i, i % 2)
            out_proj(1)
            step(NP, 0)

            def centre_2(b):
                pe.wait_ge(resid, b + 1)
                if b >= 2:
                    pe.wait_ge(normed, b - 1)
                mm(ps[:, 2 + b % 2, :], centre, xT[:, b * T:(b + 1) * T], True, True).then_inc(pe_ln2, 1)

            def variance_2(b):
                pe.wait_ge(act_ln2, 4 * (b // 2) + b % 2 + 1)
                bank = 4 + b if b < 2 else b - 2
                mm(ps[:, bank, :], mean, ln2_sq[:, b % 2, :], True, True).then_inc(pe_ln2, 1)

            def queries_2(b, groups=range(XG)):
                pe.wait_ge(normed, b + 1)
                for g in groups:
                    j = XG * b + g
                    if j >= 3:
                        pe.wait_ge(xq_parts, j - 2)
                    mm(ps[0:XR, 5 + j % 3, :], xw_q[:, g, :], xn3[:, b, :], True, True).then_inc(xq_done, 1)

            out_proj(2)
            centre_2(0)
            centre_2(1)
            variance_2(0)
            variance_2(1)
            out_proj(3)
            centre_2(2)
            centre_2(3)
            queries_2(0, (0, 1, 2))
            variance_2(2)
            variance_2(3)
            queries_2(0, (3,))
            queries_2(1)
            queries_2(2)
            queries_2(3)
            pe.wait_ge(xq_parts, XG * B)
            pe.wait_ge(masked, XH)

            def energies_left(w, slot, cols, first=False):
                if not first:
                    pe.wait_ge(x_exp, w - 1)
                for h in range(XH):
                    for b in range(B):
                        o = ps[SLP * b:SLP * b + SLP, 2 * slot + h // 8, 64 * (h % 8):64 * (h % 8) + 64]
                        ks = slice(B * 128 + SLP * b, B * 128 + SLP * b + SLP)
                        last = mm(o, keys[:, h, ks], queries[:, h // 4, bass.ds(b * T + cols, 64)], h % 8 == 0, False)
                last.then_inc(e_done, 1)

            def energies(w, slot, b, cols):
                pe.wait_ge(x_exp, w - 1)
                for h in range(XH):
                    o = ps[:, 2 * slot + h // 8, 64 * (h % 8):64 * (h % 8) + 64]
                    last = mm(o, keys[:, h, b * 128:(b + 1) * 128],
                              queries[:, h // 4, b * T + cols:b * T + cols + 64], h % 8 == 0, False)
                last.then_inc(e_done, 1)

            def shift(w, slot):
                pe.wait_ge(x_max, w + 1)
                for half in range(2):
                    last = mm(ps[:, 2 * slot + half, :].rearrange("p (h q) -> p h q", q=64), minus_ident[:, :],
                              xm[:, slot, :].unsqueeze(1).broadcast_to([128, 8, 64]), False, True)
                last.then_inc(x_shift, 1)

            energies_left(0, 0, 0, first=True)
            for w in range(1, UL):
                energies_left(w, w % 2, 64 * w, first=w < 2)
                shift(w - 1, (w - 1) % 2)
            energies(UL, 0, 0, 0)
            shift(UL - 1, 1)

            def weighted(b, q, part):
                n = 4 * b + q
                pe.wait_ge(x_lo_d, 2 * n + UL + 2)
                pe.wait_ge(x_lo_p, 2 * n + UL + 2)
                if n:
                    pe.wait_ge(x_out, n)
                s, cols = q % 2, slice(128 * q, 128 * q + 128)
                vals = [a[:, :, :].rearrange("p b n -> p (b n)") for a in (xv_hi, xv_lo, xvl_hi, xvl_lo)]
                for h in range(part * XH // 2, (part + 1) * XH // 2):
                    o = ps[:, 6, 128 * q + XD * h:128 * q + XD * h + XD]
                    v_h, v_l, l_h, l_l = (a[:, bass.ds(b * 128 + XD * h, XD)] for a in vals)
                    mm(o, xa_hi[s][:, h, :], v_h, h == 0, False)
                    mm(o, xa_hi[s][:, h, :], v_l, False, False)
                    mm(o, xa_lo[s][:, h, :], v_h, False, False)
                    mm(o, left_hi[:, h, cols], l_h, False, False)
                    mm(o, left_hi[:, h, cols], l_l, False, False)
                    last = mm(o, left_lo[:, h, cols], l_h, False, True)
                if part:
                    last.then_inc(x_pv, 1)

            def turn_tiles(b):
                pe.wait_ge(x_out, 4 * b + 4)
                if b:
                    pe.wait_ge(act_ln3, 3 * b - 1)
                for q in range(KT):
                    last = pe.transpose(ps[:, 7, 128 * q:128 * q + 128], xo[:, q, :], ident)
                last.then_inc(x_turned, 1)

            def out_proj_3(b):
                pe.wait_ge(x_T, b + 1)
                if b:
                    pe.wait_ge(normed3, b)
                mm(ps[:, 4, :], xw[:, 1, :], xoT[:, :], True, True).then_inc(x_proj, 1)

            def centre_3(b):
                pe.wait_ge(resid2, b + 1)
                mm(ps[:, 4, :], centre, xT[:, b * T:(b + 1) * T], True, True).then_inc(pe_ln3, 1)

            def variance_3(b):
                pe.wait_ge(act_ln3, 3 * b + 1)
                mm(ps[:, 7, :], mean, ln_sq[:, :], True, True).then_inc(pe_ln3, 1)

            def expert_scores(b):
                pe.wait_ge(normed3, b + 1)
                for t in range(KT):
                    last = mm(ps[:, 5, (b * KT + t) * E:(b * KT + t + 1) * E], xn3[:, b, t * 128:(t + 1) * 128],
                              proj_sb[:, :], True, True)
                last.then_inc(scored, 1)

            def half_tile(u):
                if u >= 4:
                    weighted((u - 4) // 8, (u - 4) % 8 // 2, u % 2)

            for u in range(UM):
                b, c = divmod(u, 8)
                if u:
                    energies(UL + u, u % 2, b, 64 * c)
                half_tile(u)
                shift(UL + u, u % 2)
                if c == 3 and b >= 2:
                    expert_scores(b - 2)
                if c == 4 and b:
                    turn_tiles(b - 1)
                if c == 5 and b:
                    out_proj_3(b - 1)
                if c == 6 and b:
                    centre_3(b - 1)
                if c == 7 and b:
                    variance_3(b - 1)
            expert_scores(B - 2)
            for u in range(UM, UM + 4):
                half_tile(u)
            turn_tiles(B - 1)
            out_proj_3(B - 1)
            centre_3(B - 1)
            variance_3(B - 1)
            pe.wait_ge(g_step, 2)
            expert_scores(B - 1)

            def gates_in(b):
                if b:
                    pe.wait_ge(z1_lo, b)
                if b in (0, B - 1):
                    pe.wait_ge(a_done, 6 if b else 3)
                for t in range(KT):
                    last = pe.transpose(ps[0:ER, 0, t * 128:(t + 1) * 128],
                                        a_stack[:, KT * b + t, :, :].rearrange("p j e -> p (j e)"), ident)
                last.then_inc(aT_turned, 1)

            def gates_z1(b):
                if b == 0:
                    pe.wait_ge(w_mix, 6)
                pe.wait_ge(aT_out, b + 1)
                if b:
                    pe.wait_ge(g1_out, b)
                mm(ps[:, 1, :], c_split[:, 0, :], aT[0:ER, :], True, True).then_inc(g_done, 1)
                mm(ps[:, 0, :], win1_sb[:, :], xn3[:, b, :], True, True).then_inc(z1_done, 1)
                if b:
                    pe.wait_ge(g_out, b)
                mm(ps[:, 2, :], c_split[:, 1, :], aT[0:ER, :], True, True).then_inc(g_done, 1)

            def product(o, w_hi, w_lo, z):
                mm(o, w_hi, z, True, False)
                return mm(o, w_lo, z[0:R, :], False, True)

            def hidden(b):
                pe.wait_ge(z1_lo, b + 1)
                for m in range(4):
                    j, cols = 4 * b + m, slice(m * 128, (m + 1) * 128)
                    if j >= 3:
                        pe.wait_ge(h_out, j - 2)
                    elif j == 2:
                        pe.wait_ge(g_step, G_BEFORE[1] + 2)
                    product(ps[:, 3 + j % 3, :], wout1_hi[:, cols], wout1_lo[:, cols], z1_split).then_inc(h_done, 1)

            def second(b):
                if b:
                    pe.wait_ge(z2_out, b)
                for m in range(4):
                    pe.wait_ge(h_out, 4 * b + m + 1)
                    last = mm(ps[:, 6, :], win2_sb[:, m, :], hid[:, b % 2, m, :], m == 0, m == 3)
                last.then_inc(z2_done, 1)

            def result(b):
                pe.wait_ge(z2_lo, b + 1)
                if b:
                    pe.wait_ge(stored, b)
                product(ps[:, 7, :], wout2_hi[:, :], wout2_lo[:, :], z2_split).then_inc(y_done, 1)

            gates_in(0)
            gates_z1(0)
            for b in range(B + 1):
                if b + 1 < B:
                    gates_in(b + 1)
                if b < B:
                    hidden(b)
                if b + 1 < B:
                    gates_z1(b + 1)
                if b >= 2:
                    result(b - 2)
                if b:
                    second(b - 1)
            result(B - 1)


def kernel(**inputs):
    import concourse.bacc as bacc
    from concourse.bass_utils import run_bass_kernel_spmd

    def t(a, *axes):
        return np.ascontiguousarray(np.transpose(np.asarray(a), axes))

    g = {k: np.asarray(v) for k, v in inputs.items()}
    eye = np.eye(128, dtype=np.float32)
    heads = np.zeros((128, 4), np.float32)
    heads[0:XR] = np.tile(np.repeat(np.eye(4, dtype=np.float32), XD, axis=0), (3, 1))

    def stacked(a):
        a = a.reshape(a.shape[:-1] + (XG, 1, 4 * XD))
        return np.ascontiguousarray(np.broadcast_to(a, a.shape[:-2] + (3, 4 * XD))).reshape(a.shape[:-2] + (XR,))
    left = np.zeros((128, B), np.float32)
    for b in range(B):
        left[SLP * b:SLP * b + SL, b] = 1.0
    full = np.full((128, 128), 1.0 / 128, np.float32)
    consts = np.concatenate([eye - full, full, eye, np.ones((128, 128), np.float32), heads, left,
                             np.tile(1.0 / np.arange(1, E + 1, dtype=np.float32), (128, 1))], axis=1)
    ctxT = t(g["ctx_1024"], 2, 0, 1)

    def col(a):
        return np.ascontiguousarray(a.reshape(-1, 1))

    c12 = np.zeros((3, 32, 2, 2, R), np.float32)
    c12[:, 0:E] = np.stack([g["L0_ffn_C1"], g["L0_ffn_C2"]], axis=1)[None, :, :, None, :]
    c12 = c12.reshape(ER, 2, 2 * R)

    arrays = {
        "x": t(g["x"], 2, 0, 1).reshape(D, B * T),
        "ctx_main": np.ascontiguousarray(ctxT[:, :, 0:128]).reshape(D, B * 128),
        "ctx_left": np.ascontiguousarray(ctxT[:, :, 128:]),
        "wq": t(g["L0_attn_W_Q"], 2, 0, 1).reshape(D, H * DH),
        "wk": t(g["L0_attn_W_K"], 2, 0, 1).reshape(D, H * DH),
        "wv": t(g["L0_attn_W_V"], 2, 0, 1).reshape(D, H * DH),
        "wo": t(g["L0_attn_W_O"].reshape(PAIRS, 2, D, DH), 1, 3, 0, 2).reshape(128, PAIRS, D),
        "bias_qkv": t(np.stack([g["L0_attn_b_Q"], g["L0_attn_b_K"], g["L0_attn_b_V"]]).reshape(3, PAIRS, 128), 2, 0, 1),
        "b_o": col(g["L0_attn_b_O"]),
        "xwq": stacked(g["L0_xattn_Wq_w"].T), "xwk": stacked(g["L0_xattn_Wk_w"].T),
        "xwv": t(g["L0_xattn_Wv_w"], 1, 0), "xwo": t(g["L0_xattn_Wo_w"], 1, 0),
        "xbqk": t(stacked(np.stack([g["L0_xattn_Wq_b"], g["L0_xattn_Wk_b"]])), 2, 0, 1),
        "xbo": col(g["L0_xattn_Wo_b"]),
        "xbv": g["L0_xattn_Wv_b"].reshape(1, 128),
        "proj": g["L0_ffn_proj"],
        "c12": c12,
        "win1": np.tile(g["L0_ffn_Win1"][0:D], (1, 2)),
        "wout1": np.tile(g["L0_ffn_Wout1"].T, (2, 1)),
        "win2": np.tile(t(g["L0_ffn_Win2"][0:O].reshape(O // 128, 128, R), 1, 0, 2), (1, 1, 2)),
        "wout2": np.tile(g["L0_ffn_Wout2"].T, (2, 1)),
        "bins": np.tile(np.stack([g["L0_ffn_Win1"][D], g["L0_ffn_Win2"][O]], axis=1), (2, 1)),
        "consts": consts,
    }
    nc = bacc.Bacc("TRN2", target_bir_lowering=False, num_devices=1)
    args = [nc.dram_tensor(f"in_{k}", a.shape, mybir.dt.from_np(a.dtype), kind="ExternalInput").ap()
            for k, a in arrays.items()]
    out = nc.dram_tensor("out_T", (D, B * T), F32, kind="ExternalOutput").ap()
    decoder(nc, **dict(zip(arrays, args)), out=out)
    r = run_bass_kernel_spmd(nc, [{f"in_{k}": a for k, a in arrays.items()}], core_ids=[0])
    return t(r.results[0]["out_T"].reshape(D, B, T), 1, 2, 0)
```
